# Optimizing a Trainium2 kernel written in Bass

```python
import numpy as np
import jax
import jax.numpy as jnp

def _softmax(x, axis=-1):
    return jax.nn.softmax(x, axis=axis)

def _gelu(x):
    return jax.nn.gelu(x, approximate=True)

def _silu(x):
    return jax.nn.silu(x)

def _sigmoid(x):
    return jax.nn.sigmoid(x)

def _layernorm(x, axis=-1, eps=1e-05):
    m = jnp.mean(x, axis=axis, keepdims=True)
    v = jnp.var(x, axis=axis, keepdims=True)
    return (x - m) / jnp.sqrt(v + eps)

def _scatter_add(tgt, idx, src, axis=0):
    return tgt.at[idx].add(src)

def _segment_sum(src, seg, n):
    return jax.ops.segment_sum(src, seg, n)
kernel_name = 'mk_gps_d1_gnn_r32_d4ed6f'

def setup_inputs(seed: int=0):
    np.random.seed(seed)
    _w = jnp.asarray

    def _rec_inputs():
        import jax
        import jax.numpy as jnp
        _gk = jax.random.key(seed)
        x = -0.0003713 + 1 * jax.random.normal(jax.random.fold_in(_gk, 1), (3125, 256), jnp.float32)
        src = jax.random.randint(jax.random.fold_in(_gk, 2), (50000,), 0, 3125, jnp.int32)
        dst = jax.random.randint(jax.random.fold_in(_gk, 3), (50000,), 0, 3125, jnp.int32)
        _o = jnp.argsort(dst, stable=True)
        src = src[_o]
        dst = dst[_o]
        return (x, src, dst)
    x, src, dst = _rec_inputs()

    def _L0_gnn_setup():
        import jax, jax.numpy as jnp
        import numpy as np
        N, HID, HEADS = (50000, 256, 8)
        D = HID // HEADS
        E = 25000

        def _gnn_layer(x, edge_index, Wq, bq, Wk, bk, Wv, bv, Wskip, bskip, gamma, beta):
            n = x.shape[0]
            src, dst = (edge_index[0], edge_index[1])
            q = (x @ Wq + bq).reshape(n, HEADS, D)
            k = (x @ Wk + bk).reshape(n, HEADS, D)
            v = (x @ Wv + bv).reshape(n, HEADS, D)
            logits = jnp.einsum('ehd,ehd->eh', q[dst], k[src]) / jnp.sqrt(jnp.float32(D))
            seg_max = jax.ops.segment_max(logits, dst, num_segments=n)
            expv = jnp.exp(logits - seg_max[dst])
            denom = jax.ops.segment_sum(expv, dst, num_segments=n)
            attn = expv / denom[dst]
            agg = jax.ops.segment_sum(attn[:, :, None] * v[src], dst, num_segments=n)
            out = agg.reshape(n, HID) + (x @ Wskip + bskip)
            h = jax.nn.gelu(out, approximate=False)
            y = x + h
            mu = jnp.mean(y, axis=-1, keepdims=True)
            var = jnp.var(y, axis=-1, keepdims=True)
            return (y - mu) / jnp.sqrt(var + 1e-05) * gamma + beta
        key = jax.random.key(seed)
        ks = jax.random.split(key, 12)
        s = 0.02
        x = jax.random.normal(ks[0], (N, HID), dtype=jnp.float32)
        edge_index = jax.random.randint(ks[1], (2, E), 0, N, dtype=jnp.int64)
        Wq = jax.random.normal(ks[2], (HID, HID), dtype=jnp.float32) * s
        bq = jnp.zeros((HID,), dtype=jnp.float32)
        Wk = jax.random.normal(ks[3], (HID, HID), dtype=jnp.float32) * s
        bk = jnp.zeros((HID,), dtype=jnp.float32)
        Wv = jax.random.normal(ks[4], (HID, HID), dtype=jnp.float32) * s
        bv = jnp.zeros((HID,), dtype=jnp.float32)
        Wskip = jax.random.normal(ks[5], (HID, HID), dtype=jnp.float32) * s
        bskip = jnp.zeros((HID,), dtype=jnp.float32)
        gamma = jnp.ones((HID,), dtype=jnp.float32)
        beta = jnp.zeros((HID,), dtype=jnp.float32)
        return {'x': x, 'edge_index': edge_index, 'Wq': Wq, 'bq': bq, 'Wk': Wk, 'bk': bk, 'Wv': Wv, 'bv': bv, 'Wskip': Wskip, 'bskip': bskip, 'gamma': gamma, 'beta': beta}
    _L0_gnn_all = _L0_gnn_setup()
    _L0_gnn_in = {k: v for k, v in _L0_gnn_all.items() if k in ('Wq', 'bq', 'Wk', 'bk', 'Wv', 'bv', 'Wskip', 'bskip', 'gamma', 'beta')}
    del _L0_gnn_all

    def _L0_mix_setup():
        import jax, jax.numpy as jnp
        import numpy as np
        EMB, HEADS, DEPTH, SEQ, BATCH = (256, 8, 4, 256, 4)
        DH = EMB // HEADS
        FF = 4 * EMB
        EPS = 1e-05

        def _layernorm(x, g, b):
            mu = x.mean(-1, keepdims=True)
            var = ((x - mu) ** 2).mean(-1, keepdims=True)
            return (x - mu) * jax.lax.rsqrt(var + EPS) * g + b

        def _linear_attn(x, Wq, Wk, Wv, Wo, bo):
            b, n, dm = x.shape
            split = lambda t: t.reshape(b, n, HEADS, DH).transpose(0, 2, 1, 3)
            scale = DH ** (-0.25)
            q = jax.nn.softmax(split(x @ Wq) * scale, axis=-1)
            k = jax.nn.softmax(split(x @ Wk) * scale, axis=-2)
            v = split(x @ Wv)
            context = jnp.einsum('bhnd,bhne->bhde', k, v)
            out = jnp.einsum('bhnd,bhde->bhne', q, context)
            out = out.transpose(0, 2, 1, 3).reshape(b, n, dm)
            return out @ Wo + bo

        def _forward(x, Wq, Wk, Wv, Wo, bo, ln1_g, ln1_b, W1, b1, W2, b2, ln2_g, ln2_b):
            for i in range(DEPTH):
                h = _layernorm(x, ln1_g[i], ln1_b[i])
                x = x + _linear_attn(h, Wq[i], Wk[i], Wv[i], Wo[i], bo[i])
                h = _layernorm(x, ln2_g[i], ln2_b[i])
                x = x + (jax.nn.gelu(h @ W1[i] + b1[i], approximate=False) @ W2[i] + b2[i])
            return x
        key = jax.random.key(seed)
        ks = jax.random.split(key, 8)
        w = lambda k, shape: jax.random.normal(k, shape, dtype=jnp.float32) * 0.02
        D = DEPTH
        return {'x': jax.random.normal(ks[0], (BATCH, SEQ, EMB), dtype=jnp.float32), 'Wq': w(ks[1], (D, EMB, EMB)), 'Wk': w(ks[2], (D, EMB, EMB)), 'Wv': w(ks[3], (D, EMB, EMB)), 'Wo': w(ks[4], (D, EMB, EMB)), 'bo': jnp.zeros((D, EMB), jnp.float32), 'ln1_g': jnp.ones((D, EMB), jnp.float32), 'ln1_b': jnp.zeros((D, EMB), jnp.float32), 'W1': w(ks[5], (D, EMB, FF)), 'b1': jnp.zeros((D, FF), jnp.float32), 'W2': w(ks[6], (D, FF, EMB)), 'b2': jnp.zeros((D, EMB), jnp.float32), 'ln2_g': jnp.ones((D, EMB), jnp.float32), 'ln2_b': jnp.zeros((D, EMB), jnp.float32)}
    _L0_mix_all = _L0_mix_setup()
    _L0_mix_in = {k: v for k, v in _L0_mix_all.items() if k in ('Wq', 'Wk', 'Wv', 'Wo', 'bo', 'ln1_g', 'ln1_b', 'W1', 'b1', 'W2', 'b2', 'ln2_g', 'ln2_b')}
    del _L0_mix_all

    def _L0_ffn_setup():
        import jax, jax.numpy as jnp
        import numpy as np
        B, S, D = (8, 128, 256)
        H = 4 * D
        CAPACITY = 0.5
        key = jax.random.key(seed)
        ks = jax.random.split(key, 6)
        x = jax.random.normal(ks[0], (B, S, D), dtype=jnp.float32)
        attention_mask = jnp.zeros((B, 1, 1, S), dtype=jnp.float32)
        wr = jax.random.normal(ks[1], (D, 1), dtype=jnp.float32) * 0.02
        br = jnp.zeros((1,), dtype=jnp.float32)
        w1 = jax.random.normal(ks[2], (D, H), dtype=jnp.float32) * 0.02
        b1 = jnp.zeros((H,), dtype=jnp.float32)
        w2 = jax.random.normal(ks[3], (H, D), dtype=jnp.float32) * 0.02
        b2 = jnp.zeros((D,), dtype=jnp.float32)
        return {'x': x, 'attention_mask': attention_mask, 'wr': wr, 'br': br, 'w1': w1, 'b1': b1, 'w2': w2, 'b2': b2}
    _L0_ffn_all = _L0_ffn_setup()
    _L0_ffn_in = {k: v for k, v in _L0_ffn_all.items() if k in ('attention_mask', 'wr', 'br', 'w1', 'b1', 'w2', 'b2')}
    del _L0_ffn_all
    return {'x': x, 'src': src, 'dst': dst, 'L0_gnn_Wq': _L0_gnn_in['Wq'], 'L0_gnn_bq': _L0_gnn_in['bq'], 'L0_gnn_Wk': _L0_gnn_in['Wk'], 'L0_gnn_bk': _L0_gnn_in['bk'], 'L0_gnn_Wv': _L0_gnn_in['Wv'], 'L0_gnn_bv': _L0_gnn_in['bv'], 'L0_gnn_Wskip': _L0_gnn_in['Wskip'], 'L0_gnn_bskip': _L0_gnn_in['bskip'], 'L0_gnn_gamma': _L0_gnn_in['gamma'], 'L0_gnn_beta': _L0_gnn_in['beta'], 'L0_mix_Wq': _L0_mix_in['Wq'], 'L0_mix_Wk': _L0_mix_in['Wk'], 'L0_mix_Wv': _L0_mix_in['Wv'], 'L0_mix_Wo': _L0_mix_in['Wo'], 'L0_mix_bo': _L0_mix_in['bo'], 'L0_mix_ln1_g': _L0_mix_in['ln1_g'], 'L0_mix_ln1_b': _L0_mix_in['ln1_b'], 'L0_mix_W1': _L0_mix_in['W1'], 'L0_mix_b1': _L0_mix_in['b1'], 'L0_mix_W2': _L0_mix_in['W2'], 'L0_mix_b2': _L0_mix_in['b2'], 'L0_mix_ln2_g': _L0_mix_in['ln2_g'], 'L0_mix_ln2_b': _L0_mix_in['ln2_b'], 'L0_ffn_attention_mask': _L0_ffn_in['attention_mask'], 'L0_ffn_wr': _L0_ffn_in['wr'], 'L0_ffn_br': _L0_ffn_in['br'], 'L0_ffn_w1': _L0_ffn_in['w1'], 'L0_ffn_b1': _L0_ffn_in['b1'], 'L0_ffn_w2': _L0_ffn_in['w2'], 'L0_ffn_b2': _L0_ffn_in['b2']}

def reference(x, src, dst, L0_gnn_Wq, L0_gnn_bq, L0_gnn_Wk, L0_gnn_bk, L0_gnn_Wv, L0_gnn_bv, L0_gnn_Wskip, L0_gnn_bskip, L0_gnn_gamma, L0_gnn_beta, L0_mix_Wq, L0_mix_Wk, L0_mix_Wv, L0_mix_Wo, L0_mix_bo, L0_mix_ln1_g, L0_mix_ln1_b, L0_mix_W1, L0_mix_b1, L0_mix_W2, L0_mix_b2, L0_mix_ln2_g, L0_mix_ln2_b, L0_ffn_attention_mask, L0_ffn_wr, L0_ffn_br, L0_ffn_w1, L0_ffn_b1, L0_ffn_w2, L0_ffn_b2):
    import jax
    import jax.numpy as jnp

    def _L0_gnn_ref(x, edge_index, Wq, bq, Wk, bk, Wv, bv, Wskip, bskip, gamma, beta):
        import jax, jax.numpy as jnp
        import numpy as np
        N, HID, HEADS = (50000, 256, 8)
        D = HID // HEADS
        E = 25000

        def _gnn_layer(x, edge_index, Wq, bq, Wk, bk, Wv, bv, Wskip, bskip, gamma, beta):
            n = x.shape[0]
            src, dst = (edge_index[0], edge_index[1])
            q = (x @ Wq + bq).reshape(n, HEADS, D)
            k = (x @ Wk + bk).reshape(n, HEADS, D)
            v = (x @ Wv + bv).reshape(n, HEADS, D)
            logits = jnp.einsum('ehd,ehd->eh', q[dst], k[src]) / jnp.sqrt(jnp.float32(D))
            seg_max = jax.ops.segment_max(logits, dst, num_segments=n)
            expv = jnp.exp(logits - seg_max[dst])
            denom = jax.ops.segment_sum(expv, dst, num_segments=n)
            attn = expv / denom[dst]
            agg = jax.ops.segment_sum(attn[:, :, None] * v[src], dst, num_segments=n)
            out = agg.reshape(n, HID) + (x @ Wskip + bskip)
            h = jax.nn.gelu(out, approximate=False)
            y = x + h
            mu = jnp.mean(y, axis=-1, keepdims=True)
            var = jnp.var(y, axis=-1, keepdims=True)
            return (y - mu) / jnp.sqrt(var + 1e-05) * gamma + beta
        return _gnn_layer(x, edge_index, Wq, bq, Wk, bk, Wv, bv, Wskip, bskip, gamma, beta)

    def _L0_mix_ref(x, Wq, Wk, Wv, Wo, bo, ln1_g, ln1_b, W1, b1, W2, b2, ln2_g, ln2_b):
        import jax, jax.numpy as jnp
        import numpy as np
        EMB, HEADS, DEPTH, SEQ, BATCH = (256, 8, 4, 256, 4)
        DH = EMB // HEADS
        FF = 4 * EMB
        EPS = 1e-05

        def _layernorm(x, g, b):
            mu = x.mean(-1, keepdims=True)
            var = ((x - mu) ** 2).mean(-1, keepdims=True)
            return (x - mu) * jax.lax.rsqrt(var + EPS) * g + b

        def _linear_attn(x, Wq, Wk, Wv, Wo, bo):
            b, n, dm = x.shape
            split = lambda t: t.reshape(b, n, HEADS, DH).transpose(0, 2, 1, 3)
            scale = DH ** (-0.25)
            q = jax.nn.softmax(split(x @ Wq) * scale, axis=-1)
            k = jax.nn.softmax(split(x @ Wk) * scale, axis=-2)
            v = split(x @ Wv)
            context = jnp.einsum('bhnd,bhne->bhde', k, v)
            out = jnp.einsum('bhnd,bhde->bhne', q, context)
            out = out.transpose(0, 2, 1, 3).reshape(b, n, dm)
            return out @ Wo + bo

        def _forward(x, Wq, Wk, Wv, Wo, bo, ln1_g, ln1_b, W1, b1, W2, b2, ln2_g, ln2_b):
            for i in range(DEPTH):
                h = _layernorm(x, ln1_g[i], ln1_b[i])
                x = x + _linear_attn(h, Wq[i], Wk[i], Wv[i], Wo[i], bo[i])
                h = _layernorm(x, ln2_g[i], ln2_b[i])
                x = x + (jax.nn.gelu(h @ W1[i] + b1[i], approximate=False) @ W2[i] + b2[i])
            return x
        return _forward(x, Wq, Wk, Wv, Wo, bo, ln1_g, ln1_b, W1, b1, W2, b2, ln2_g, ln2_b)

    def _L0_ffn_ref(x, attention_mask, wr, br, w1, b1, w2, b2):
        import jax, jax.numpy as jnp
        import numpy as np
        B, S, D = (8, 128, 256)
        H = 4 * D
        CAPACITY = 0.5
        b, s, d = x.shape
        weights = (jnp.einsum('bsd,do->bso', x, wr) + br)[..., 0]
        k = max(1, int(CAPACITY * s))
        kk = k - 1 if k > 1 else 1
        _, idx = jax.lax.top_k(weights, k)
        sel_idx = idx[:, :kk]
        sel = jnp.take_along_axis(x, sel_idx[:, :, None], axis=1)
        h = jax.nn.gelu(jnp.einsum('bkd,dh->bkh', sel, w1) + b1)
        y = jnp.einsum('bkh,hd->bkd', h, w2) + b2
        w_sel = jnp.take_along_axis(weights, sel_idx, axis=1)
        y = y * w_sel[..., None]
        batch_idx = jnp.arange(b)[:, None]
        processed = jnp.zeros_like(x).at[batch_idx, sel_idx].set(y)
        return processed + x
    edge_index = jnp.stack([src, dst])
    xn = _layernorm(x, axis=-1)
    x = x + _L0_gnn_ref(xn, edge_index, L0_gnn_Wq, L0_gnn_bq, L0_gnn_Wk, L0_gnn_bk, L0_gnn_Wv, L0_gnn_bv, L0_gnn_Wskip, L0_gnn_bskip, L0_gnn_gamma, L0_gnn_beta) + _L0_mix_ref(xn[None], L0_mix_Wq, L0_mix_Wk, L0_mix_Wv, L0_mix_Wo, L0_mix_bo, L0_mix_ln1_g, L0_mix_ln1_b, L0_mix_W1, L0_mix_b1, L0_mix_W2, L0_mix_b2, L0_mix_ln2_g, L0_mix_ln2_b)[0]
    x = x + _L0_ffn_ref(_layernorm(x, axis=-1)[None], L0_ffn_attention_mask, L0_ffn_wr, L0_ffn_br, L0_ffn_w1, L0_ffn_b1, L0_ffn_w2, L0_ffn_b2)[0]
    return x

_drawn_inputs = setup_inputs


def setup_inputs(seed=0):
    import zlib

    import numpy as np

    out = dict(_drawn_inputs(seed))
    spreads = {'L0_gnn_bq': (0.0, 0.8),
     'L0_gnn_bk': (0.0, 0.8),
     'L0_gnn_bv': (0.0, 0.432),
     'L0_gnn_bskip': (0.0, 0.422),
     'L0_gnn_gamma': (1.0, 0.2),
     'L0_gnn_beta': (0.0, 0.1),
     'L0_mix_bo': (0.0, 0.1),
     'L0_mix_ln1_g': (1.0, 0.6),
     'L0_mix_ln1_b': (0.0, 0.8),
     'L0_mix_b1': (0.0, 0.319),
     'L0_mix_b2': (0.0, 0.1),
     'L0_mix_ln2_g': (1.0, 0.6),
     'L0_mix_ln2_b': (0.0, 0.8),
     'L0_ffn_b1': (0.0, 0.8),
     'L0_ffn_b2': (0.0, 0.8)}
    factors = {'L0_gnn_Wq': 8.0,
     'L0_gnn_Wk': 8.0,
     'L0_gnn_Wv': 3.677,
     'L0_mix_Wq': 8.0,
     'L0_mix_Wk': 8.0,
     'L0_mix_Wv': 4.307,
     'L0_mix_Wo': 4.02,
     'L0_ffn_wr': 7.496,
     'L0_ffn_w1': 8.0,
     'L0_ffn_w2': 8.0}
    for name, (base, spread) in spreads.items():
        noise = np.random.default_rng([zlib.crc32(name.encode()), seed]).standard_normal(out[name].shape)
        drawn = base * np.exp(spread * noise) if base else spread * noise
        out[name] = jnp.asarray(drawn.astype(out[name].dtype))
    for name, factor in factors.items():
        out[name] = (out[name] * factor).astype(out[name].dtype)
    return out
```

```python
import concourse.bass as bass
from concourse import mybir
from contextlib import ExitStack

F32 = mybir.dt.float32
I32 = mybir.dt.int32
ALU = mybir.AluOpType
ACT = mybir.ActivationFunctionType
AX = mybir.AxisListType

N, E, HID, HEADS, LAYERS, FF = 3125, 50000, 256, 8, 4, 1024
DH = HID // HEADS
P = 125
NT = N // P
G = 5
NG = NT // G
C = HID // 128
KC = FF // 128
EPP = E // P
T = 5
NB = EPP // T
VW = DH + 1
AW = HEADS * VW
TW = AW + HEADS
W7 = T + 2
KVW = HID + AW
HEAD_ROWS = N
SKIP = 8000
BIG = 1e30
EPS = 1e-5
GNN_SCALE = float(DH) ** -0.5
MIX_SCALE = float(DH) ** -0.25
CONSTS = 4 + 4
KEPT = max(1, int(0.5 * N)) - 1
RSQRT_SEED = float(0x5F3759DF)


class Order:

    def __init__(self, engine, sem):
        self.engine, self.sem, self.base, self.n = engine, sem, 0, 0

    def mark(self, instruction):
        self.n += 1
        instruction.then_inc(self.sem, 1)
        return self.n

    def need(self, n):
        self.engine.wait_ge(self.sem, self.base + n)

    def link(self, instruction):
        self.need(self.mark(instruction))


def gps_kernel(nc, A, out):
    ctx = ExitStack()
    with ctx:
        def sb(name, shape, dt=F32):
            return ctx.enter_context(nc.sbuf_tensor(name, shape, dt))

        def sem(name):
            return ctx.enter_context(nc.semaphore(name))

        def dram(name, shape):
            return nc.dram_tensor(name, shape, F32, kind="Internal").ap()

        kv_tab = dram("kv_tab", [N, KVW])
        q_tab = dram("q_tab", [N, HID])
        run_tab = dram("run_tab", [N + P, TW])
        skip_d = dram("skip_d", [N, HID])
        xn_d = dram("xn_d", [N, HID])
        w_d = dram("w_d", [NT, P])

        xm = sb("xm", [P, NT, HID])
        qe = sb("qe", [P, NT, HID])
        kst = sb("kst", [P, NT, HID])
        vst = sb("vst", [P, NT, AW])
        vmix = vst[:, :, :].rearrange("p n (c f) -> p n c f", c=C)
        vgnn = vst[:, :, :].rearrange("p n (h f) -> p n h f", h=HEADS)
        KV = sb("KV", [P, 2, T, KVW])
        QWB = sb("QWB", [P, N])
        ring = QWB[:, 0:G * HID].rearrange("p (j f) -> p j f", j=G)
        Q = QWB[:, 0:2 * T * HID].rearrange("p (k t f) -> p k t f", k=2, t=T)
        S = sb("S", [P, 2, T, TW])
        L7 = sb("L7", [P, 2, HEADS * W7])
        F7 = sb("F7", [P, HEADS * W7])
        M7 = sb("M7", [P, 2, HEADS * W7])
        E7 = sb("E7", [P, 2, HEADS * W7])
        P7 = sb("P7", [P, HEADS * W7 + 1])
        src_i = sb("src_i", [P, EPP], I32)
        dst_i = sb("dst_i", [P, EPP], I32)
        sct_i = sb("sct_i", [P, EPP], I32)
        same = sb("same", [P, EPP])
        idx = sb("idx", [P, 2, 3, T], I32)
        xh = sb("xh", [P, G, HID])
        dst_f = xh[:, :, :].rearrange("p j f -> p (j f)")[:, 0:EPP]
        goal = xh[:, :, :].rearrange("p j f -> p (j f)")[:, EPP:2 * EPP]
        ends = sb("ends", [P, 2])
        hT = sb("hT", [128, G, C, P])
        ek = xh
        hg = sb("hg", [128, 2, KC, P])
        w_big = sb("w_big", [128, C, FF])
        w_down = sb("w_down", [128, KC, HID])
        w_qkv = sb("w_qkv", [128, C, 3 * HID])
        w_o = sb("w_o", [128, C, HID])
        m_sb = sb("m_sb", [128, C, HID])
        ln1 = sb("ln1", [128, 2, LAYERS, C])
        ln2 = sb("ln2", [128, 2, LAYERS, C])
        b1_mix = sb("b1_mix", [128, LAYERS, KC])
        cur = sb("cur", [128, 4, C])
        cur_b1 = sb("cur_b1", [128, KC])
        b1_ffn = sb("b1_ffn", [128, KC])
        b2_b = sb("b2_b", [P, HID])
        bo_b = sb("bo_b", [DH, HID])
        b2_row = sb("b2_row", [1, HID])
        br_b = sb("br_b", [P, 1])
        vecs = w_qkv[0:P, 0, :].rearrange("p (i f) -> p i f", i=3)
        gnn_b = hg[0:P, :, :, :].rearrange("p a k n -> p (a k n)")[:, 0:4 * HID]
        onehots = hg[0:P, :, :, :].rearrange("p a k n -> p (a k n)")[:, 0:10 * P].rearrange("p (j s n) -> p j s n", j=G, s=2)
        ident = sb("ident", [128, 128])
        ones = sb("ones", [128, 128])
        zeros = sb("zeros", [128, 129])
        iota_tile = sb("iota_tile", [P, NT])
        head_row = sb("head_row", [P, 1])
        bst = sb("bst", [P, G, 6])
        mv = sb("mv", [P, NT, 2])
        mvs = sb("mvs", [P, G, 2])
        rstd = sb("rstd", [P, NT])
        nr_v = sb("nr_v", [P, NT])
        nr_i = sb("nr_i", [P, NT], I32)
        nr_t = sb("nr_t", [P, NT])
        kmx = sb("kmx", [P, HID])
        kmx_b = sb("kmx_b", [P, HID])
        iota_row, lower = kmx[:, 0:P], kmx[:, P:2 * P]
        km = sb("km", [128, C])
        s40 = sb("s40", [P, G * HEADS])
        mx8 = s40[:, :].rearrange("p (j h) -> p j h", j=G)
        r40 = sb("r40", [P, G * HEADS])
        rS = sb("rS", [128, C])
        BD = sb("BD", [128, C, 128])
        BDT = sb("BDT", [128, C, 128])
        dg = BDT
        hd = sb("hd", [P, TW])
        carried = hd[:, 0:AW]
        keys = sb("keys", [P, 4, HEADS])
        K2, V2 = w_o[0:HEADS, 0, 0:2 * P], w_o[0:HEADS, 1, 0:2 * P]
        F2, M2 = m_sb[0:HEADS, 0, 0:2 * P], m_sb[0:HEADS, 1, 0:2 * P]
        pen2 = BDT[0:HEADS, :, :].rearrange("h c n -> h (c n)")[:, 0:2 * P + 1]
        fac = sb("fac", [P, 2, HEADS])
        key_tile = sb("key_tile", [P, 2, NT])
        den = sb("den", [P, 2, HEADS])
        wcol = s40[:, 0:NT]
        wrow = kmx_b[0:NT, 0:P]
        cnt = BDT[0:P, :, :].rearrange("p c n -> p (c n)")[:, 0:3 * NT].rearrange("p (s n) -> p s n", s=3)
        LW = TW + 3 * HID
        fl = KV[:, :, :, :].rearrange("p a t f -> p (a t f)")[:, 0:G * LW].rearrange("p (j f) -> p j f", j=G)
        junk = KV[:, :, :, :].rearrange("p a t f -> p (a t f)")[:, 0:N]

        bank = [ctx.enter_context(nc.psum_tensor(f"bank{i}", [128, 512], F32)) for i in range(8)]

        def psT(j):
            return bank[j % 2][:, 0:C * P].rearrange("p (c n) -> p c n", c=C)

        def psQ(j):
            return bank[2 + j % 2][0:P, 0:HID]

        def psKV(j):
            return bank[4 + j % 2][0:P, :]

        def psQK(j):
            return bank[2 + j % 2][0:P, :]

        def psVS(j):
            return bank[4 + j % 2][0:P, :]

        def psY(j):
            return bank[6 + j % 2][0:P, 0:HID]

        def psH(j, half):
            return bank[2 + 2 * (j % 2) + half][:, 0:4 * P].rearrange("p (k n) -> p k n", k=4)

        def psC(c):
            return bank[2 + c][:, 0:129]

        def psB(j):
            return bank[2 + j % 2][0:P, 0:AW]

        psX, psM = bank[7], bank[4]

        s_x, s_idx, s_wg, s_const = sem("x_loaded"), sem("edges_loaded"), sem("gnn_weights_loaded"), sem("constants_loaded")
        s_wqkv, s_wo, s_w1, s_w2 = sem("wqkv_loaded"), sem("wo_loaded"), sem("w1_loaded"), sem("w2_loaded")
        s_vec = sem("last_vectors_loaded")
        gn = sem("made_constants")
        waited = sem("waited")
        xh_ready, pt_done, hT_ready = sem("xh_ready"), sem("transposed_plus_5"), sem("hT_ready_plus_2")
        xh_copied = sem("xh_copied_plus_1")
        gp_done, gp_free, gp_stored = sem("gnn_products_done"), sem("gnn_products_read_plus_2"), sem("gnn_rows_stored_plus_1")
        mix_start, tab_init = sem("value_ones_set"), sem("run_table_cleared")
        e_prep, e_gath, e_used, e_logit, e_exp, e_state, e_scat, e_idx = (
            sem("edge_tables_ready"), [sem(f"gathered{k}") for k in range(2)], sem("gather_buffer_used_plus_2"),
            sem("logits_ready"), sem("weights_ready"), sem("sums_ready"), [sem(f"scattered{k}_plus_16") for k in range(2)],
            sem("indices_copied"))
        qk_done, qk_act, qsub, qexp = (sem("qkv_done"), sem("qkv_read_by_act_plus_2"),
                                       sem("q_shifted_plus_2"), sem("q_exponentiated"))
        km_col, km_t, km_dg, km_b, km_ok = sem("kmax_columns"), sem("kmax_transposed"), sem("kmax_diagonal"), sem("kmax_spread"), sem("kmax_read")
        kd, ek_ok, ek_used = sem("k_shifted"), sem("k_exponentiated"), sem("ek_used_plus_5")
        ctx_done, bd_ok, bdt, bdt_ok, m_done, m_ok = (sem("context_done_plus_1"), sem("context_scaled"), sem("context_transposed"),
                                                      sem("contextT_read"), sem("M_done"), sem("M_read_plus_1"))
        at_done, at_free = sem("attention_done"), sem("attention_read_plus_2")
        h_done, hg_ok, y_done, y_free = sem("hidden_done"), sem("gelu_done_plus_1"), sem("ffn_done"), sem("ffn_read_plus_2")
        hd_in, hd_used = sem("first_runs_loaded"), sem("boundary_ready")
        b_t, b_k, b_m, b_f, b_d, b_e = sem("keys_transposed"), sem("keys_ready"), sem("maxima_found"), sem("maxima_transposed"), sem("factor_logits_ready"), sem("factors_ready")
        f_in = [sem(f"rows_loaded{j}") for j in range(G)]
        f_used, oh_ok, oh_ps, oh_free = sem("rows_used_plus_1"), sem("onehots_ready"), sem("boundary_sums_plus_1"), sem("boundary_sums_read_plus_2")
        f_pre, f_gelu, f_xmx, x1_ok = sem("gnn_out_ready"), sem("gnn_gelu_done"), sem("residuals_added"), sem("x1_ready")
        w_ok, w_t, w_row, w_st, w_b = sem("w_ready"), sem("w_transposed"), sem("w_row_ready"), sem("w_stored"), sem("w_spread")
        f_y, o_ok, o_st = sem("ffn_rows_ready"), sem("out_ready"), sem("out_stored")
        dve_order, act_order, pool_order = sem("dve_order"), sem("act_order"), sem("pool_order")

        x_v = A["x"].rearrange("(n p) f -> p n f", p=P)
        out_v = out.rearrange("(n p) f -> p n f", p=P)
        kv_v = kv_tab.rearrange("(n p) f -> p n f", p=P)
        q_v = q_tab.rearrange("(n p) f -> p n f", p=P)
        skip_v = skip_d.rearrange("(n p) f -> p n f", p=P)
        xn_v = xn_d.rearrange("(n p) f -> p n f", p=P)
        run_v = run_tab.rearrange("(n p) f -> p n f", p=P)

        def row(v):
            return v.rearrange("(a n) -> a n", a=1)

        PER_LAYER = 3 * NT

        def w_a(L, i):
            return L * PER_LAYER + i + NT

        def w_c1(L, i):
            return L * PER_LAYER + i + 2 * NT

        def w_c2(L, i):
            return L * PER_LAYER + i + 3 * NT

        def w_f(i):
            return i + NT + LAYERS * PER_LAYER

        def settle(engine):
            engine.sem_inc(waited, 1)

        block = ctx.enter_context(nc.Block())

        @block.sync
        def _(sp):
            sp.dma_start(xm[:, :, :], x_v).then_inc(s_x, 16)
            for i, w in enumerate(("L0_gnn_Wq", "L0_gnn_Wk", "L0_gnn_Wv", "L0_gnn_Wskip")):
                sp.dma_start(w_big[:, :, i * HID:(i + 1) * HID], A[w].rearrange("(c k) n -> k c n", k=128)).then_inc(s_wg, 16)
            for i, b in enumerate(("L0_gnn_bq", "L0_gnn_bk", "L0_gnn_bv", "L0_gnn_bskip")):
                sp.dma_start(gnn_b[:, i * HID:(i + 1) * HID], row(A[b]).to_broadcast([P, HID])).then_inc(s_wg, 16)
            sp.dma_start(src_i[:, :], A["src"].rearrange("(p t) -> p t", p=P)).then_inc(s_idx, 16)
            sp.dma_start(dst_i[:, :], A["dst"].rearrange("(p t) -> p t", p=P)).then_inc(s_idx, 16)
            for t, (g_, b_) in ((ln1, ("L0_mix_ln1_g", "L0_mix_ln1_b")), (ln2, ("L0_mix_ln2_g", "L0_mix_ln2_b"))):
                for i, v in enumerate((g_, b_)):
                    sp.dma_start(t[:, i, :, :], A[v].rearrange("l (c k) -> k l c", k=128), allow_slow_non_contiguous=True).then_inc(s_const, 16)
            sp.dma_start(b1_mix[:, :, :], A["L0_mix_b1"].rearrange("l (c k) -> k l c", k=128), allow_slow_non_contiguous=True).then_inc(s_const, 16)
            sp.dma_start(b1_ffn[:, :], A["L0_ffn_b1"].rearrange("(c k) -> k c", k=128), allow_slow_non_contiguous=True).then_inc(s_const, 16)
            sp.dma_start(b2_row[:, :], row(A["L0_ffn_b2"])).then_inc(s_const, 16)
            sp.dma_start(br_b[:, :], row(A["L0_ffn_br"]).to_broadcast([P, 1])).then_inc(s_const, 16)
            sp.wait_ge(gn, 4)
            sp.dma_start(run_v, hd[:, :].unsqueeze(1).to_broadcast([P, NT + 1, TW])).then_inc(tab_init, 16)
            with sp.Fori(0, NG) as g:
                sp.wait_ge(gp_free, g * G + G + 2)
                settle(sp)
                sp.wait_ge(xh_copied, g * G + G + 1)
                settle(sp)
                sp.dma_start(q_v[:, bass.ds(g * G, G), :], qe[:, bass.ds(g * G, G), :]).then_inc(gp_stored, 16)
                sp.dma_start(kv_v[:, bass.ds(g * G, G), 0:HID], kst[:, bass.ds(g * G, G), :]).then_inc(gp_stored, 16)
                sp.dma_start(kv_v[:, bass.ds(g * G, G), HID:KVW], vst[:, bass.ds(g * G, G), :]).then_inc(gp_stored, 16)
                sp.dma_start(xn_v[:, bass.ds(g * G, G), :], xm[:, bass.ds(g * G, G), :]).then_inc(gp_stored, 16)
                sp.dma_start(skip_v[:, bass.ds(g * G, G), :], ring[:, :, :]).then_inc(gp_stored, 16)
            with sp.Fori(0, LAYERS) as L:
                sp.wait_ge(ctx_done, L + 1)
                for i, w in enumerate(("L0_mix_Wq", "L0_mix_Wk", "L0_mix_Wv")):
                    sp.dma_start(w_qkv[:, :, i * HID:(i + 1) * HID], A[w][bass.ds(L, 1), :, :].rearrange("l (c k) n -> k (l c) n", k=128)).then_inc(s_wqkv, 16)
                sp.wait_ge(m_ok, L + 1)
                sp.dma_start(w_o[:, :, :], A["L0_mix_Wo"][bass.ds(L, 1), :, :].rearrange("l (c k) n -> k (l c) n", k=128)).then_inc(s_wo, 16)
                sp.dma_start(bo_b[:, :], A["L0_mix_bo"][bass.ds(L, 1), :].to_broadcast([DH, HID])).then_inc(s_wo, 16)
                sp.wait_ge(gp_done, NT)
                sp.wait_ge(y_free, L * NT + 2)
                sp.dma_start(w_big[:, :, :], A["L0_mix_W1"][bass.ds(L, 1), :, :].rearrange("l (c k) n -> k (l c) n", k=128)).then_inc(s_w1, 16)
                sp.dma_start(w_down[:, :, :], A["L0_mix_W2"][bass.ds(L, 1), :, :].rearrange("l (c k) n -> k (l c) n", k=128)).then_inc(s_w2, 16)
                sp.dma_start(b2_b[:, :], A["L0_mix_b2"][bass.ds(L, 1), :].to_broadcast([P, HID])).then_inc(s_w2, 16)
            sp.wait_ge(ctx_done, LAYERS + 1)
            for i, v in enumerate(("L0_gnn_gamma", "L0_gnn_beta")):
                sp.dma_start(vecs[:, i, :], row(A[v]).to_broadcast([P, HID])).then_inc(s_vec, 16)
            sp.dma_start(vecs[:, 2, :], A["L0_ffn_wr"].rearrange("n a -> a n").to_broadcast([P, HID])).then_inc(s_vec, 16)
            for k in range(2):
                sp.wait_ge(e_scat[k], 16 + 16 * T * (NB // 2))
            sp.dma_start(hd[:, :], run_tab[HEAD_ROWS:HEAD_ROWS + P, :]).then_inc(hd_in, 16)
            sp.wait_ge(e_state, NB)
            sp.wait_ge(y_free, LAYERS * NT + 2)
            sp.dma_start(w_big[:, :, :], A["L0_ffn_w1"].rearrange("(c k) n -> k c n", k=128)).then_inc(s_w1, 16)
            sp.dma_start(w_down[:, :, :], A["L0_ffn_w2"].rearrange("(c k) n -> k c n", k=128)).then_inc(s_w2, 16)
            with sp.Fori(0, NG) as g:
                for j in range(G):
                    i = g * G + j
                    sp.wait_ge(f_used, g * G + 1)
                    sp.dma_start(fl[:, j:j + 1, 0:TW], run_v[:, bass.ds(i, 1), :]).then_inc(f_in[j], 16)
                    sp.dma_start(fl[:, j:j + 1, TW:TW + HID], skip_v[:, bass.ds(i, 1), :]).then_inc(f_in[j], 16)
                    sp.dma_start(fl[:, j:j + 1, TW + HID:TW + 2 * HID], xn_v[:, bass.ds(i, 1), :]).then_inc(f_in[j], 16)
                    sp.dma_start(fl[:, j:j + 1, TW + 2 * HID:LW], x_v[:, bass.ds(i, 1), :]).then_inc(f_in[j], 16)
            sp.wait_ge(w_row, 1)
            sp.dma_start(w_d, wrow[:, :]).then_inc(w_st, 16)
            sp.wait_ge(w_st, 16)
            sp.dma_start(QWB[:, :], w_d.rearrange("n p -> (n p)").rearrange("(a f) -> a f", a=1).to_broadcast([P, N])).then_inc(w_b, 16)
            with sp.Fori(0, NG) as g:
                sp.wait_ge(o_ok, g + 1)
                sp.dma_start(out_v[:, bass.ds(g * G, G), :], vst[:, bass.ds(g * G, G), 0:HID]).then_inc(o_st, 16)
            sp.wait_ge(o_st, 16 * NG)

        @block.gpsimd
        def _(gp):
            order = Order(gp, pool_order)
            gp.memset(ident[:, :], 0.0).then_inc(gn, 1)
            gp.memset(ones[:, :], 1.0).then_inc(gn, 1)
            gp.memset(zeros[:, :], 0.0)
            gp.memset(hd[:, 0:AW], 0.0).then_inc(gn, 1)
            gp.memset(hd[:, AW:TW], -BIG).then_inc(gn, 1)
            gp.wait_ge(gn, 4)
            gp.iota(iota_tile[:, :], pattern=[[P, NT]], base=0, channel_multiplier=0, allow_small_or_imprecise_dtypes=True).then_inc(gn, 1)
            gp.iota(head_row[:, :], pattern=[[0, 1]], base=HEAD_ROWS, channel_multiplier=1, allow_small_or_imprecise_dtypes=True).then_inc(gn, 1)
            gp.affine_select(out=ident[:, :], in_=ident[:, :], compare_op=ALU.not_equal, fill=1.0, base=0,
                             pattern=[[-1, 128]], channel_multiplier=1).then_inc(gn, 1)

            def gather(b, k):
                gp.wait_ge(e_used, b + 1)
                order.mark(gp.tensor_copy(idx[:, k, 0, :], src_i[:, bass.ds(b * T, T)]))
                order.link(gp.tensor_copy(idx[:, k, 1, :], dst_i[:, bass.ds(b * T, T)]))
                settle(gp)
                for t in range(T):
                    gp.indirect_dma_start(out=KV[:, k, t, :], out_offset=None, in_=kv_tab,
                                          in_offset=bass.IndirectOffsetOnAxis(ap=idx[:, k, 0, t:t + 1], axis=0)).then_inc(e_gath[k], 16)
                    gp.indirect_dma_start(out=Q[:, k, t, :], out_offset=None, in_=q_tab,
                                          in_offset=bass.IndirectOffsetOnAxis(ap=idx[:, k, 1, t:t + 1], axis=0)).then_inc(e_gath[k], 16)

            def scatter(b, turn, k):
                gp.wait_ge(e_scat[k], turn * 16 * T + 16)
                order.link(gp.tensor_copy(idx[:, k, 2, :], sct_i[:, bass.ds(b * T, T)]))
                gp.wait_ge(e_state, b + 1)
                settle(gp)
                for t in range(T):
                    gp.indirect_dma_start(out=run_tab, out_offset=bass.IndirectOffsetOnAxis(ap=idx[:, k, 2, t:t + 1], axis=0),
                                          in_=S[:, k, t, :], in_offset=None, bounds_check=N + P - 1, oob_is_err=False).then_inc(e_scat[k], 16)

            gp.wait_ge(e_prep, 1)
            gp.wait_ge(gp_stored, 5 * 16 * NG + 1)
            gp.wait_ge(tab_init, 16)
            for k in range(2):
                gp.indirect_dma_start(out=run_tab, out_offset=bass.IndirectOffsetOnAxis(ap=sct_i[:, EPP - 1:EPP], axis=0),
                                      in_=S[:, k, 0, :], in_offset=None, bounds_check=N + P - 1, oob_is_err=False).then_inc(e_scat[k], 16)
            gather(0, 0)
            gather(1, 1)
            scatter(0, 0, 0)
            PER = 2 * 3
            start = order.n
            with gp.Fori(0, NB // 2 - 1) as r:
                order.base, order.n = start + r * PER, 0
                gather(2 * r + 2, 0)
                scatter(2 * r + 1, r, 1)
                gather(2 * r + 3, 1)
                scatter(2 * r + 2, r + 1, 0)
                assert order.n == PER
            order.base, order.n = 0, start + (NB // 2 - 1) * PER
            scatter(NB - 1, NB // 2 - 1, 1)
            gp.wait_ge(s_vec, 3 * 16)
            gp.wait_ge(y_free, LAYERS * NT + 2)
            gp.iota(iota_row[:, :], pattern=[[1, P]], base=0, channel_multiplier=0, allow_small_or_imprecise_dtypes=True).then_inc(gn, 1)
            gp.affine_select(out=lower[:, :], in_=ones[0:P, 0:P], compare_op=ALU.is_gt, fill=0.0, base=0,
                             pattern=[[-1, P]], channel_multiplier=1).then_inc(gn, 1)
            base = order.n
            with gp.Fori(0, NG) as g:
                order.base, order.n = base + g * G, 0
                for j in range(G):
                    xr = fl[:, j, TW + 2 * HID:LW]
                    gp.wait_ge(f_in[j], g * 64 + 64)
                    order.link(gp.tensor_tensor(xr, xr, xm[:, g * G + j, :], ALU.add))
                    gp.tensor_tensor(xr, xr, vecs[:, 1, :], ALU.add).then_inc(f_xmx, 1)
                assert order.n == G

        @block.vector
        def _(v):
            order = Order(v, dve_order)
            link, mark, need = order.link, order.mark, order.need
            total = [0]

            def enter(register, per):
                order.base, order.n = total[0] + register * per, 0

            def leave(turns, per):
                assert order.n == per, (order.n, per)
                total[0] += turns * per
                order.base, order.n = 0, total[0]

            def straight():
                total[0] = order.n

            def inv_std(n0, n):
                a, y, t = nr_v[:, 0:n], nr_i[:, 0:n].bitcast(F32), nr_t[:, 0:n]
                link(nc.vector.tensor_scalar(a, mv[:, bass.ds(n0, n), 1], EPS, None, ALU.add))
                link(nc.vector.tensor_scalar(nr_i[:, 0:n], nr_v[:, 0:n].bitcast(I32), -0.5, RSQRT_SEED, ALU.mult, ALU.add))
                for step in range(3):
                    link(nc.vector.tensor_tensor(t, y, y, ALU.mult))
                    link(nc.vector.tensor_tensor(t, t, a, ALU.mult))
                    link(nc.vector.tensor_scalar(t, t, -0.5, 1.5, ALU.mult, ALU.add))
                    link(nc.vector.tensor_tensor(rstd[:, bass.ds(n0, n)] if step == 2 else y, y, t, ALU.mult))

            INV = 14

            v.sem_inc(pt_done, G)
            for s in (xh_copied, gp_stored, hg_ok, ctx_done, m_ok, oh_ps, f_used):
                v.sem_inc(s, 1)
            v.sem_inc(hT_ready, 2)
            v.sem_inc(gp_free, 2)
            v.sem_inc(e_used, 2)
            v.sem_inc(qsub, 2)
            v.sem_inc(f_y, 2)
            v.sem_inc(qk_act, 2)
            v.sem_inc(ek_used, G)
            v.sem_inc(at_free, 2)
            v.sem_inc(y_free, 2)
            v.sem_inc(oh_free, 2)

            v.wait_ge(s_idx, 32)
            v.wait_ge(gn, 7)
            link(nc.vector.tensor_copy(dst_f[:, :], dst_i[:, :]))
            mark(nc.vector.memset(same[:, 0:1], 0.0))
            link(nc.vector.tensor_tensor(same[:, 1:EPP], dst_f[:, 1:EPP], dst_f[:, 0:EPP - 1], ALU.is_equal))
            link(nc.vector.tensor_scalar(goal[:, :], dst_f[:, :], -1.0, head_row[:, 0:1], ALU.mult, ALU.add))
            link(nc.vector.scalar_tensor_tensor(out=goal[:, :], in0=dst_f[:, :], scalar=dst_f[:, 0:1], in1=goal[:, :],
                                                op0=ALU.is_equal, op1=ALU.mult))
            link(nc.vector.tensor_tensor(goal[:, :], goal[:, :], dst_f[:, :], ALU.add))
            link(nc.vector.scalar_tensor_tensor(out=goal[:, 0:EPP - 1], in0=same[:, 1:EPP], scalar=float(SKIP), in1=goal[:, 0:EPP - 1],
                                                op0=ALU.mult, op1=ALU.add))
            link(nc.vector.memset(goal[:, EPP - 1:EPP], float(SKIP)))
            link(nc.vector.tensor_copy(sct_i[:, :], goal[:, :]))
            mark(nc.vector.tensor_copy(ends[:, 0:1], dst_f[:, 0:1]))
            link(nc.vector.tensor_copy(ends[:, 1:2], dst_f[:, EPP - 1:EPP]))
            mark(nc.vector.memset(P7[:, :], -BIG))
            mark(nc.vector.memset(L7[:, :, :], -BIG))
            mark(nc.vector.memset(M7[:, :, :], -BIG))
            mark(nc.vector.memset(S[:, :, :, :], 0.0))
            mark(nc.vector.memset(BD[:, :, :], 0.0))
            mark(nc.vector.tensor_scalar(key_tile[:, 0, :], iota_tile[:, :], -1.0, ends[:, 0:1], ALU.mult, ALU.add))
            mark(nc.vector.tensor_scalar(key_tile[:, 1, :], iota_tile[:, :], -1.0, ends[:, 1:2], ALU.mult, ALU.add))
            link(nc.vector.memset(vgnn[:, :, :, DH:VW], 1.0))
            v.sem_inc(e_prep, 1)
            straight()

            v.wait_ge(s_x, 16)

            def aggregate(g):
                settle(v)
                for j in range(G):
                    n = mark(nc.vector.bn_aggr(mvs[:, j, :], bst[:, j, :]))
                need(n)
                settle(v)
                link(nc.vector.tensor_copy(mv[:, bass.ds(g * G, G), :], mvs[:, :, :]))

            def stats(g):
                for j in range(G):
                    n = mark(nc.vector.bn_stats(bst[:, j, :], xm[:, g * G + j, :]))
                need(n)
                aggregate(g)

            with v.Fori(0, NG) as g:
                enter(g, 2 * G + 1)
                stats(g)
            leave(NG, 2 * G + 1)
            inv_std(0, NT)
            straight()
            v.wait_ge(s_wg, 8 * 16)
            with v.Fori(0, NG) as g:
                for j in range(G):
                    i = g * G + j
                    v.wait_ge(pt_done, i + 1)
                    v.wait_ge(xh_copied, g * G + 1)
                    nc.vector.tensor_scalar(xh[:, j, :], xm[:, i, :], mv[:, i, 0:1], rstd[:, bass.ds(i, 1)],
                                            ALU.subtract, ALU.mult).then_inc(xh_ready, 1)
                v.wait_ge(gp_stored, g * 5 * 16 + 1)
                for j in range(G):
                    i = g * G + j
                    v.wait_ge(gp_done, i + 1)
                    nc.vector.tensor_tensor(qe[:, i, :], psQK(j)[:, 0:HID], gnn_b[:, 0:HID], ALU.add)
                    nc.vector.tensor_tensor(kst[:, i, :], psQK(j)[:, HID:2 * HID], gnn_b[:, HID:2 * HID], ALU.add)
                    nc.vector.tensor_tensor(vgnn[:, i, :, 0:DH], psVS(j)[:, 0:HID].rearrange("p (h d) -> p h d", d=DH),
                                            gnn_b[:, 2 * HID:3 * HID].rearrange("p (h d) -> p h d", d=DH), ALU.add)
                    nc.vector.tensor_tensor(ring[:, j, :], psVS(j)[:, HID:2 * HID], gnn_b[:, 3 * HID:4 * HID], ALU.add).then_inc(gp_free, 1)

            v.wait_ge(xh_ready, NT)
            mark(nc.vector.memset(mv[:, :, 0], 0.0))
            link(nc.vector.tensor_tensor(mv[:, :, 1], mv[:, :, 1], rstd[:, :], ALU.mult))
            link(nc.vector.tensor_tensor(mv[:, :, 1], mv[:, :, 1], rstd[:, :], ALU.mult))
            straight()

            def seven(t):
                return t.rearrange("p (h w) -> p h w", h=HEADS)

            def edge_logits(b, turn, k):
                prev = 1 - k
                v.wait_ge(e_gath[k], turn * (2 * T * 16) + 2 * T * 16)
                mark(nc.vector.tensor_scalar(seven(P7[:, 0:HEADS * W7])[:, :, 1:1 + T],
                                                   same[:, bass.ds(b * T, T)].unsqueeze(1).to_broadcast([P, HEADS, T]),
                                                   -1.0, BIG, ALU.add, ALU.mult))
                mark(nc.vector.tensor_copy(seven(L7[:, k, :])[:, :, 0], seven(M7[:, prev, :])[:, :, T]))
                link(nc.vector.tensor_tensor(Q[:, k, :, :], Q[:, k, :, :], KV[:, k, :, 0:HID], ALU.mult))
                link(nc.vector.tensor_reduce(out=seven(L7[:, k, :])[:, :, 1:1 + T].rearrange("p h t -> p t h"),
                                             in_=Q[:, k, :, :].rearrange("p t (h d) -> p t h d", d=DH), axis=AX.X, op=ALU.add))
                link(nc.vector.tensor_tensor_scan(F7[:, :], P7[:, 0:HEADS * W7], L7[:, k, :], initial=-BIG, op0=ALU.add, op1=ALU.max))
                link(nc.vector.tensor_tensor_scan(M7[:, k, ::-1], P7[:, 1:HEADS * W7 + 1][:, ::-1], F7[:, ::-1], initial=-BIG,
                                                  op0=ALU.add, op1=ALU.max))
                nc.vector.tensor_tensor(E7[:, k, :], L7[:, k, :], M7[:, k, :], ALU.subtract).then_inc(e_logit, 1)

            def edge_sums(b, turn, k):
                prev = 1 - k
                v.wait_ge(e_scat[k], turn * 16 * T + 16)
                v.wait_ge(e_exp, b + 1)
                w = seven(E7[:, k, :])
                mark(nc.vector.tensor_tensor(seven(carried[:, :]), seven(S[:, prev, T - 1, 0:AW]),
                                             w[:, :, 0:1].to_broadcast([P, HEADS, VW]), ALU.mult))
                mark(nc.vector.tensor_copy(S[:, k, :, AW:TW], seven(M7[:, k, :])[:, :, 1:1 + T].rearrange("p h t -> p t h")))
                n = mark(nc.vector.tensor_tensor(S[:, k, :, 0:AW].rearrange("p t (h w) -> p t h w", h=HEADS),
                                             KV[:, k, :, HID:KVW].rearrange("p t (h w) -> p t h w", h=HEADS),
                                             w[:, :, 1:1 + T].rearrange("p h t -> p t h").unsqueeze(3).to_broadcast([P, T, HEADS, VW]), ALU.mult))
                need(n)
                v.sem_inc(e_used, 1)
                for t in range(T):
                    before = carried[:, :] if t == 0 else S[:, k, t - 1, 0:AW]
                    ins = nc.vector.scalar_tensor_tensor(out=S[:, k, t, 0:AW], in0=before, scalar=same[:, bass.ds(b * T + t, 1)],
                                                         in1=S[:, k, t, 0:AW], op0=ALU.mult, op1=ALU.add)
                    link(ins)
                v.sem_inc(e_state, 1)

            EDGE = 9 + T

            def edge_steps(turn):
                b = 2 * turn
                edge_logits(b, turn, 0)
                yield
                edge_sums(b, turn, 0)
                edge_logits(b + 1, turn, 1)
                yield
                edge_sums(b + 1, turn, 1)
                yield

            v.wait_ge(gp_stored, 5 * 16 * NG + 1)
            nc.vector.memset(vmix[:, :, :, 128:129], 1.0).then_inc(mix_start, 1)

            def residual(L, g, done, free, edges=None):
                for j in range(G + 1):
                    i = g * G + j
                    if edges and j in (0, 2, 4):
                        next(edges)
                    if j < G:
                        v.wait_ge(done, L * NT + i + 1)
                        nc.vector.tensor_tensor(xm[:, i, :], psY(j), xm[:, i, :], ALU.add).then_inc(free, 1)
                    if j:
                        v.wait_ge(free, L * NT + i - 1 + 3)
                        settle(v)
                        n = mark(nc.vector.bn_stats(bst[:, j - 1, :], xm[:, i - 1, :]))
                need(n)
                aggregate(g)

            def layer_a(L, g):
                for j in range(G):
                    i = g * G + j
                    v.wait_ge(pt_done, w_a(L, i) + 1)
                    nc.vector.tensor_scalar(xh[:, j, :], xm[:, i, :], mv[:, i, 0:1], rstd[:, bass.ds(i, 1)],
                                            ALU.subtract, ALU.mult).then_inc(xh_ready, 1)
                edges = edge_steps(L * (2 * NG) + g)
                for j in range(G):
                    i = g * G + j
                    if j in (0, 2, 4):
                        next(edges)
                    ps = psQ(j).rearrange("p (h d) -> p h d", d=DH)
                    v.wait_ge(qk_done, L * NT + i + 1)
                    link(nc.vector.tensor_reduce(out=mx8[:, j, :], in_=ps, axis=AX.X, op=ALU.max))
                    nc.vector.tensor_tensor(qe[:, i, :].rearrange("p (h d) -> p h d", d=DH), ps,
                                            mx8[:, j, :].unsqueeze(2).to_broadcast([P, HEADS, DH]), ALU.subtract).then_inc(qsub, 1)
                    v.wait_ge(qk_act, L * NT + i + 3)
                    n = mark(nc.vector.tensor_tensor(kmx[:, :], kmx[:, :], kst[:, i, :], ALU.max))
                need(n)

            LA = 2 * G + 2 * EDGE
            assert NB == LAYERS * 2 * NG * 2

            with v.Fori(0, LAYERS) as L:
                LAYER = (14 + 1) + NG * LA + 4 + 12 + NG * (3 + 2 * G) + 14 + NG * (1 + 3 * G + 2 * EDGE)
                lbase = total[0] + L * LAYER
                used = [0]

                def part(register, per):
                    order.base, order.n = lbase + used[0] + register * per, 0

                def end_part(turns, per):
                    assert order.n == per, (order.n, per)
                    used[0] += turns * per

                part(0, 15)
                inv_std(0, NT)
                link(nc.vector.memset(kmx[:, :], -3e38))
                end_part(1, 15)
                settle(v)
                with v.Fori(0, NG) as g:
                    part(g, LA)
                    layer_a(L, g)
                end_part(NG, LA)
                part(0, 4)
                v.sem_inc(km_col, 1)
                v.wait_ge(km_t, L + 1)
                link(nc.vector.tensor_reduce(out=km[:, :], in_=psX[:, 0:C * P].rearrange("p (c n) -> p c n", c=C), axis=AX.X, op=ALU.max))
                for c in range(C):
                    link(nc.vector.tensor_scalar(dg[:, c, :], ident[:, :], km[:, c:c + 1], None, ALU.mult))
                v.sem_inc(km_dg, 1)
                v.wait_ge(km_b, L + 1)
                link(nc.vector.tensor_copy(kmx_b[:, :], psX[0:P, 256:512]))
                end_part(1, 4)
                v.wait_ge(qk_act, L * NT + NT + 2)
                settle(v)
                with v.Fori(0, NG) as g:
                    for j in range(G):
                        v.wait_ge(ek_used, L * NT + g * G + j + 1)
                        nc.vector.tensor_tensor(ek[:, j, :], kst[:, g * G + j, :], kmx_b[:, :], ALU.subtract).then_inc(kd, 1)
                part(0, 12)
                v.wait_ge(ctx_done, L + 2)
                for c in range(C):
                    n = mark(nc.vector.reciprocal(rS[:, c:c + 1], psC(c)[:, 128:129]))
                need(n)
                for c in range(C):
                    for h in range(4):
                        r = slice(h * DH, h * DH + DH)
                        n = mark(nc.vector.tensor_scalar(BD[r, c, r], psC(c)[r, r], rS[r, c:c + 1], None, ALU.mult))
                need(n)
                v.sem_inc(bd_ok, 1)
                v.wait_ge(bdt, L + 1)
                nc.vector.tensor_copy(BDT[:, :, :], psX[:, 0:256].rearrange("p (c n) -> p c n", c=C)).then_inc(bdt_ok, 1)
                v.wait_ge(m_done, L + 1)
                link(nc.vector.tensor_copy(m_sb[:, :, :], psM[:, :].rearrange("p (c n) -> p c n", c=C)))
                link(nc.vector.tensor_tensor(m_sb[0:DH, 0, :], m_sb[0:DH, 0, :], bo_b[:, :], ALU.add))
                end_part(1, 12)
                v.sem_inc(m_ok, 1)
                v.wait_ge(qexp, L * NT + NT)
                settle(v)
                PER = 3 + 2 * G
                with v.Fori(0, NG) as g:
                    part(g, PER)
                    link(nc.vector.tensor_reduce(out=s40[:, :], in_=qe[:, bass.ds(g * G, G), :].rearrange("p j (h d) -> p (j h) d", d=DH),
                                                 axis=AX.X, op=ALU.add))
                    link(nc.vector.reciprocal(r40[:, :], s40[:, :]))
                    for j in range(G):
                        i = g * G + j
                        v.wait_ge(pt_done, w_c1(L, i) + 1)
                        nc.vector.tensor_tensor(xh[:, j, :].rearrange("p (h d) -> p h d", d=DH), qe[:, i, :].rearrange("p (h d) -> p h d", d=DH),
                                                r40[:, j * HEADS:(j + 1) * HEADS].unsqueeze(2).to_broadcast([P, HEADS, DH]), ALU.mult).then_inc(xh_ready, 1)
                    residual(L, g, at_done, at_free)
                end_part(NG, PER)
                part(0, 14)
                inv_std(0, NT)
                end_part(1, 14)
                v.wait_ge(s_w2, L * 32 + 32)
                settle(v)
                PER = 1 + 3 * G + 2 * EDGE
                with v.Fori(0, NG) as g:
                    part(g, PER)
                    for j in range(G):
                        i = g * G + j
                        v.wait_ge(pt_done, w_c2(L, i) + 1)
                        nc.vector.tensor_scalar(xh[:, j, :], xm[:, i, :], mv[:, i, 0:1], rstd[:, bass.ds(i, 1)],
                                                ALU.subtract, ALU.mult).then_inc(xh_ready, 1)
                    for j in range(G):
                        n = mark(nc.vector.tensor_tensor(xm[:, g * G + j, :], xm[:, g * G + j, :], b2_b[:, :], ALU.add))
                    need(n)
                    residual(L, g, y_done, y_free, edge_steps(L * (2 * NG) + NG + g))
                end_part(NG, PER)
                assert used[0] == LAYER
            total[0] += LAYERS * LAYER
            order.base, order.n = 0, total[0]

            v.wait_ge(hd_in, 16)
            last = S[:, 1, T - 1, :]
            mark(nc.vector.tensor_copy(keys[:, 0, :], hd[:, AW:TW]))
            mark(nc.vector.tensor_copy(keys[:, 1, :], last[:, AW:TW]))
            mark(nc.vector.tensor_copy(keys[:, 2, :], ends[:, 0:1].to_broadcast([P, HEADS])))
            link(nc.vector.tensor_copy(keys[:, 3, :], ends[:, 1:2].to_broadcast([P, HEADS])))
            v.sem_inc(b_k, 1)
            v.wait_ge(b_t, 1)
            for i, t in enumerate((V2, K2)):
                for s in range(2):
                    n = mark(nc.vector.tensor_copy(t[:, :].rearrange("h (p s) -> h s p", s=2)[:, s, :],
                                                   psX[0:HEADS, (2 * i + s) * 128:(2 * i + s) * 128 + P]))
            need(n)
            link(nc.vector.memset(pen2[:, :], -BIG))
            link(nc.vector.tensor_tensor(F2[:, 1:2 * P], K2[:, 1:2 * P], K2[:, 0:2 * P - 1], ALU.is_equal))
            link(nc.vector.tensor_scalar(pen2[:, 1:2 * P], F2[:, 1:2 * P], -1.0, BIG, ALU.add, ALU.mult))
            link(nc.vector.tensor_tensor_scan(F2[:, :], pen2[:, 0:2 * P], V2[:, :], initial=-BIG, op0=ALU.add, op1=ALU.max))
            link(nc.vector.tensor_tensor_scan(M2[:, ::-1], pen2[:, 1:2 * P + 1][:, ::-1], F2[:, ::-1], initial=-BIG, op0=ALU.add, op1=ALU.max))
            for s in range(2):
                n = mark(nc.vector.tensor_copy(F2[:, s * P:(s + 1) * P], M2[:, :].rearrange("h (p s) -> h s p", s=2)[:, s, :]))
            need(n)
            v.sem_inc(b_m, 1)
            v.wait_ge(b_f, 1)
            for s in range(2):
                n = mark(nc.vector.tensor_tensor(fac[:, s, :], keys[:, s, :], bank[6][0:P, s * HEADS:(s + 1) * HEADS], ALU.subtract))
            need(n)
            v.sem_inc(b_d, 1)
            v.wait_ge(b_e, 1)
            for s, t in enumerate((hd[:, 0:AW], last[:, 0:AW])):
                rows = t.rearrange("p (h w) -> p h w", h=HEADS)
                n = mark(nc.vector.tensor_tensor(rows, rows, fac[:, s, :].unsqueeze(2).to_broadcast([P, HEADS, VW]), ALU.mult))
            need(n)
            v.sem_inc(hd_used, 1)
            straight()

            v.wait_ge(s_vec, 3 * 16)
            v.wait_ge(s_const, 16 * CONSTS)
            v.wait_ge(gn, 9)
            per_group = 17 * G + 2 + 2 * INV
            with v.Fori(0, NG) as g:
                enter(g, per_group)
                for j in range(G):
                    i = g * G + j
                    if j == 0:
                        v.wait_ge(oh_ps, g * G + 1)
                    for s in range(2):
                        n = mark(nc.vector.tensor_scalar(onehots[:, j, s, :], iota_row[:, :], key_tile[:, s, bass.ds(i, 1)], None, ALU.is_equal))
                    need(n)
                    v.sem_inc(oh_ok, 1)
                for j in range(G):
                    i = g * G + j
                    rows = fl[:, j, 0:AW].rearrange("p (h w) -> p h w", h=HEADS)
                    gn_out = fl[:, j, 0:HID]
                    v.wait_ge(f_in[j], g * 64 + 64)
                    v.wait_ge(oh_ps, i + 2)
                    link(nc.vector.tensor_tensor(fl[:, j, 0:AW], fl[:, j, 0:AW], psB(j), ALU.add))
                    v.sem_inc(oh_free, 1)
                    link(nc.vector.tensor_scalar(den[:, 0, :], rows[:, :, DH], 1e-30, None, ALU.max))
                    link(nc.vector.reciprocal(den[:, 1, :], den[:, 0, :]))
                    link(nc.vector.tensor_tensor(ring[:, j, :].rearrange("p (h d) -> p h d", d=DH), rows[:, :, 0:DH],
                                                 den[:, 1, :].unsqueeze(2).to_broadcast([P, HEADS, DH]), ALU.mult))
                    nc.vector.tensor_tensor(ring[:, j, :], ring[:, j, :], fl[:, j, TW:TW + HID], ALU.add).then_inc(f_pre, 1)
                for j in range(G):
                    i = g * G + j
                    v.wait_ge(f_gelu, i + 1)
                    link(nc.vector.tensor_tensor(ring[:, j, :], ring[:, j, :], fl[:, j, TW + HID:TW + 2 * HID], ALU.add))
                    n = mark(nc.vector.bn_stats(bst[:, j, :], ring[:, j, :]))
                need(n)
                aggregate(g)
                inv_std(g * G, G)
                for j in range(G):
                    i = g * G + j
                    link(nc.vector.tensor_scalar(ring[:, j, :], ring[:, j, :], mv[:, i, 0:1], rstd[:, bass.ds(i, 1)], ALU.subtract, ALU.mult))
                    link(nc.vector.tensor_tensor(ring[:, j, :], ring[:, j, :], vecs[:, 0, :], ALU.mult))
                    v.wait_ge(f_xmx, i + 1)
                    link(nc.vector.tensor_tensor(ring[:, j, :], ring[:, j, :], fl[:, j, TW + 2 * HID:LW], ALU.add))
                    v.sem_inc(f_used, 1)
                    n = mark(nc.vector.bn_stats(bst[:, j, :], ring[:, j, :]))
                need(n)
                aggregate(g)
                inv_std(g * G, G)
                for j in range(G):
                    i = g * G + j
                    link(nc.vector.tensor_scalar(kst[:, i, :], ring[:, j, :], mv[:, i, 0:1], rstd[:, bass.ds(i, 1)], ALU.subtract, ALU.mult))
                    mark(nc.vector.scalar_tensor_tensor(out=xh[:, j, :], in0=kst[:, i, :], scalar=1.0, in1=vecs[:, 2, :],
                                                        op0=ALU.mult, op1=ALU.mult, accum_out=wcol[:, bass.ds(i, 1)]))
                    n = mark(nc.vector.tensor_tensor(qe[:, i, :], kst[:, i, :], ring[:, j, :], ALU.add))
                need(n)
                v.sem_inc(x1_ok, 1)
            leave(NG, per_group)
            link(nc.vector.tensor_scalar(wcol[:, :], wcol[:, :], br_b[:, 0:1], None, ALU.add))
            v.sem_inc(w_ok, 1)
            v.wait_ge(w_t, 1)
            link(nc.vector.tensor_copy(wrow[:, :], psX[0:NT, 0:P]))
            v.sem_inc(w_row, 1)

            v.wait_ge(w_b, 16)
            link(nc.vector.memset(cnt[:, :, :], 0.0))
            for n in range(NT):
                w = wcol[:, n:n + 1]
                if n:
                    link(nc.vector.tensor_scalar(junk[:, 0:n * P], QWB[:, 0:n * P], w, 0.0, ALU.is_ge, ALU.add, accum_out=cnt[:, 0, n:n + 1]))
                link(nc.vector.tensor_scalar(junk[:, n * P:N], QWB[:, n * P:N], w, 0.0, ALU.is_gt, ALU.add, accum_out=cnt[:, 1, n:n + 1]))
                link(nc.vector.scalar_tensor_tensor(out=junk[:, n * P:(n + 1) * P], in0=QWB[:, n * P:(n + 1) * P], scalar=w, in1=lower[:, :],
                                                    op0=ALU.is_equal, op1=ALU.mult, accum_out=cnt[:, 2, n:n + 1]))
            link(nc.vector.tensor_tensor(cnt[:, 0, :], cnt[:, 0, :], cnt[:, 1, :], ALU.add))
            link(nc.vector.tensor_tensor(cnt[:, 0, :], cnt[:, 0, :], cnt[:, 2, :], ALU.add))
            link(nc.vector.scalar_tensor_tensor(out=wcol[:, :], in0=cnt[:, 0, :], scalar=float(KEPT) - 0.5, in1=wcol[:, :],
                                                op0=ALU.is_lt, op1=ALU.mult))
            with v.Fori(0, NG) as g:
                for j in range(G):
                    i = g * G + j
                    v.wait_ge(f_y, i + 3)
                    ins = nc.vector.scalar_tensor_tensor(out=vst[:, i, 0:HID], in0=vst[:, i, 0:HID], scalar=wcol[:, bass.ds(i, 1)],
                                                         in1=qe[:, i, :], op0=ALU.mult, op1=ALU.add)
                ins.then_inc(o_ok, 1)

        @block.scalar
        def _(act):
            order = Order(act, act_order)

            def turned(w, j, gain, shift):
                act.wait_ge(pt_done, w + 1 + G)
                if gain is None:
                    nc.scalar.activation(hT[:, j, :, :], psT(j), ACT.Copy).then_inc(hT_ready, 1)
                else:
                    nc.scalar.activation(hT[:, j, 0, :], psT(j)[:, 0, :], ACT.Identity, scale=gain[0], bias=shift[0])
                    nc.scalar.activation(hT[:, j, 1, :], psT(j)[:, 1, :], ACT.Identity, scale=gain[1], bias=shift[1]).then_inc(hT_ready, 1)

            with act.Fori(0, NG) as g:
                for j in range(G):
                    i = g * G + j
                    act.wait_ge(xh_ready, i + 1)
                    nc.scalar.activation(xm[:, i, :], xh[:, j, :], ACT.Copy).then_inc(xh_copied, 1)
                    turned(i, j, None, None)
            def edge_weights(turn, k):
                act.wait_ge(e_logit, 2 * turn + k + 1)
                nc.scalar.activation(E7[:, k, :], E7[:, k, :], ACT.Exp, scale=GNN_SCALE).then_inc(e_exp, 1)

            act.wait_ge(s_const, 16 * CONSTS)
            act.wait_ge(mix_start, 1)
            with act.Fori(0, LAYERS) as L:
                act.wait_ge(hg_ok, L * (2 * NT) + 1)
                settle(act)
                order.base, order.n = L * 3, 0
                order.mark(nc.scalar.activation(cur[:, 0:2, :], ln1[:, :, bass.ds(L, 1), :].rearrange("k s l c -> k s (l c)"), ACT.Copy))
                order.mark(nc.scalar.activation(cur[:, 2:4, :], ln2[:, :, bass.ds(L, 1), :].rearrange("k s l c -> k s (l c)"), ACT.Copy))
                order.link(nc.scalar.activation(cur_b1[:, :], b1_mix[:, bass.ds(L, 1), :].rearrange("k l c -> k (l c)"), ACT.Copy))
                settle(act)
                gain1, shift1, gain2, shift2 = ([cur[:, s, c:c + 1] for c in range(C)] for s in range(4))
                with act.Fori(0, NG) as g:
                    turned(w_a(L, g * G), 0, gain1, shift1)
                    for j in range(G):
                        i = g * G + j
                        if j + 1 < G:
                            turned(w_a(L, i + 1), j + 1, gain1, shift1)
                        act.wait_ge(qk_done, L * NT + i + 1)
                        nc.scalar.activation(kst[:, i, :], psKV(j)[:, 0:HID], ACT.Copy)
                        nc.scalar.activation(vmix[:, i, :, 0:128], psKV(j)[:, HID:2 * HID].rearrange("p (c f) -> p c f", c=C), ACT.Copy).then_inc(qk_act, 1)
                        act.wait_ge(qsub, L * NT + i + 3)
                        nc.scalar.activation(qe[:, i, :], qe[:, i, :], ACT.Exp, scale=MIX_SCALE).then_inc(qexp, 1)
                        if j in (0, 2):
                            edge_weights(L * (2 * NG) + g, j // 2)
                with act.Fori(0, NG) as g:
                    for j in range(G):
                        act.wait_ge(kd, L * NT + g * G + j + 1)
                        nc.scalar.activation(ek[:, j, :], ek[:, j, :], ACT.Exp, scale=MIX_SCALE).then_inc(ek_ok, 1)
                with act.Fori(0, NG) as g:
                    for j in range(G):
                        turned(w_c1(L, g * G + j), j, None, None)
                with act.Fori(0, NG) as g:
                    turned(w_c2(L, g * G), 0, gain2, shift2)
                    for j in range(G):
                        i = g * G + j
                        for half in range(2):
                            act.wait_ge(h_done, L * (2 * NT) + i * 2 + half + 1)
                            for k in range(4):
                                ins = nc.scalar.activation(hg[:, j % 2, 4 * half + k, :], psH(j, half)[:, k, :], ACT.Gelu,
                                                           bias=cur_b1[:, 4 * half + k:4 * half + k + 1])
                            ins.then_inc(hg_ok, 1)
                        if j in (0, 2):
                            edge_weights(L * (2 * NG) + NG + g, j // 2)
                        if j + 1 < G:
                            turned(w_c2(L, i + 1), j + 1, gain2, shift2)
            act.wait_ge(b_d, 1)
            nc.scalar.activation(fac[:, :, :], fac[:, :, :], ACT.Exp, scale=GNN_SCALE).then_inc(b_e, 1)
            with act.Fori(0, NG) as g:
                for j in range(G):
                    act.wait_ge(f_pre, g * G + j + 1)
                    nc.scalar.activation(ring[:, j, :], ring[:, j, :], ACT.Gelu).then_inc(f_gelu, 1)
            act.wait_ge(x1_ok, NG)
            with act.Fori(0, NG) as g:
                def copied(i, j):
                    act.wait_ge(pt_done, w_f(i) + 1)
                    nc.scalar.activation(xh[:, j, :], kst[:, i, :], ACT.Copy).then_inc(xh_ready, 1)

                copied(g * G, 0)
                turned(w_f(g * G), 0, None, None)
                for j in range(G):
                    i = g * G + j
                    if j + 1 < G:
                        copied(i + 1, j + 1)
                    for half in range(2):
                        act.wait_ge(h_done, i * 2 + half + 1 + LAYERS * 2 * NT)
                        for k in range(4):
                            ins = nc.scalar.activation(hg[:, j % 2, 4 * half + k, :], psH(j, half)[:, k, :], ACT.Gelu_apprx_tanh,
                                                       bias=b1_ffn[:, 4 * half + k:4 * half + k + 1])
                        ins.then_inc(hg_ok, 1)
                    if j + 1 < G:
                        turned(w_f(i + 1), j + 1, None, None)
                    act.wait_ge(y_done, i + 1 + LAYERS * NT)
                    nc.scalar.activation(vst[:, i, 0:HID], psY(j), ACT.Copy).then_inc(f_y, 1)

        @block.tensor
        def _(pe):
            mm = nc.tensor.matmul

            def room(sem, n, j):
                pe.wait_ge(sem, n + 1 + (j == 0))

            def turn(w, j):
                pe.wait_ge(xh_ready, w + 1)
                room(hT_ready, w, j)
                for c in range(C):
                    ins = nc.tensor.transpose(psT(j)[:, c, :], xh[:, j, c * 128:(c + 1) * 128], ident[0:P, 0:P])
                ins.then_inc(pt_done, 1)

            def ffn_up(base, i, j):
                for half in range(2):
                    for k in range(4):
                        for c in range(C):
                            ins = mm(psH(j, half)[:, k, :], w_big[:, c, (4 * half + k) * 128:(4 * half + k + 1) * 128], hT[:, j, c, :],
                                     start=(c == 0), stop=(c == C - 1))
                    ins.then_inc(h_done, 1)

            def ffn_down(free, y0, h0, i, j, bias):
                room(free, y0 + i, j)
                if bias:
                    mm(psY(j), ones[0:1, 0:P], b2_row[0:1, :], start=True, stop=False)
                for half in range(2):
                    pe.wait_ge(hg_ok, h0 + i * 2 + half + 2)
                    for k in range(4 * half, 4 * half + 4):
                        ins = mm(psY(j), hg[:, j % 2, k, :], w_down[:, k, :], start=(k == 0 and not bias), stop=(k == KC - 1))
                ins.then_inc(y_done, 1)

            pe.wait_ge(gn, 7)
            pe.wait_ge(s_wg, 8 * 16)
            with pe.Fori(0, NG) as g:
                turn(g * G, 0)
                for j in range(G):
                    i = g * G + j
                    if j + 1 < G:
                        turn(i + 1, j + 1)
                    pe.wait_ge(hT_ready, i + 3)
                    room(gp_free, i, j)
                    for half, ps in enumerate((psQK(j), psVS(j))):
                        for c in range(C):
                            ins = mm(ps, hT[:, j, c, :], w_big[:, c, half * 512:(half + 1) * 512], start=(c == 0), stop=(c == C - 1))
                    ins.then_inc(gp_done, 1)
            with pe.Fori(0, LAYERS) as L:
                pe.wait_ge(s_wqkv, L * 48 + 48)
                settle(pe)
                with pe.Fori(0, NG) as g:
                    turn(w_a(L, g * G), 0)
                    for j in range(G):
                        i = g * G + j
                        if j + 1 < G:
                            turn(w_a(L, i + 1), j + 1)
                        pe.wait_ge(hT_ready, w_a(L, i) + 3)
                        room(qsub, L * NT + i, j)
                        for c in range(C):
                            mm(psQ(j), hT[:, j, c, :], w_qkv[:, c, 0:HID], start=(c == 0), stop=(c == C - 1))
                        room(qk_act, L * NT + i, j)
                        for c in range(C):
                            ins = mm(psKV(j), hT[:, j, c, :], w_qkv[:, c, HID:3 * HID], start=(c == 0), stop=(c == C - 1))
                        ins.then_inc(qk_done, 1)
                pe.wait_ge(km_col, L + 1)
                for c in range(C):
                    ins = nc.tensor.transpose(psX[:, c * P:(c + 1) * P], kmx[:, c * 128:(c + 1) * 128], ident[0:P, 0:P])
                ins.then_inc(km_t, 1)
                pe.wait_ge(km_dg, L + 1)
                mm(psX[0:P, 256:512], ones[:, 0:P], dg[:, :, :].rearrange("p c n -> p (c n)"), start=True, stop=True).then_inc(km_b, 1)
                for c in range(C):
                    mm(psC(c), zeros[:, 0:128], zeros[:, :], start=True, stop=False)
                with pe.Fori(0, NG) as g:
                    for j in range(G):
                        i = g * G + j
                        pe.wait_ge(ek_ok, L * NT + i + 1)
                        for c in range(C):
                            ins = mm(psC(c), ek[:, j, c * 128:(c + 1) * 128], vmix[:, i, c, 0:129], start=False, stop=False)
                        ins.then_inc(ek_used, 1)
                for c in range(C):
                    ins = mm(psC(c), zeros[:, 0:128], zeros[:, :], start=False, stop=True)
                ins.then_inc(ctx_done, 1)
                pe.wait_ge(bd_ok, L + 1)
                for c in range(C):
                    ins = nc.tensor.transpose(psX[:, c * 128:(c + 1) * 128], BD[:, c, :], ident[:, :])
                ins.then_inc(bdt, 1)
                pe.wait_ge(bdt_ok, L + 1)
                pe.wait_ge(s_wo, L * 32 + 32)
                for c in range(C):
                    ins = mm(psM[:, c * HID:(c + 1) * HID], BDT[:, c, :], w_o[:, c, :], start=True, stop=True)
                ins.then_inc(m_done, 1)
                pe.wait_ge(m_ok, L + 2)
                settle(pe)
                with pe.Fori(0, NG) as g:
                    turn(w_c1(L, g * G), 0)
                    for j in range(G):
                        i = g * G + j
                        if j + 1 < G:
                            turn(w_c1(L, i + 1), j + 1)
                        pe.wait_ge(hT_ready, w_c1(L, i) + 3)
                        room(at_free, L * NT + i, j)
                        for c in range(C):
                            ins = mm(psY(j), hT[:, j, c, :], m_sb[:, c, :], start=(c == 0), stop=(c == C - 1))
                        ins.then_inc(at_done, 1)
                pe.wait_ge(s_w1, L * 16 + 16)
                pe.wait_ge(s_w2, L * 32 + 32)
                settle(pe)
                with pe.Fori(0, NG) as g:
                    turn(w_c2(L, g * G), 0)
                    for j in range(G):
                        i = g * G + j
                        pe.wait_ge(hT_ready, w_c2(L, i) + 3)
                        ffn_up(None, i, j)
                        if j + 1 < G:
                            turn(w_c2(L, i + 1), j + 1)
                        ffn_down(y_free, L * NT, L * (2 * NT), i, j, False)
            pe.wait_ge(b_k, 1)
            for i in range(4):
                ins = nc.tensor.transpose(psX[0:HEADS, i * 128:i * 128 + P], keys[:, i, :], ident[0:P, 0:P])
            ins.then_inc(b_t, 1)
            pe.wait_ge(b_m, 1)
            for s in range(2):
                ins = nc.tensor.transpose(bank[6][0:P, s * HEADS:(s + 1) * HEADS], F2[:, s * P:(s + 1) * P], ident[0:HEADS, 0:HEADS])
            ins.then_inc(b_f, 1)
            pe.wait_ge(hd_used, 1)
            with pe.Fori(0, NG) as g:
                for j in range(G):
                    i = g * G + j
                    pe.wait_ge(oh_ok, i + 1)
                    room(oh_free, i, j)
                    mm(psB(j), onehots[:, j, 0, :], hd[:, 0:AW], start=True, stop=False)
                    mm(psB(j), onehots[:, j, 1, :], S[:, 1, T - 1, 0:AW], start=False, stop=True).then_inc(oh_ps, 1)
            pe.wait_ge(w_ok, 1)
            nc.tensor.transpose(psX[0:NT, 0:P], wcol[:, :], ident[0:P, 0:P]).then_inc(w_t, 1)
            pe.wait_ge(w_row, 1)
            pe.wait_ge(s_const, 16 * CONSTS)
            pe.wait_ge(s_w1, LAYERS * 16 + 16)
            pe.wait_ge(s_w2, LAYERS * 32 + 16)
            with pe.Fori(0, NG) as g:
                turn(w_f(g * G), 0)
                for j in range(G):
                    i = g * G + j
                    pe.wait_ge(hT_ready, w_f(i) + 3)
                    ffn_up(None, i, j)
                    if j + 1 < G:
                        turn(w_f(i + 1), j + 1)
                    ffn_down(f_y, 0, LAYERS * 2 * NT, i, j, True)


INS = ["x", "src", "dst", "L0_gnn_Wq", "L0_gnn_bq", "L0_gnn_Wk", "L0_gnn_bk", "L0_gnn_Wv", "L0_gnn_bv", "L0_gnn_Wskip", "L0_gnn_bskip",
       "L0_gnn_gamma", "L0_gnn_beta", "L0_mix_Wq", "L0_mix_Wk", "L0_mix_Wv", "L0_mix_Wo", "L0_mix_bo", "L0_mix_ln1_g", "L0_mix_ln1_b",
       "L0_mix_W1", "L0_mix_b1", "L0_mix_W2", "L0_mix_b2", "L0_mix_ln2_g", "L0_mix_ln2_b", "L0_ffn_wr", "L0_ffn_br", "L0_ffn_w1",
       "L0_ffn_b1", "L0_ffn_w2", "L0_ffn_b2"]


def kernel(**inputs):
    import numpy as np
    import concourse.bacc as bacc
    from concourse.bass_utils import run_bass_kernel_spmd

    nc = bacc.Bacc("TRN2", target_bir_lowering=False, num_devices=1)
    arrays, aps = {}, {}
    for name in INS:
        a = np.ascontiguousarray(inputs[name])
        arrays["in_" + name] = a
        aps[name] = nc.dram_tensor("in_" + name, a.shape, mybir.dt.from_np(a.dtype), kind="ExternalInput").ap()
    out = nc.dram_tensor("out", [N, HID], F32, kind="ExternalOutput").ap()
    gps_kernel(nc, aps, out)
    r = run_bass_kernel_spmd(nc, [arrays], core_ids=[0])
    return r.results[0]["out"]
```

```python
import concourse.bass as bass
from concourse import mybir
from contextlib import ExitStack

F32 = mybir.dt.float32
I32 = mybir.dt.int32
ALU = mybir.AluOpType
ACT = mybir.ActivationFunctionType
AX = mybir.AxisListType

N, E, HID, HEADS, LAYERS, FF = 3125, 50000, 256, 8, 4, 1024
DH = HID // HEADS
P = 125
NT = N // P
G = 5
NG = NT // G
C = HID // 128
KC = FF // 128
EPP = E // P
T = 5
NB = EPP // T
VW = DH + 1
AW = HEADS * VW
TW = AW + HEADS
W7 = T + 2
KVW = HID + AW
NO_RUN = E
BIG = 1e30
EPS = 1e-5
GNN_SCALE = float(DH) ** -0.5
MIX_SCALE = float(DH) ** -0.25
CONSTS = 4 + 4
KEPT = max(1, int(0.5 * N)) - 1
RSQRT_SEED = float(0x5F3759DF)


class Order:

    def __init__(self, engine, sem):
        self.engine, self.sem, self.base, self.n = engine, sem, 0, 0

    def mark(self, instruction):
        self.n += 1
        instruction.then_inc(self.sem, 1)
        return self.n

    def need(self, n):
        self.engine.wait_ge(self.sem, self.base + n)

    def link(self, instruction):
        self.need(self.mark(instruction))


def gps_kernel(nc, A, out):
    ctx = ExitStack()
    with ctx:
        def sb(name, shape, dt=F32):
            return ctx.enter_context(nc.sbuf_tensor(name, shape, dt))

        def sem(name):
            return ctx.enter_context(nc.semaphore(name))

        def dram(name, shape):
            return nc.dram_tensor(name, shape, F32, kind="Internal").ap()

        kv_tab = dram("kv_tab", [N, KVW])
        q_tab = dram("q_tab", [N, HID])
        log = dram("log", [E + 2, TW])
        dst_tab = dram("dst_tab", [P, EPP])
        skip_d = dram("skip_d", [N, HID])
        xn_d = dram("xn_d", [N, HID])
        w_d = dram("w_d", [NT, P])

        xm = sb("xm", [P, NT, HID])
        qe = sb("qe", [P, NT, HID])
        kst = sb("kst", [P, NT, HID])
        vst = sb("vst", [P, NT, AW])
        vmix = vst[:, :, :].rearrange("p n (c f) -> p n c f", c=C)
        vgnn = vst[:, :, :].rearrange("p n (h f) -> p n h f", h=HEADS)
        KV = sb("KV", [P, 2, T, KVW])
        QWB = sb("QWB", [P, N])
        ring = QWB[:, 0:G * HID].rearrange("p (j f) -> p j f", j=G)
        Q = QWB[:, 0:2 * T * HID].rearrange("p (k t f) -> p k t f", k=2, t=T)
        S = sb("S", [P, 2, T, TW])
        L7 = sb("L7", [P, 2, HEADS * W7])
        F7 = sb("F7", [P, HEADS * W7])
        M7 = sb("M7", [P, 2, HEADS * W7])
        E7 = sb("E7", [P, 2, HEADS * W7])
        P7 = sb("P7", [P, HEADS * W7 + 1])
        src_i = sb("src_i", [P, EPP], I32)
        dst_i = sb("dst_i", [P, EPP], I32)
        part_ring = sb("part_ring", [P, G], I32)
        part_i = sb("part_i", [P, NT], I32)
        end_i = sb("end_i", [P, NT + 1], I32)
        node = sb("node", [P, NT])
        part_f = sb("part_f", [P, NT])
        firsts = sb("firsts", [P, NT])
        upto = sb("upto", [P, NT])
        own = sb("own", [P, NT])
        end_f = sb("end_f", [P, NT + 1])
        run1 = sb("run1", [P, 1])
        same = sb("same", [P, EPP])
        sm = sb("sm", [P, 2, T])
        idx = sb("idx", [P, 2, 2, T], I32)
        xh = sb("xh", [P, G, HID])
        dst_x = xh[:, :, :].rearrange("p j f -> p (j f)")[:, 0:EPP + 1]
        dst_f = dst_x[:, 1:EPP + 1]
        ends = sb("ends", [P, 2])
        hT = sb("hT", [128, 3, C, P])
        ek = xh
        hg = sb("hg", [128, 2, KC, P])
        w_big = sb("w_big", [128, C, FF])
        w_down = sb("w_down", [128, KC, HID])
        w_qkv = sb("w_qkv", [128, C, 3 * HID])
        w_o = sb("w_o", [128, C, HID])
        m_sb = sb("m_sb", [128, C, HID])
        ln1 = sb("ln1", [128, 2, LAYERS, C])
        ln2 = sb("ln2", [128, 2, LAYERS, C])
        b1_mix = sb("b1_mix", [128, LAYERS, KC])
        cur = sb("cur", [128, 4, C])
        cur_b1 = sb("cur_b1", [128, KC])
        b1_ffn = sb("b1_ffn", [128, KC])
        b2_b = sb("b2_b", [P, HID])
        bo_b = sb("bo_b", [DH, HID])
        b2_row = sb("b2_row", [1, HID])
        br_b = sb("br_b", [P, 1])
        vecs = w_qkv[0:P, 0, :].rearrange("p (i f) -> p i f", i=3)
        gnn_b = hg[0:P, :, :, :].rearrange("p a k n -> p (a k n)")[:, 0:4 * HID]
        onehots = hg[0:P, :, :, :].rearrange("p a k n -> p (a k n)")[:, 0:10 * P].rearrange("p (j s n) -> p j s n", j=G, s=2)
        ident = sb("ident", [128, 128])
        ones = sb("ones", [128, 128])
        zeros = sb("zeros", [128, 129])
        iota_tile = sb("iota_tile", [P, NT])
        part_base = sb("part_base", [P, 1])
        bst = sb("bst", [P, G, 6])
        mv = sb("mv", [P, NT, 2])
        mvs = sb("mvs", [P, G, 2])
        rstd = sb("rstd", [P, NT])
        nmr = sb("nmr", [P, NT])
        nr_v = sb("nr_v", [P, NT])
        nr_i = sb("nr_i", [P, NT], I32)
        nr_t = sb("nr_t", [P, NT])
        kmx = sb("kmx", [P, HID])
        kmx_b = sb("kmx_b", [P, HID])
        iota_row, lower = kmx[:, 0:P], kmx[:, P:2 * P]
        km = sb("km", [128, C])
        s40 = sb("s40", [P, G * HEADS])
        mx8 = s40[:, :].rearrange("p (j h) -> p j h", j=G)
        qsum = sb("qsum", [P, NT * HEADS])
        rS = sb("rS", [128, C])
        BD = sb("BD", [128, C, 128])
        BDT = sb("BDT", [128, C, 128])
        dg = BDT
        hd = sb("hd", [P, TW])
        carried = hd[:, 0:AW]
        keys = sb("keys", [P, 4, HEADS])
        K2, V2 = w_o[0:HEADS, 0, 0:2 * P], w_o[0:HEADS, 1, 0:2 * P]
        F2, M2 = m_sb[0:HEADS, 0, 0:2 * P], m_sb[0:HEADS, 1, 0:2 * P]
        pen2 = BDT[0:HEADS, :, :].rearrange("h c n -> h (c n)")[:, 0:2 * P + 1]
        fac = sb("fac", [P, 2, HEADS])
        key_tile = sb("key_tile", [P, 2, NT])
        wcol = s40[:, 0:NT]
        wrow = kmx_b[0:NT, 0:P]
        cnt = BDT[0:P, :, :].rearrange("p c n -> p (c n)")[:, 0:3 * NT].rearrange("p (s n) -> p s n", s=3)
        kv_flat = KV[:, :, :, :].rearrange("p a t f -> p (a t f)")
        first_row = QWB[:, G * HID:G * HID + P]
        compared = kv_flat[:, 0:N].rearrange("p (n q) -> p n q", n=NT)
        dst_rows = kv_flat[:, 0:G * EPP].rearrange("p (j t) -> p j t", j=G)
        dst_junk = kv_flat[:, G * EPP:(G + 1) * EPP]
        fl = kv_flat[:, 0:G * TW].rearrange("p (j f) -> p j f", j=G)
        agg = QWB[:, 0:G * AW]
        mean = QWB[:, G * AW:G * AW + G * HID]
        dots = mean.rearrange("p (j f) -> p j f", j=G)
        junk = KV[:, :, :, :].rearrange("p a t f -> p (a t f)")[:, 0:N]

        bank = [ctx.enter_context(nc.psum_tensor(f"bank{i}", [128, 512], F32)) for i in range(8)]

        def psT(j):
            return bank[j % 2][:, 0:C * P].rearrange("p (c n) -> p c n", c=C)

        def psQ(j):
            return bank[2 + j % 2][0:P, 0:HID]

        def psKV(j):
            return bank[4 + j % 2][0:P, :]

        def psQK(j):
            return bank[2 + j % 2][0:P, :]

        def psVS(j):
            return bank[4 + j % 2][0:P, :]

        def psY(j):
            return bank[6 + j % 2][0:P, 0:HID]

        def psH(j, half):
            return bank[2 + 2 * (j % 2) + half][:, 0:4 * P].rearrange("p (k n) -> p k n", k=4)

        def psC(c):
            return bank[2 + c][:, 0:129]

        def psB(j):
            return bank[2 + j % 2][0:P, 0:AW]

        psX, psM = bank[7], bank[4]

        s_x, s_dst, s_idx, s_wg, s_const = [sem(f"x_loaded{g}") for g in range(NG)], sem("destinations_loaded"), sem("sources_loaded"), sem("gnn_weights_loaded"), sem("constants_loaded")
        s_wqkv, s_wo, s_w1, s_w2 = sem("wqkv_loaded"), sem("wo_loaded"), sem("w1_loaded"), sem("w2_loaded")
        s_vec = sem("last_vectors_loaded")
        gn = sem("made_constants")
        waited = sem("waited")
        xh_ready, pt_done, hT_ready = sem("xh_ready"), sem("transposed_plus_5"), sem("hT_ready_plus_2")
        xh_copied = sem("xh_copied_plus_5")
        gp_done, gp_free, gp_stored = sem("gnn_products_done"), sem("gnn_products_read_plus_2"), sem("gnn_rows_stored_plus_1")
        mix_start = sem("value_ones_set")
        d_f, d_st, d_b, d_row = sem("destinations_ready"), sem("destinations_stored"), sem("firsts_spread"), sem("node_partitions_ready")
        d_in, d_used, d_ok = [sem(f"destinations_gathered{j}") for j in range(G)], sem("destinations_used_plus_1"), sem("run_ends_ready")
        e_prep, e_gath, e_logits_used, e_used, e_logit, e_exp, e_state, e_scat, e_idx = (
            sem("edge_tables_ready"), [sem(f"gathered{k}") for k in range(2)],
            sem("queries_used_plus_2"), sem("keys_and_values_used_plus_2"),
            sem("logits_ready"), sem("weights_ready"), sem("sums_ready"), [sem(f"scattered{k}_plus_16") for k in range(2)],
            sem("indices_copied"))
        qk_done, qk_act, qsub, qexp = (sem("qkv_done"), sem("qkv_read_by_act_plus_2"),
                                       sem("q_shifted_plus_2"), sem("q_exponentiated"))
        km_col, km_t, km_dg, km_b, km_ok = sem("kmax_columns"), sem("kmax_transposed"), sem("kmax_diagonal"), sem("kmax_spread"), sem("kmax_read")
        kd, ek_ok, ek_used = sem("k_shifted"), sem("k_exponentiated"), sem("ek_used_plus_5")
        ctx_done, bd_ok, bdt, bdt_ok, m_done, m_ok = (sem("context_done_plus_1"), sem("context_scaled"), sem("context_transposed"),
                                                      sem("contextT_read"), sem("M_done"), sem("M_read_plus_1"))
        at_done, at_free = sem("attention_done"), sem("attention_read_plus_2")
        q_ok = sem("query_sums_ready")
        ln_ok, b2_ok = sem("layer_norm_ready"), sem("b2_added")
        h_done, hg_ok, y_done, y_free = sem("hidden_done"), sem("gelu_done_plus_1"), sem("ffn_done"), sem("ffn_read_plus_2")
        hd_in, hd_used = sem("first_runs_loaded"), sem("boundary_ready")
        b_t, b_k, b_m, b_f, b_d, b_e = sem("keys_transposed"), sem("keys_ready"), sem("maxima_found"), sem("maxima_transposed"), sem("factor_logits_ready"), sem("factors_ready")
        x_in, xn_in, skip_in = sem("x_reloaded"), sem("normalised_x_reloaded"), sem("skips_reloaded")
        f_run = [sem(f"runs_gathered{j}") for j in range(G)]
        f_used, oh_ok, oh_ps = sem("runs_summed_plus_5"), sem("onehots_ready"), sem("boundary_sums_plus_1")
        f_pre, f_gelu, f_xmx, x1_ok = sem("gnn_out_ready_plus_1"), sem("gnn_gelu_done"), sem("residuals_added"), sem("x1_normalised")
        y_norm, y_normed, x1_norm = sem("gnn_layer_norm_ready"), sem("gnn_rows_normalised"), sem("x1_layer_norm_ready")
        xx_ok = sem("x1_used")
        w_ok, w_t, w_row, w_st, w_b = sem("w_ready"), sem("w_transposed"), sem("w_row_ready"), sem("w_stored"), sem("w_spread")
        f_y, o_ok, o_st = sem("ffn_rows_ready"), sem("out_ready"), sem("out_stored")
        dve_order, act_order, pool_order = sem("dve_order"), sem("act_order"), sem("pool_order")

        x_v = A["x"].rearrange("(n p) f -> p n f", p=P)
        out_v = out.rearrange("(n p) f -> p n f", p=P)
        kv_v = kv_tab.rearrange("(n p) f -> p n f", p=P)
        q_v = q_tab.rearrange("(n p) f -> p n f", p=P)
        skip_v = skip_d.rearrange("(n p) f -> p n f", p=P)
        xn_v = xn_d.rearrange("(n p) f -> p n f", p=P)
        log_v = log[0:E, :].rearrange("(p t) f -> p t f", p=P)

        def row(v):
            return v.rearrange("(a n) -> a n", a=1)

        PER_LAYER = 3 * NT

        def w_a(L, i):
            return L * PER_LAYER + i + NT

        def w_c1(L, i):
            return L * PER_LAYER + i + 2 * NT

        def w_c2(L, i):
            return L * PER_LAYER + i + 3 * NT

        def w_f(i):
            return i + NT + LAYERS * PER_LAYER

        def settle(engine):
            engine.sem_inc(waited, 1)

        def groups(engine, body):
            with engine.Fori(0, NG - 1) as g:
                body(g, False)
            body(NG - 1, True)

        block = ctx.enter_context(nc.Block())

        @block.sync
        def _(sp):
            sp.dma_start(dst_i[:, :], A["dst"].rearrange("(p t) -> p t", p=P)).then_inc(s_dst, 16)
            for g in range(NG):
                sp.dma_start(xm[:, g * G:(g + 1) * G, :], x_v[:, g * G:(g + 1) * G, :]).then_inc(s_x[g], 16)
            for i, w in enumerate(("L0_gnn_Wq", "L0_gnn_Wk", "L0_gnn_Wv", "L0_gnn_Wskip")):
                sp.dma_start(w_big[:, :, i * HID:(i + 1) * HID], A[w].rearrange("(c k) n -> k c n", k=128)).then_inc(s_wg, 16)
            for i, b in enumerate(("L0_gnn_bq", "L0_gnn_bk", "L0_gnn_bv", "L0_gnn_bskip")):
                sp.dma_start(gnn_b[:, i * HID:(i + 1) * HID], row(A[b]).to_broadcast([P, HID])).then_inc(s_wg, 16)
            sp.dma_start(src_i[:, :], A["src"].rearrange("(p t) -> p t", p=P)).then_inc(s_idx, 16)
            sp.wait_ge(d_f, 1)
            sp.dma_start(dst_tab, dst_f[:, :]).then_inc(d_st, 16)
            for t, (g_, b_) in ((ln1, ("L0_mix_ln1_g", "L0_mix_ln1_b")), (ln2, ("L0_mix_ln2_g", "L0_mix_ln2_b"))):
                for i, v in enumerate((g_, b_)):
                    sp.dma_start(t[:, i, :, :], A[v].rearrange("l (c k) -> k l c", k=128), allow_slow_non_contiguous=True).then_inc(s_const, 16)
            sp.dma_start(b1_mix[:, :, :], A["L0_mix_b1"].rearrange("l (c k) -> k l c", k=128), allow_slow_non_contiguous=True).then_inc(s_const, 16)
            sp.dma_start(b1_ffn[:, :], A["L0_ffn_b1"].rearrange("(c k) -> k c", k=128), allow_slow_non_contiguous=True).then_inc(s_const, 16)
            sp.dma_start(b2_row[:, :], row(A["L0_ffn_b2"])).then_inc(s_const, 16)
            sp.dma_start(br_b[:, :], row(A["L0_ffn_br"]).to_broadcast([P, 1])).then_inc(s_const, 16)
            with sp.Fori(0, NG) as g:
                sp.wait_ge(gp_free, g * G + G + 2)
                settle(sp)
                sp.wait_ge(xh_copied, g * G + G + G)
                settle(sp)
                sp.dma_start(q_v[:, bass.ds(g * G, G), :], qe[:, bass.ds(g * G, G), :]).then_inc(gp_stored, 16)
                sp.dma_start(kv_v[:, bass.ds(g * G, G), 0:HID], kst[:, bass.ds(g * G, G), :]).then_inc(gp_stored, 16)
                sp.dma_start(kv_v[:, bass.ds(g * G, G), HID:KVW], vst[:, bass.ds(g * G, G), :]).then_inc(gp_stored, 16)
                sp.dma_start(xn_v[:, bass.ds(g * G, G), :], xm[:, bass.ds(g * G, G), :]).then_inc(gp_stored, 16)
                sp.dma_start(skip_v[:, bass.ds(g * G, G), :], ring[:, :, :]).then_inc(gp_stored, 16)
            with sp.Fori(0, LAYERS) as L:
                sp.wait_ge(ctx_done, L + 1)
                for i, w in enumerate(("L0_mix_Wq", "L0_mix_Wk", "L0_mix_Wv")):
                    sp.dma_start(w_qkv[:, :, i * HID:(i + 1) * HID], A[w][bass.ds(L, 1), :, :].rearrange("l (c k) n -> k (l c) n", k=128)).then_inc(s_wqkv, 16)
                sp.wait_ge(m_ok, L + 1)
                sp.dma_start(w_o[:, :, :], A["L0_mix_Wo"][bass.ds(L, 1), :, :].rearrange("l (c k) n -> k (l c) n", k=128)).then_inc(s_wo, 16)
                sp.dma_start(bo_b[:, :], A["L0_mix_bo"][bass.ds(L, 1), :].to_broadcast([DH, HID])).then_inc(s_wo, 16)
                sp.wait_ge(gp_done, NT)
                sp.wait_ge(y_free, L * NT + 2)
                sp.dma_start(w_big[:, :, :], A["L0_mix_W1"][bass.ds(L, 1), :, :].rearrange("l (c k) n -> k (l c) n", k=128)).then_inc(s_w1, 16)
                sp.dma_start(w_down[:, :, :], A["L0_mix_W2"][bass.ds(L, 1), :, :].rearrange("l (c k) n -> k (l c) n", k=128)).then_inc(s_w2, 16)
                sp.dma_start(b2_b[:, :], A["L0_mix_b2"][bass.ds(L, 1), :].to_broadcast([P, HID])).then_inc(s_w2, 16)
            sp.wait_ge(ctx_done, LAYERS + 1)
            for i, v in enumerate(("L0_gnn_gamma", "L0_gnn_beta")):
                sp.dma_start(vecs[:, i, :], row(A[v]).to_broadcast([P, HID])).then_inc(s_vec, 16)
            sp.dma_start(vecs[:, 2, :], A["L0_ffn_wr"].rearrange("n a -> a n").to_broadcast([P, HID])).then_inc(s_vec, 16)
            sp.dma_start(kst[:, :, :], xn_v).then_inc(xn_in, 16)
            sp.dma_start(vst[:, :, 0:HID], skip_v).then_inc(skip_in, 16)
            sp.wait_ge(at_free, LAYERS * NT + 2)
            sp.dma_start(qe[:, :, :], x_v).then_inc(x_in, 16)
            sp.wait_ge(y_free, LAYERS * NT + 2)
            sp.dma_start(w_big[:, :, :], A["L0_ffn_w1"].rearrange("(c k) n -> k c n", k=128)).then_inc(s_w1, 16)
            sp.dma_start(w_down[:, :, :], A["L0_ffn_w2"].rearrange("(c k) n -> k c n", k=128)).then_inc(s_w2, 16)
            sp.wait_ge(w_row, 1)
            sp.dma_start(w_d, wrow[:, :]).then_inc(w_st, 16)
            sp.wait_ge(w_st, 16)
            sp.dma_start(QWB[:, :], w_d.rearrange("n p -> (n p)").rearrange("(a f) -> a f", a=1).to_broadcast([P, N])).then_inc(w_b, 16)
            with sp.Fori(0, NG) as g:
                sp.wait_ge(o_ok, g + 1)
                sp.dma_start(out_v[:, bass.ds(g * G, G), :], vst[:, bass.ds(g * G, G), 0:HID]).then_inc(o_st, 16)
            sp.wait_ge(o_st, 16 * NG)

        @block.gpsimd
        def _(gp):
            order = Order(gp, pool_order)
            gp.memset(ident[:, :], 0.0).then_inc(gn, 1)
            gp.memset(ones[:, :], 1.0).then_inc(gn, 1)
            gp.memset(zeros[:, :], 0.0)
            gp.memset(hd[:, 0:AW], 0.0).then_inc(gn, 1)
            gp.memset(hd[:, AW:TW], -BIG).then_inc(gn, 1)
            gp.wait_ge(gn, 4)
            gp.iota(iota_tile[:, :], pattern=[[P, NT]], base=0, channel_multiplier=0, allow_small_or_imprecise_dtypes=True).then_inc(gn, 1)
            gp.iota(part_base[:, :], pattern=[[0, 1]], base=0, channel_multiplier=EPP, allow_small_or_imprecise_dtypes=True).then_inc(gn, 1)
            gp.iota(node[:, :], pattern=[[P, NT]], base=0, channel_multiplier=1, allow_small_or_imprecise_dtypes=True).then_inc(gn, 1)
            gp.affine_select(out=ident[:, :], in_=ident[:, :], compare_op=ALU.not_equal, fill=1.0, base=0,
                             pattern=[[-1, 128]], channel_multiplier=1).then_inc(gn, 1)

            def gather(b, k, between=None):
                gp.wait_ge(e_logits_used, b + 1)
                order.mark(gp.tensor_copy(idx[:, k, 0, :], src_i[:, bass.ds(b * T, T)]))
                order.link(gp.tensor_copy(idx[:, k, 1, :], dst_i[:, bass.ds(b * T, T)]))
                settle(gp)
                for t in range(T):
                    gp.indirect_dma_start(out=Q[:, k, t, :], out_offset=None, in_=q_tab,
                                          in_offset=bass.IndirectOffsetOnAxis(ap=idx[:, k, 1, t:t + 1], axis=0)).then_inc(e_gath[k], 16)
                if between:
                    between()
                gp.wait_ge(e_used, b + 1)
                settle(gp)
                for t in range(T):
                    gp.indirect_dma_start(out=KV[:, k, t, :], out_offset=None, in_=kv_tab,
                                          in_offset=bass.IndirectOffsetOnAxis(ap=idx[:, k, 0, t:t + 1], axis=0)).then_inc(e_gath[k], 16)

            def store(b, k):
                gp.wait_ge(e_state, b + 1)
                settle(gp)
                gp.dma_start(log_v[:, bass.ds(b * T, T), :], S[:, k, :, :]).then_inc(e_scat[k], 16)

            gp.wait_ge(d_st, 16)
            gp.wait_ge(d_row, 1)
            with gp.Fori(0, NG) as g:
                gp.wait_ge(d_used, g + 1)
                settle(gp)
                order.base, order.n = g, 0
                order.link(gp.tensor_copy(part_ring[:, :], part_i[:, bass.ds(g * G, G)]))
                settle(gp)
                for j in range(G):
                    gp.indirect_dma_start(out=dst_rows[:, j, :], out_offset=None, in_=dst_tab,
                                          in_offset=bass.IndirectOffsetOnAxis(ap=part_ring[:, j:j + 1], axis=0)).then_inc(d_in[j], 16)
            order.base, order.n = 0, NG
            for k in range(2):
                gp.dma_start(log[E + k:E + k + 1, :], hd[k:k + 1, :]).then_inc(e_scat[k], 16)
            gp.wait_ge(e_prep, 1)
            gp.wait_ge(gp_stored, 5 * 16 * NG + 1)
            gp.wait_ge(d_ok, 1)
            gp.wait_ge(s_idx, 16)
            gather(0, 0)
            gather(1, 1)
            PER = 2 * 2
            start = order.n

            def turn(r, more=True, between=None):
                order.base, order.n = start + r * PER, 0
                for k in range(2):
                    if more:
                        gather(2 * r + 2 + k, k, between if k == 0 else None)
                    store(2 * r + k, k)

            def bias(L, g):
                gp.wait_ge(xh_ready, w_c2(L, g * G + G - 1) + 1)
                settle(gp)
                for j in range(G):
                    ins = gp.tensor_tensor(xm[:, g * G + j, :], xm[:, g * G + j, :], b2_b[:, :], ALU.add)
                ins.then_inc(b2_ok, 1)

            def layer(L, more):
                with gp.Fori(0, NG) as g:
                    turn(L * (2 * NG) + g)
                gp.wait_ge(q_ok, L + 1)
                settle(gp)
                gp.wait_ge(ctx_done, L + 2)
                settle(gp)
                with gp.Fori(0, NG) as g:
                    for j in range(G):
                        i = g * G + j
                        gp.wait_ge(pt_done, w_c1(L, i) + 1)
                        settle(gp)
                        gp.tensor_tensor(xh[:, j, :].rearrange("p (h d) -> p h d", d=DH), qe[:, i, :].rearrange("p (h d) -> p h d", d=DH),
                                         qsum[:, bass.ds(i * HEADS, HEADS)].unsqueeze(2).to_broadcast([P, HEADS, DH]), ALU.mult).then_inc(xh_ready, 1)
                gp.wait_ge(s_w2, L * 32 + 32)
                settle(gp)
                bias(L, 0)
                settle(gp)
                with gp.Fori(0, NG - 1) as g:
                    turn(L * (2 * NG) + NG + g, between=lambda: bias(L, g + 1))
                turn(L * (2 * NG) + 2 * NG - 1, more)

            with gp.Fori(0, LAYERS - 1) as L:
                layer(L, True)
            layer(LAYERS - 1, False)
            order.base, order.n = 0, start + (NB // 2 - 1) * PER
            for k in range(2):
                gp.wait_ge(e_scat[k], 16 + 16 * (NB // 2))
            gp.wait_ge(e_state, NB)
            gp.indirect_dma_start(out=hd[:, :], out_offset=None, in_=log,
                                  in_offset=bass.IndirectOffsetOnAxis(ap=end_i[:, NT:NT + 1], axis=0)).then_inc(hd_in, 16)
            gp.wait_ge(s_vec, 3 * 16)
            gp.wait_ge(y_free, LAYERS * NT + 2)
            gp.iota(iota_row[:, :], pattern=[[1, P]], base=0, channel_multiplier=0, allow_small_or_imprecise_dtypes=True).then_inc(gn, 1)
            gp.affine_select(out=lower[:, :], in_=ones[0:P, 0:P], compare_op=ALU.is_gt, fill=0.0, base=0,
                             pattern=[[-1, P]], channel_multiplier=1).then_inc(gn, 1)
            gp.wait_ge(x_in, 16)
            base = order.n
            with gp.Fori(0, NG) as g:
                order.base, order.n = base + g * 2, 0
                for j in range(G):
                    gp.wait_ge(f_used, g * G + j + 1)
                settle(gp)
                order.link(gp.tensor_copy(part_ring[:, :], end_i[:, bass.ds(g * G, G)]))
                settle(gp)
                for j in range(G):
                    gp.indirect_dma_start(out=fl[:, j, :], out_offset=None, in_=log,
                                          in_offset=bass.IndirectOffsetOnAxis(ap=part_ring[:, j:j + 1], axis=0)).then_inc(f_run[j], 16)
                rows = qe[:, bass.ds(g * G, G), :]
                order.link(gp.tensor_tensor(rows, rows, xm[:, bass.ds(g * G, G), :], ALU.add))
                settle(gp)
                gp.tensor_tensor(rows, rows, vecs[:, 1:2, :].to_broadcast([P, G, HID]), ALU.add).then_inc(f_xmx, 1)
                assert order.n == 2

        @block.vector
        def _(v):
            order = Order(v, dve_order)
            link, mark, need = order.link, order.mark, order.need
            total = [0]

            def enter(register, per):
                order.base, order.n = total[0] + register * per, 0

            def leave(turns, per):
                assert order.n == per, (order.n, per)
                total[0] += turns * per
                order.base, order.n = 0, total[0]

            def straight():
                total[0] = order.n

            def inv_std(n0, n):
                a, y, t = nr_v[:, 0:n], nr_i[:, 0:n].bitcast(F32), nr_t[:, 0:n]
                link(nc.vector.tensor_scalar(a, mv[:, bass.ds(n0, n), 1], EPS, None, ALU.add))
                link(nc.vector.tensor_scalar(nr_i[:, 0:n], nr_v[:, 0:n].bitcast(I32), -0.5, RSQRT_SEED, ALU.mult, ALU.add))
                for step in range(3):
                    link(nc.vector.tensor_tensor(t, y, y, ALU.mult))
                    link(nc.vector.tensor_tensor(t, t, a, ALU.mult))
                    link(nc.vector.tensor_scalar(t, t, -0.5, 1.5, ALU.mult, ALU.add))
                    link(nc.vector.tensor_tensor(rstd[:, bass.ds(n0, n)] if step == 2 else y, y, t, ALU.mult))
                link(nc.vector.scalar_tensor_tensor(out=nmr[:, bass.ds(n0, n)], in0=mv[:, bass.ds(n0, n), 0], scalar=-1.0,
                                                    in1=rstd[:, bass.ds(n0, n)], op0=ALU.mult, op1=ALU.mult))

            INV = 15

            v.sem_inc(pt_done, G)
            v.sem_inc(xh_copied, G)
            for s in (gp_stored, hg_ok, ctx_done, m_ok, oh_ps, f_pre, d_used):
                v.sem_inc(s, 1)
            v.sem_inc(hT_ready, 2)
            v.sem_inc(gp_free, 2)
            v.sem_inc(e_used, 2)
            v.sem_inc(e_logits_used, 2)
            v.sem_inc(qsub, 2)
            v.sem_inc(f_y, 2)
            v.sem_inc(qk_act, 2)
            v.sem_inc(ek_used, G)
            v.sem_inc(at_free, 2)
            v.sem_inc(y_free, 2)
            v.sem_inc(f_used, G)

            v.wait_ge(s_dst, 16)
            v.wait_ge(gn, 8)
            link(nc.vector.tensor_copy(dst_f[:, :], dst_i[:, :]))
            link(nc.vector.memset(dst_x[:, 0:1], -1.0))
            link(nc.vector.tensor_tensor(same[:, :], dst_f[:, :], dst_x[:, 0:EPP], ALU.is_equal))
            mark(nc.vector.tensor_copy(ends[:, 0:1], dst_f[:, 0:1]))
            link(nc.vector.tensor_copy(ends[:, 1:2], dst_f[:, EPP - 1:EPP]))
            v.sem_inc(d_f, 1)
            mark(nc.vector.memset(P7[:, :], -BIG))
            mark(nc.vector.memset(L7[:, :, :], -BIG))
            mark(nc.vector.memset(M7[:, :, :], -BIG))
            mark(nc.vector.memset(S[:, :, :, :], 0.0))
            mark(nc.vector.memset(BD[:, :, :], 0.0))
            mark(nc.vector.tensor_scalar(key_tile[:, 0, :], iota_tile[:, :], -1.0, ends[:, 0:1], ALU.mult, ALU.add))
            mark(nc.vector.tensor_scalar(key_tile[:, 1, :], iota_tile[:, :], -1.0, ends[:, 1:2], ALU.mult, ALU.add))
            link(nc.vector.memset(vgnn[:, :, :, DH:VW], 1.0))
            v.sem_inc(e_prep, 1)
            link(nc.vector.tensor_scalar(dst_junk[:, :], dst_f[:, :], ends[:, 0:1], 0.0, ALU.is_equal, ALU.add, accum_out=run1[:, 0:1]))
            link(nc.vector.tensor_scalar(end_f[:, NT:NT + 1], run1[:, :], part_base[:, 0:1], -1.0 - NO_RUN, ALU.add, ALU.add))
            link(nc.vector.scalar_tensor_tensor(out=end_f[:, NT:NT + 1], in0=run1[:, :], scalar=EPP - 0.5, in1=end_f[:, NT:NT + 1],
                                                op0=ALU.is_lt, op1=ALU.mult))
            v.wait_ge(d_b, 1)
            link(nc.vector.tensor_copy(first_row[:, :], psX[0:P, 0:P]))
            for t, op in ((part_f, ALU.is_le), (firsts, ALU.is_equal)):
                link(nc.vector.tensor_tensor(compared[:, :, :], first_row[:, :].unsqueeze(1).to_broadcast([P, NT, P]),
                                             node[:, :].unsqueeze(2).to_broadcast([P, NT, P]), op))
                link(nc.vector.tensor_reduce(out=t[:, :], in_=compared[:, :, :], axis=AX.X, op=ALU.add))
            link(nc.vector.tensor_scalar(part_f[:, :], part_f[:, :], -1.0, None, ALU.add))
            link(nc.vector.tensor_scalar(upto[:, :], part_f[:, :], 0.0, None, ALU.max))
            link(nc.vector.tensor_copy(part_i[:, :], upto[:, :]))
            v.sem_inc(d_row, 1)
            straight()


            def aggregate(g):
                settle(v)
                for j in range(G):
                    n = mark(nc.vector.bn_aggr(mvs[:, j, :], bst[:, j, :]))
                need(n)
                settle(v)
                link(nc.vector.tensor_copy(mv[:, bass.ds(g * G, G), :], mvs[:, :, :]))

            def stats(g):
                for j in range(G):
                    n = mark(nc.vector.bn_stats(bst[:, j, :], xm[:, g * G + j, :]))
                need(n)
                aggregate(g)

            for g in range(NG):
                v.wait_ge(s_x[g], 16)
                stats(g)
            inv_std(0, NT)
            straight()
            v.wait_ge(s_wg, 8 * 16)
            v.wait_ge(d_st, 16)
            def rows_of_x(i, j):
                v.wait_ge(pt_done, i + 1)
                v.wait_ge(xh_copied, i + 1)
                nc.vector.tensor_scalar(xh[:, j, :], xm[:, i, :], mv[:, i, 0:1], rstd[:, bass.ds(i, 1)],
                                        ALU.subtract, ALU.mult).then_inc(xh_ready, 1)

            for j in range(G):
                rows_of_x(j, j)

            def gnn_group(g, last):
                enter(g, 2 * G)
                for j in range(G):
                    i = g * G + j
                    v.wait_ge(d_in[j], g * 16 + 16)
                    if not last:
                        settle(v)
                    for t, op in ((upto, ALU.is_le), (own, ALU.is_equal)):
                        link(nc.vector.tensor_scalar(dst_junk[:, :], dst_rows[:, j, :], node[:, bass.ds(i, 1)], 0.0, op, ALU.add,
                                                     accum_out=t[:, bass.ds(i, 1)]))
                v.sem_inc(d_used, 1)
                v.wait_ge(gp_stored, g * 5 * 16 + 1)
                for j in range(G):
                    i = g * G + j
                    v.wait_ge(gp_done, i + 1)
                    nc.vector.tensor_tensor(qe[:, i, :], psQK(j)[:, 0:HID], gnn_b[:, 0:HID], ALU.add)
                    nc.vector.tensor_tensor(kst[:, i, :], psQK(j)[:, HID:2 * HID], gnn_b[:, HID:2 * HID], ALU.add)
                    nc.vector.tensor_tensor(vgnn[:, i, :, 0:DH], psVS(j)[:, 0:HID].rearrange("p (h d) -> p h d", d=DH),
                                            gnn_b[:, 2 * HID:3 * HID].rearrange("p (h d) -> p h d", d=DH), ALU.add)
                    nc.vector.tensor_tensor(ring[:, j, :], psVS(j)[:, HID:2 * HID], gnn_b[:, 3 * HID:4 * HID], ALU.add).then_inc(gp_free, 1)
                    if not last:
                        rows_of_x(i + G, j)

            groups(v, gnn_group)
            leave(NG, 2 * G)
            link(nc.vector.tensor_scalar(part_f[:, :], part_f[:, :], float(EPP), -1.0 - NO_RUN, ALU.mult, ALU.add))
            link(nc.vector.tensor_tensor(end_f[:, 0:NT], part_f[:, :], upto[:, :], ALU.add))
            for t, op in ((own, ALU.is_gt), (firsts, ALU.is_lt)):
                link(nc.vector.scalar_tensor_tensor(out=end_f[:, 0:NT], in0=t[:, :], scalar=0.5, in1=end_f[:, 0:NT], op0=op, op1=ALU.mult))
            link(nc.vector.tensor_scalar(end_f[:, :], end_f[:, :], float(NO_RUN), None, ALU.add))
            link(nc.vector.tensor_copy(end_i[:, :], end_f[:, :]))
            v.sem_inc(d_ok, 1)
            v.wait_ge(xh_ready, NT)
            mark(nc.vector.memset(mv[:, :, 0], 0.0))
            link(nc.vector.tensor_tensor(mv[:, :, 1], mv[:, :, 1], rstd[:, :], ALU.mult))
            link(nc.vector.tensor_tensor(mv[:, :, 1], mv[:, :, 1], rstd[:, :], ALU.mult))
            straight()

            def seven(t):
                return t.rearrange("p (h w) -> p h w", h=HEADS)

            def edge_logits(b, turn, k):
                prev = 1 - k
                v.wait_ge(e_gath[k], turn * (2 * T * 16) + 2 * T * 16)
                link(nc.vector.tensor_copy(sm[:, k, :], same[:, bass.ds(b * T, T)]))
                mark(nc.vector.tensor_scalar(seven(P7[:, 0:HEADS * W7])[:, :, 1:1 + T],
                                                   sm[:, k, :].unsqueeze(1).to_broadcast([P, HEADS, T]),
                                                   -1.0, BIG, ALU.add, ALU.mult))
                mark(nc.vector.tensor_copy(seven(L7[:, k, :])[:, :, 0], seven(M7[:, prev, :])[:, :, T]))
                link(nc.vector.tensor_tensor(Q[:, k, :, :], Q[:, k, :, :], KV[:, k, :, 0:HID], ALU.mult))
                link(nc.vector.tensor_reduce(out=seven(L7[:, k, :])[:, :, 1:1 + T].rearrange("p h t -> p t h"),
                                             in_=Q[:, k, :, :].rearrange("p t (h d) -> p t h d", d=DH), axis=AX.X, op=ALU.add))
                v.sem_inc(e_logits_used, 1)
                link(nc.vector.tensor_tensor_scan(F7[:, :], P7[:, 0:HEADS * W7], L7[:, k, :], initial=-BIG, op0=ALU.add, op1=ALU.max))
                link(nc.vector.tensor_tensor_scan(M7[:, k, ::-1], P7[:, 1:HEADS * W7 + 1][:, ::-1], F7[:, ::-1], initial=-BIG,
                                                  op0=ALU.add, op1=ALU.max))
                nc.vector.tensor_tensor(E7[:, k, :], L7[:, k, :], M7[:, k, :], ALU.subtract).then_inc(e_logit, 1)

            def edge_sums(b, turn, k):
                prev = 1 - k
                v.wait_ge(e_scat[k], turn * 16 + 16)
                v.wait_ge(e_exp, b + 1)
                w = seven(E7[:, k, :])
                mark(nc.vector.tensor_tensor(seven(carried[:, :]), seven(S[:, prev, T - 1, 0:AW]),
                                             w[:, :, 0:1].to_broadcast([P, HEADS, VW]), ALU.mult))
                mark(nc.vector.tensor_copy(S[:, k, :, AW:TW], seven(M7[:, k, :])[:, :, 1:1 + T].rearrange("p h t -> p t h")))
                n = mark(nc.vector.tensor_tensor(S[:, k, :, 0:AW].rearrange("p t (h w) -> p t h w", h=HEADS),
                                             KV[:, k, :, HID:KVW].rearrange("p t (h w) -> p t h w", h=HEADS),
                                             w[:, :, 1:1 + T].rearrange("p h t -> p t h").unsqueeze(3).to_broadcast([P, T, HEADS, VW]), ALU.mult))
                need(n)
                v.sem_inc(e_used, 1)
                for t in range(T):
                    before = carried[:, :] if t == 0 else S[:, k, t - 1, 0:AW]
                    link(nc.vector.scalar_tensor_tensor(out=S[:, k, t, 0:AW], in0=before, scalar=sm[:, k, t:t + 1],
                                                        in1=S[:, k, t, 0:AW], op0=ALU.mult, op1=ALU.add))
                v.sem_inc(e_state, 1)

            EDGE = 10 + T

            def edge_steps(turn):
                b = 2 * turn
                edge_logits(b, turn, 0)
                yield
                edge_sums(b, turn, 0)
                edge_logits(b + 1, turn, 1)
                yield
                edge_sums(b + 1, turn, 1)
                yield

            v.wait_ge(gp_stored, 5 * 16 * NG + 1)
            nc.vector.memset(vmix[:, :, :, 128:129], 1.0).then_inc(mix_start, 1)

            def residual(L, g, done, free, prepare=None):
                for j in range(G + 1):
                    i = g * G + j
                    if j < G:
                        v.wait_ge(done, L * NT + i + 1)
                        nc.vector.tensor_tensor(xm[:, i, :], psY(j), xm[:, i, :], ALU.add).then_inc(free, 1)
                        if prepare:
                            prepare(j)
                    if j:
                        v.wait_ge(free, L * NT + i - 1 + 3)
                        settle(v)
                        n = mark(nc.vector.bn_stats(bst[:, j - 1, :], xm[:, i - 1, :]))
                need(n)
                aggregate(g)

            def layer_a(L, g):
                edges = edge_steps(L * (2 * NG) + g)
                for j in range(G):
                    i = g * G + j
                    if j in (0, 2, 4):
                        next(edges)
                    ps = psQ(j).rearrange("p (h d) -> p h d", d=DH)
                    v.wait_ge(qk_done, L * NT + i + 1)
                    link(nc.vector.tensor_reduce(out=mx8[:, j, :], in_=ps, axis=AX.X, op=ALU.max))
                    nc.vector.tensor_tensor(qe[:, i, :].rearrange("p (h d) -> p h d", d=DH), ps,
                                            mx8[:, j, :].unsqueeze(2).to_broadcast([P, HEADS, DH]), ALU.subtract).then_inc(qsub, 1)
                    v.wait_ge(qk_act, L * NT + i + 3)
                    n = mark(nc.vector.tensor_tensor(kmx[:, :], kmx[:, :], kst[:, i, :], ALU.max))
                need(n)

            LA = 2 * G + 2 * EDGE
            assert NB == LAYERS * 2 * NG * 2

            with v.Fori(0, LAYERS) as L:
                LAYER = (INV + 1) + NG * LA + 4 + (NG + 1) + 12 + NG * (1 + 2 * G) + INV + NG * (1 + 2 * G + 2 * EDGE)
                lbase = total[0] + L * LAYER
                used = [0]

                def part(register, per):
                    order.base, order.n = lbase + used[0] + register * per, 0

                def end_part(turns, per):
                    assert order.n == per, (order.n, per)
                    used[0] += turns * per

                part(0, INV + 1)
                inv_std(0, NT)
                v.sem_inc(ln_ok, 1)
                link(nc.vector.memset(kmx[:, :], -3e38))
                end_part(1, INV + 1)
                settle(v)
                with v.Fori(0, NG) as g:
                    part(g, LA)
                    layer_a(L, g)
                end_part(NG, LA)
                part(0, 4)
                v.sem_inc(km_col, 1)
                v.wait_ge(km_t, L + 1)
                link(nc.vector.tensor_reduce(out=km[:, :], in_=psX[:, 0:C * P].rearrange("p (c n) -> p c n", c=C), axis=AX.X, op=ALU.max))
                for c in range(C):
                    link(nc.vector.tensor_scalar(dg[:, c, :], ident[:, :], km[:, c:c + 1], None, ALU.mult))
                v.sem_inc(km_dg, 1)
                v.wait_ge(km_b, L + 1)
                link(nc.vector.tensor_copy(kmx_b[:, :], psX[0:P, 256:512]))
                end_part(1, 4)
                v.wait_ge(qk_act, L * NT + NT + 2)
                settle(v)
                v.wait_ge(qexp, L * NT + NT)
                settle(v)
                with v.Fori(0, NG) as g:
                    part(g, 1)
                    for j in range(G):
                        v.wait_ge(ek_used, L * NT + g * G + j + 1)
                        nc.vector.tensor_tensor(ek[:, j, :], kst[:, g * G + j, :], kmx_b[:, :], ALU.subtract).then_inc(kd, 1)
                    mark(nc.vector.tensor_reduce(out=qsum[:, bass.ds(g * (G * HEADS), G * HEADS)],
                                                 in_=qe[:, bass.ds(g * G, G), :].rearrange("p j (h d) -> p (j h) d", d=DH),
                                                 axis=AX.X, op=ALU.add))
                end_part(NG, 1)
                part(0, 1)
                need(0)
                link(nc.vector.reciprocal(qsum[:, :], qsum[:, :]))
                end_part(1, 1)
                v.sem_inc(q_ok, 1)
                part(0, 12)
                v.wait_ge(ctx_done, L + 2)
                for c in range(C):
                    n = mark(nc.vector.reciprocal(rS[:, c:c + 1], psC(c)[:, 128:129]))
                need(n)
                for c in range(C):
                    for h in range(4):
                        r = slice(h * DH, h * DH + DH)
                        n = mark(nc.vector.tensor_scalar(BD[r, c, r], psC(c)[r, r], rS[r, c:c + 1], None, ALU.mult))
                need(n)
                v.sem_inc(bd_ok, 1)
                v.wait_ge(bdt, L + 1)
                nc.vector.tensor_copy(BDT[:, :, :], psX[:, 0:256].rearrange("p (c n) -> p c n", c=C)).then_inc(bdt_ok, 1)
                v.wait_ge(m_done, L + 1)
                link(nc.vector.tensor_copy(m_sb[:, :, :], psM[:, :].rearrange("p (c n) -> p c n", c=C)))
                link(nc.vector.tensor_tensor(m_sb[0:DH, 0, :], m_sb[0:DH, 0, :], bo_b[:, :], ALU.add))
                end_part(1, 12)
                v.sem_inc(m_ok, 1)
                PER = 1 + 2 * G
                with v.Fori(0, NG) as g:
                    part(g, PER)
                    residual(L, g, at_done, at_free)
                end_part(NG, PER)
                part(0, INV)
                inv_std(0, NT)
                v.sem_inc(ln_ok, 1)
                end_part(1, INV)
                PER = 1 + 2 * G + 2 * EDGE
                with v.Fori(0, NG) as g:
                    part(g, PER)
                    turn = L * (2 * NG) + NG + g
                    v.wait_ge(b2_ok, L * NG + g + 1)
                    settle(v)

                    def logits(j):
                        if j in (1, 3):
                            edge_logits(2 * turn + j // 2, turn, j // 2)

                    residual(L, g, y_done, y_free, logits)
                    for k in range(2):
                        edge_sums(2 * turn + k, turn, k)
                end_part(NG, PER)
                assert used[0] == LAYER
            total[0] += LAYERS * LAYER
            order.base, order.n = 0, total[0]

            v.wait_ge(hd_in, 16)
            last = S[:, 1, T - 1, :]
            mark(nc.vector.tensor_copy(keys[:, 0, :], hd[:, AW:TW]))
            mark(nc.vector.tensor_copy(keys[:, 1, :], last[:, AW:TW]))
            mark(nc.vector.tensor_copy(keys[:, 2, :], ends[:, 0:1].to_broadcast([P, HEADS])))
            link(nc.vector.tensor_copy(keys[:, 3, :], ends[:, 1:2].to_broadcast([P, HEADS])))
            v.sem_inc(b_k, 1)
            v.wait_ge(b_t, 1)
            for i, t in enumerate((V2, K2)):
                for s in range(2):
                    n = mark(nc.vector.tensor_copy(t[:, :].rearrange("h (p s) -> h s p", s=2)[:, s, :],
                                                   psX[0:HEADS, (2 * i + s) * 128:(2 * i + s) * 128 + P]))
            need(n)
            link(nc.vector.memset(pen2[:, :], -BIG))
            link(nc.vector.tensor_tensor(F2[:, 1:2 * P], K2[:, 1:2 * P], K2[:, 0:2 * P - 1], ALU.is_equal))
            link(nc.vector.tensor_scalar(pen2[:, 1:2 * P], F2[:, 1:2 * P], -1.0, BIG, ALU.add, ALU.mult))
            link(nc.vector.tensor_tensor_scan(F2[:, :], pen2[:, 0:2 * P], V2[:, :], initial=-BIG, op0=ALU.add, op1=ALU.max))
            link(nc.vector.tensor_tensor_scan(M2[:, ::-1], pen2[:, 1:2 * P + 1][:, ::-1], F2[:, ::-1], initial=-BIG, op0=ALU.add, op1=ALU.max))
            for s in range(2):
                n = mark(nc.vector.tensor_copy(F2[:, s * P:(s + 1) * P], M2[:, :].rearrange("h (p s) -> h s p", s=2)[:, s, :]))
            need(n)
            v.sem_inc(b_m, 1)
            v.wait_ge(b_f, 1)
            for s in range(2):
                n = mark(nc.vector.tensor_tensor(fac[:, s, :], keys[:, s, :], bank[6][0:P, s * HEADS:(s + 1) * HEADS], ALU.subtract))
            need(n)
            v.sem_inc(b_d, 1)
            v.wait_ge(b_e, 1)
            for s, t in enumerate((hd[:, 0:AW], last[:, 0:AW])):
                rows = t.rearrange("p (h w) -> p h w", h=HEADS)
                n = mark(nc.vector.tensor_tensor(rows, rows, fac[:, s, :].unsqueeze(2).to_broadcast([P, HEADS, VW]), ALU.mult))
            need(n)
            v.sem_inc(hd_used, 1)
            straight()

            v.wait_ge(s_vec, 3 * 16)
            v.wait_ge(s_const, 16 * CONSTS)
            v.wait_ge(gn, 10)
            v.wait_ge(skip_in, 16)
            heads = lambda t: t.rearrange("p (x w) -> p x w", w=VW)
            rows_of = lambda t, g: t[:, bass.ds(g * G, G), 0:HID]
            per_group = 2 * G + 3
            with v.Fori(0, NG) as g:
                enter(g, per_group)
                for j in range(G):
                    i = g * G + j
                    if j == 0:
                        v.wait_ge(oh_ps, g * G + 1)
                    for s in range(2):
                        n = mark(nc.vector.tensor_scalar(onehots[:, j, s, :], iota_row[:, :], key_tile[:, s, bass.ds(i, 1)], None, ALU.is_equal))
                    need(n)
                    v.sem_inc(oh_ok, 1)
                for j in range(G):
                    v.wait_ge(f_run[j], g * 16 + 16)
                    v.wait_ge(oh_ps, g * G + j + 2)
                    nc.vector.tensor_tensor(agg[:, j * AW:(j + 1) * AW], fl[:, j, 0:AW], psB(j), ALU.add).then_inc(f_used, 1)
                v.wait_ge(f_used, g * G + G + G)
                settle(v)
                link(nc.vector.tensor_scalar(s40[:, :], heads(agg)[:, :, DH], 1e-30, None, ALU.max))
                link(nc.vector.reciprocal(s40[:, :], s40[:, :]))
                v.wait_ge(f_pre, g + 1)
                settle(v)
                link(nc.vector.tensor_tensor(mean.rearrange("p (x d) -> p x d", d=DH), heads(agg)[:, :, 0:DH],
                                             s40[:, :].unsqueeze(2).to_broadcast([P, G * HEADS, DH]), ALU.mult))
                nc.vector.tensor_tensor(rows_of(vst, g), rows_of(vst, g), mean.rearrange("p (j f) -> p j f", j=G), ALU.add).then_inc(f_pre, 1)
            leave(NG, per_group)
            v.wait_ge(xn_in, 16)

            def group_stats(g):
                settle(v)
                for j in range(G):
                    n = mark(nc.vector.bn_stats(bst[:, j, :], vst[:, g * G + j, 0:HID]))
                need(n)
                aggregate(g)

            per_group = 2 + 2 * G
            with v.Fori(0, NG) as g:
                enter(g, per_group)
                v.wait_ge(f_gelu, g + 1)
                settle(v)
                link(nc.vector.tensor_tensor(rows_of(vst, g), rows_of(vst, g), rows_of(kst, g), ALU.add))
                group_stats(g)
            leave(NG, per_group)
            inv_std(0, NT)
            v.sem_inc(y_norm, 1)
            straight()
            per_group = 3 + 2 * G
            with v.Fori(0, NG) as g:
                enter(g, per_group)
                v.wait_ge(y_normed, g * G + G)
                settle(v)
                link(nc.vector.tensor_tensor(rows_of(vst, g), rows_of(vst, g), vecs[:, 0:1, :].to_broadcast([P, G, HID]), ALU.mult))
                v.wait_ge(f_xmx, g + 1)
                settle(v)
                link(nc.vector.tensor_tensor(rows_of(vst, g), rows_of(vst, g), rows_of(qe, g), ALU.add))
                group_stats(g)
            leave(NG, per_group)
            inv_std(0, NT)
            v.sem_inc(x1_norm, 1)
            straight()
            per_group = G + 1
            with v.Fori(0, NG) as g:
                enter(g, per_group)
                v.wait_ge(x1_ok, g * G + G)
                settle(v)
                for j in range(G):
                    i = g * G + j
                    mark(nc.vector.scalar_tensor_tensor(out=dots[:, j, :], in0=kst[:, i, :], scalar=1.0, in1=vecs[:, 2, :],
                                                        op0=ALU.mult, op1=ALU.mult, accum_out=wcol[:, bass.ds(i, 1)]))
                link(nc.vector.tensor_tensor(rows_of(qe, g), rows_of(vst, g), rows_of(kst, g), ALU.add))
            leave(NG, per_group)
            v.sem_inc(xx_ok, 1)
            link(nc.vector.tensor_scalar(wcol[:, :], wcol[:, :], br_b[:, 0:1], None, ALU.add))
            v.sem_inc(w_ok, 1)
            v.wait_ge(w_t, 1)
            link(nc.vector.tensor_copy(wrow[:, :], psX[0:NT, 0:P]))
            v.sem_inc(w_row, 1)

            v.wait_ge(w_b, 16)
            link(nc.vector.memset(cnt[:, :, :], 0.0))
            for n in range(NT):
                w = wcol[:, n:n + 1]
                if n:
                    link(nc.vector.tensor_scalar(junk[:, 0:n * P], QWB[:, 0:n * P], w, 0.0, ALU.is_ge, ALU.add, accum_out=cnt[:, 0, n:n + 1]))
                link(nc.vector.tensor_scalar(junk[:, n * P:N], QWB[:, n * P:N], w, 0.0, ALU.is_gt, ALU.add, accum_out=cnt[:, 1, n:n + 1]))
                link(nc.vector.scalar_tensor_tensor(out=junk[:, n * P:(n + 1) * P], in0=QWB[:, n * P:(n + 1) * P], scalar=w, in1=lower[:, :],
                                                    op0=ALU.is_equal, op1=ALU.mult, accum_out=cnt[:, 2, n:n + 1]))
            link(nc.vector.tensor_tensor(cnt[:, 0, :], cnt[:, 0, :], cnt[:, 1, :], ALU.add))
            link(nc.vector.tensor_tensor(cnt[:, 0, :], cnt[:, 0, :], cnt[:, 2, :], ALU.add))
            link(nc.vector.scalar_tensor_tensor(out=wcol[:, :], in0=cnt[:, 0, :], scalar=float(KEPT) - 0.5, in1=wcol[:, :],
                                                op0=ALU.is_lt, op1=ALU.mult))
            with v.Fori(0, NG) as g:
                for j in range(G):
                    i = g * G + j
                    v.wait_ge(f_y, i + 3)
                    ins = nc.vector.scalar_tensor_tensor(out=vst[:, i, 0:HID], in0=vst[:, i, 0:HID], scalar=wcol[:, bass.ds(i, 1)],
                                                         in1=qe[:, i, :], op0=ALU.mult, op1=ALU.add)
                ins.then_inc(o_ok, 1)

        @block.scalar
        def _(act):
            order = Order(act, act_order)

            def turned(w, j, gain, shift):
                act.wait_ge(pt_done, w + 1 + G)
                if gain is None:
                    nc.scalar.activation(hT[:, j % 3, :, :], psT(j), ACT.Copy).then_inc(hT_ready, 1)
                else:
                    nc.scalar.activation(hT[:, j % 3, 0, :], psT(j)[:, 0, :], ACT.Identity, scale=gain[0], bias=shift[0])
                    nc.scalar.activation(hT[:, j % 3, 1, :], psT(j)[:, 1, :], ACT.Identity, scale=gain[1], bias=shift[1]).then_inc(hT_ready, 1)

            def normalised(w, i, j):
                act.wait_ge(pt_done, w + 1)
                settle(act)
                nc.scalar.activation(xh[:, j, :], xm[:, i, :], ACT.Identity, scale=rstd[:, bass.ds(i, 1)],
                                     bias=nmr[:, bass.ds(i, 1)]).then_inc(xh_ready, 1)

            def hidden(h0, i, j, function, bias):
                for half in range(2):
                    act.wait_ge(h_done, h0 + i * 2 + half + 1)
                    for k in range(4):
                        ins = nc.scalar.activation(hg[:, j % 2, 4 * half + k, :], psH(j, half)[:, k, :], function,
                                                   bias=bias[:, 4 * half + k:4 * half + k + 1])
                    ins.then_inc(hg_ok, 1)

            with act.Fori(0, NG) as g:
                for j in range(G):
                    i = g * G + j
                    act.wait_ge(xh_ready, i + 1)
                    nc.scalar.activation(xm[:, i, :], xh[:, j, :], ACT.Copy).then_inc(xh_copied, 1)
                    turned(i, j, None, None)
            def edge_weights(turn, k):
                act.wait_ge(e_logit, 2 * turn + k + 1)
                nc.scalar.activation(E7[:, k, :], E7[:, k, :], ACT.Exp, scale=GNN_SCALE).then_inc(e_exp, 1)

            act.wait_ge(s_const, 16 * CONSTS)
            act.wait_ge(mix_start, 1)
            with act.Fori(0, LAYERS) as L:
                act.wait_ge(hg_ok, L * (2 * NT) + 1)
                settle(act)
                order.base, order.n = L * 3, 0
                order.mark(nc.scalar.activation(cur[:, 0:2, :], ln1[:, :, bass.ds(L, 1), :].rearrange("k s l c -> k s (l c)"), ACT.Copy))
                order.mark(nc.scalar.activation(cur[:, 2:4, :], ln2[:, :, bass.ds(L, 1), :].rearrange("k s l c -> k s (l c)"), ACT.Copy))
                order.link(nc.scalar.activation(cur_b1[:, :], b1_mix[:, bass.ds(L, 1), :].rearrange("k l c -> k (l c)"), ACT.Copy))
                settle(act)
                gain1, shift1, gain2, shift2 = ([cur[:, s, c:c + 1] for c in range(C)] for s in range(4))
                act.wait_ge(ln_ok, 2 * L + 1)
                settle(act)
                for j in range(G):
                    normalised(w_a(L, j), j, j)
                turned(w_a(L, 0), 0, gain1, shift1)

                def projections(g, last):
                    for j in range(G):
                        i = g * G + j
                        if j + 1 < G or not last:
                            turned(w_a(L, i + 1), (j + 1) % G, gain1, shift1)
                        act.wait_ge(qk_done, L * NT + i + 1)
                        nc.scalar.activation(kst[:, i, :], psKV(j)[:, 0:HID], ACT.Copy)
                        nc.scalar.activation(vmix[:, i, :, 0:128], psKV(j)[:, HID:2 * HID].rearrange("p (c f) -> p c f", c=C), ACT.Copy).then_inc(qk_act, 1)
                        if not last:
                            normalised(w_a(L, i + G), i + G, j)
                        act.wait_ge(qsub, L * NT + i + 3)
                        nc.scalar.activation(qe[:, i, :], qe[:, i, :], ACT.Exp, scale=MIX_SCALE).then_inc(qexp, 1)
                        if j in (0, 2):
                            edge_weights(L * (2 * NG) + g, j // 2)

                groups(act, projections)
                with act.Fori(0, NG) as g:
                    for j in range(G):
                        act.wait_ge(kd, L * NT + g * G + j + 1)
                        nc.scalar.activation(ek[:, j, :], ek[:, j, :], ACT.Exp, scale=MIX_SCALE).then_inc(ek_ok, 1)
                with act.Fori(0, NG) as g:
                    for j in range(G):
                        turned(w_c1(L, g * G + j), j, None, None)
                act.wait_ge(ln_ok, 2 * L + 2)
                settle(act)
                for j in range(G):
                    normalised(w_c2(L, j), j, j)
                turned(w_c2(L, 0), 0, gain2, shift2)

                def ffn(g, last):
                    for j in range(G):
                        i = g * G + j
                        if j + 1 < G or not last:
                            turned(w_c2(L, i + 1), (j + 1) % G, gain2, shift2)
                        hidden(L * (2 * NT), i, j, ACT.Gelu, cur_b1)
                        if not last:
                            normalised(w_c2(L, i + G), i + G, j)
                    for k in range(2):
                        edge_weights(L * (2 * NG) + NG + g, k)

                groups(act, ffn)
            act.wait_ge(b_d, 1)
            nc.scalar.activation(fac[:, :, :], fac[:, :, :], ACT.Exp, scale=GNN_SCALE).then_inc(b_e, 1)
            with act.Fori(0, NG) as g:
                act.wait_ge(f_pre, g + 2)
                settle(act)
                nc.scalar.activation(vst[:, bass.ds(g * G, G), 0:HID], vst[:, bass.ds(g * G, G), 0:HID], ACT.Gelu).then_inc(f_gelu, 1)
            for ready, out_rows, done in ((y_norm, vst, y_normed), (x1_norm, kst, x1_ok)):
                act.wait_ge(ready, 1)
                with act.Fori(0, NT) as i:
                    nc.scalar.activation(out_rows[:, i, 0:HID], vst[:, i, 0:HID], ACT.Identity, scale=rstd[:, bass.ds(i, 1)],
                                         bias=nmr[:, bass.ds(i, 1)]).then_inc(done, 1)
            act.wait_ge(x1_ok, NT)

            def copied(i, j):
                act.wait_ge(pt_done, w_f(i) + 1)
                nc.scalar.activation(xh[:, j, :], kst[:, i, :], ACT.Copy).then_inc(xh_ready, 1)

            for j in range(G):
                copied(j, j)
            turned(w_f(0), 0, None, None)

            def routed_ffn(g, last):
                for j in range(G):
                    i = g * G + j
                    if j + 1 < G or not last:
                        turned(w_f(i + 1), (j + 1) % G, None, None)
                    hidden(LAYERS * 2 * NT, i, j, ACT.Gelu_apprx_tanh, b1_ffn)
                    if not last:
                        copied(i + G, j)
                    if j:
                        ffn_rows(i - 1, j - 1)
                ffn_rows(g * G + G - 1, G - 1)

            def ffn_rows(i, j):
                act.wait_ge(xx_ok, 1)
                act.wait_ge(y_done, i + 1 + LAYERS * NT)
                nc.scalar.activation(vst[:, i, 0:HID], psY(j), ACT.Copy).then_inc(f_y, 1)

            groups(act, routed_ffn)

        @block.tensor
        def _(pe):
            mm = nc.tensor.matmul

            def room(sem, n, j):
                pe.wait_ge(sem, n + 1 + (j == 0))

            def turn(w, j):
                pe.wait_ge(xh_ready, w + 1)
                room(hT_ready, w, j)
                for c in range(C):
                    ins = nc.tensor.transpose(psT(j)[:, c, :], xh[:, j, c * 128:(c + 1) * 128], ident[0:P, 0:P])
                ins.then_inc(pt_done, 1)

            def ffn_up(i, j):
                for half in range(2):
                    for k in range(4):
                        for c in range(C):
                            ins = mm(psH(j, half)[:, k, :], w_big[:, c, (4 * half + k) * 128:(4 * half + k + 1) * 128], hT[:, j % 3, c, :],
                                     start=(c == 0), stop=(c == C - 1))
                    ins.then_inc(h_done, 1)

            def ffn_down(free, y0, h0, i, j, bias):
                room(free, y0 + i, j)
                if bias:
                    mm(psY(j), ones[0:1, 0:P], b2_row[0:1, :], start=True, stop=False)
                for half in range(2):
                    pe.wait_ge(hg_ok, h0 + i * 2 + half + 2)
                    for k in range(4 * half, 4 * half + 4):
                        ins = mm(psY(j), hg[:, j % 2, k, :], w_down[:, k, :], start=(k == 0 and not bias), stop=(k == KC - 1))
                ins.then_inc(y_done, 1)

            def ffn(w, free, y0, h0, bias):
                turn(w(0), 0)

                def up(i, j):
                    pe.wait_ge(hT_ready, w(i) + 3)
                    ffn_up(i, j)

                def group(g, last):
                    turn(w(g * G + 1), 1)
                    up(g * G, 0)
                    for j in range(G):
                        i = g * G + j
                        if j + 2 < G or (j + 2 == G and not last):
                            turn(w(i + 2), (j + 2) % G)
                        if j + 1 < G:
                            up(i + 1, j + 1)
                        ffn_down(free, y0, h0, i, j, bias)

                groups(pe, group)

            pe.wait_ge(gn, 8)
            pe.wait_ge(d_f, 1)
            mm(psX[0:P, 0:P], ends[:, 0:1].to_broadcast([P, P]), ident[0:P, 0:P], start=True, stop=True).then_inc(d_b, 1)
            pe.wait_ge(s_wg, 8 * 16)
            turn(0, 0)

            def gnn_group(g, last):
                for j in range(G):
                    i = g * G + j
                    if j + 1 < G or not last:
                        turn(i + 1, (j + 1) % G)
                    pe.wait_ge(hT_ready, i + 3)
                    room(gp_free, i, j)
                    for half, ps in enumerate((psQK(j), psVS(j))):
                        for c in range(C):
                            ins = mm(ps, hT[:, j % 3, c, :], w_big[:, c, half * 512:(half + 1) * 512], start=(c == 0), stop=(c == C - 1))
                    ins.then_inc(gp_done, 1)

            groups(pe, gnn_group)
            with pe.Fori(0, LAYERS) as L:
                pe.wait_ge(s_wqkv, L * 48 + 48)
                settle(pe)
                turn(w_a(L, 0), 0)

                def projections(g, last):
                    for j in range(G):
                        i = g * G + j
                        if j + 1 < G or not last:
                            turn(w_a(L, i + 1), (j + 1) % G)
                        pe.wait_ge(hT_ready, w_a(L, i) + 3)
                        room(qsub, L * NT + i, j)
                        for c in range(C):
                            mm(psQ(j), hT[:, j % 3, c, :], w_qkv[:, c, 0:HID], start=(c == 0), stop=(c == C - 1))
                        room(qk_act, L * NT + i, j)
                        for c in range(C):
                            ins = mm(psKV(j), hT[:, j % 3, c, :], w_qkv[:, c, HID:3 * HID], start=(c == 0), stop=(c == C - 1))
                        ins.then_inc(qk_done, 1)

                groups(pe, projections)
                pe.wait_ge(km_col, L + 1)
                for c in range(C):
                    ins = nc.tensor.transpose(psX[:, c * P:(c + 1) * P], kmx[:, c * 128:(c + 1) * 128], ident[0:P, 0:P])
                ins.then_inc(km_t, 1)
                pe.wait_ge(km_dg, L + 1)
                mm(psX[0:P, 256:512], ones[:, 0:P], dg[:, :, :].rearrange("p c n -> p (c n)"), start=True, stop=True).then_inc(km_b, 1)
                for c in range(C):
                    mm(psC(c), zeros[:, 0:128], zeros[:, :], start=True, stop=False)
                with pe.Fori(0, NG) as g:
                    for j in range(G):
                        i = g * G + j
                        pe.wait_ge(ek_ok, L * NT + i + 1)
                        for c in range(C):
                            ins = mm(psC(c), ek[:, j, c * 128:(c + 1) * 128], vmix[:, i, c, 0:129], start=False, stop=False)
                        ins.then_inc(ek_used, 1)
                for c in range(C):
                    ins = mm(psC(c), zeros[:, 0:128], zeros[:, :], start=False, stop=True)
                ins.then_inc(ctx_done, 1)
                pe.wait_ge(bd_ok, L + 1)
                for c in range(C):
                    ins = nc.tensor.transpose(psX[:, c * 128:(c + 1) * 128], BD[:, c, :], ident[:, :])
                ins.then_inc(bdt, 1)
                pe.wait_ge(bdt_ok, L + 1)
                pe.wait_ge(s_wo, L * 32 + 32)
                for c in range(C):
                    ins = mm(psM[:, c * HID:(c + 1) * HID], BDT[:, c, :], w_o[:, c, :], start=True, stop=True)
                ins.then_inc(m_done, 1)
                pe.wait_ge(m_ok, L + 2)
                settle(pe)
                turn(w_c1(L, 0), 0)

                def attention(g, last):
                    for j in range(G):
                        i = g * G + j
                        if j + 1 < G or not last:
                            turn(w_c1(L, i + 1), (j + 1) % G)
                        pe.wait_ge(hT_ready, w_c1(L, i) + 3)
                        room(at_free, L * NT + i, j)
                        for c in range(C):
                            ins = mm(psY(j), hT[:, j % 3, c, :], m_sb[:, c, :], start=(c == 0), stop=(c == C - 1))
                        ins.then_inc(at_done, 1)

                groups(pe, attention)
                pe.wait_ge(s_w1, L * 16 + 16)
                pe.wait_ge(s_w2, L * 32 + 32)
                settle(pe)
                ffn(lambda i: w_c2(L, i), y_free, L * NT, L * (2 * NT), False)
            pe.wait_ge(b_k, 1)
            for i in range(4):
                ins = nc.tensor.transpose(psX[0:HEADS, i * 128:i * 128 + P], keys[:, i, :], ident[0:P, 0:P])
            ins.then_inc(b_t, 1)
            pe.wait_ge(b_m, 1)
            for s in range(2):
                ins = nc.tensor.transpose(bank[6][0:P, s * HEADS:(s + 1) * HEADS], F2[:, s * P:(s + 1) * P], ident[0:HEADS, 0:HEADS])
            ins.then_inc(b_f, 1)
            pe.wait_ge(hd_used, 1)
            with pe.Fori(0, NG) as g:
                for j in range(G):
                    i = g * G + j
                    pe.wait_ge(oh_ok, i + 1)
                    pe.wait_ge(f_used, i + 4 + (j == 0))
                    mm(psB(j), onehots[:, j, 0, :], hd[:, 0:AW], start=True, stop=False)
                    mm(psB(j), onehots[:, j, 1, :], S[:, 1, T - 1, 0:AW], start=False, stop=True).then_inc(oh_ps, 1)
            pe.wait_ge(w_ok, 1)
            nc.tensor.transpose(psX[0:NT, 0:P], wcol[:, :], ident[0:P, 0:P]).then_inc(w_t, 1)
            pe.wait_ge(w_row, 1)
            pe.wait_ge(s_const, 16 * CONSTS)
            pe.wait_ge(s_w1, LAYERS * 16 + 16)
            pe.wait_ge(s_w2, LAYERS * 32 + 16)
            ffn(w_f, f_y, 0, LAYERS * 2 * NT, True)


INS = ["x", "src", "dst", "L0_gnn_Wq", "L0_gnn_bq", "L0_gnn_Wk", "L0_gnn_bk", "L0_gnn_Wv", "L0_gnn_bv", "L0_gnn_Wskip", "L0_gnn_bskip",
       "L0_gnn_gamma", "L0_gnn_beta", "L0_mix_Wq", "L0_mix_Wk", "L0_mix_Wv", "L0_mix_Wo", "L0_mix_bo", "L0_mix_ln1_g", "L0_mix_ln1_b",
       "L0_mix_W1", "L0_mix_b1", "L0_mix_W2", "L0_mix_b2", "L0_mix_ln2_g", "L0_mix_ln2_b", "L0_ffn_wr", "L0_ffn_br", "L0_ffn_w1",
       "L0_ffn_b1", "L0_ffn_w2", "L0_ffn_b2"]


def kernel(**inputs):
    import numpy as np
    import concourse.bacc as bacc
    from concourse.bass_utils import run_bass_kernel_spmd

    nc = bacc.Bacc("TRN2", target_bir_lowering=False, num_devices=1)
    arrays, aps = {}, {}
    for name in INS:
        a = np.ascontiguousarray(inputs[name])
        arrays["in_" + name] = a
        aps[name] = nc.dram_tensor("in_" + name, a.shape, mybir.dt.from_np(a.dtype), kind="ExternalInput").ap()
    out = nc.dram_tensor("out", [N, HID], F32, kind="ExternalOutput").ap()
    gps_kernel(nc, aps, out)
    r = run_bass_kernel_spmd(nc, [arrays], core_ids=[0])
    return r.results[0]["out"]
```

```python
import concourse.bass as bass
from concourse import mybir
from contextlib import ExitStack

F32 = mybir.dt.float32
I32 = mybir.dt.int32
ALU = mybir.AluOpType
ACT = mybir.ActivationFunctionType
AX = mybir.AxisListType

N, E, HID, HEADS, LAYERS, FF = 3125, 50000, 256, 8, 4, 1024
DH = HID // HEADS
P = 125
NT = N // P
G = 5
NG = NT // G
C = HID // 128
KC = FF // 128
EPP = E // P
T = 5
NB = EPP // T
VW = DH + 1
AW = HEADS * VW
TW = AW + HEADS
W7 = T + 2
KVW = HID + AW
NO_RUN = E
BIG = 1e30
EPS = 1e-5
GNN_SCALE = float(DH) ** -0.5
MIX_SCALE = float(DH) ** -0.25
CONSTS = 4 + 3
KEPT = max(1, int(0.5 * N)) - 1
RSQRT_SEED = float(0x5F3759DF)


class Order:

    def __init__(self, engine, sem):
        self.engine, self.sem, self.base, self.n = engine, sem, 0, 0

    def mark(self, instruction):
        self.n += 1
        instruction.then_inc(self.sem, 1)
        return self.n

    def need(self, n):
        self.engine.wait_ge(self.sem, self.base + n)

    def link(self, instruction):
        self.need(self.mark(instruction))


def gps_kernel(nc, A, out):
    ctx = ExitStack()
    with ctx:
        def sb(name, shape, dt=F32):
            return ctx.enter_context(nc.sbuf_tensor(name, shape, dt))

        def sem(name):
            return ctx.enter_context(nc.semaphore(name))

        def dram(name, shape):
            return nc.dram_tensor(name, shape, F32, kind="Internal").ap()

        kv_tab = dram("kv_tab", [N, KVW])
        q_tab = dram("q_tab", [N, HID])
        log = dram("log", [E + 2, TW])
        dst_tab = dram("dst_tab", [P, EPP])
        skip_d = dram("skip_d", [N, HID])
        xn_d = dram("xn_d", [N, HID])
        w_d = dram("w_d", [P, NT])

        xm = sb("xm", [P, NT, HID])
        qe = sb("qe", [P, NT, HID])
        kst = sb("kst", [P, NT, HID])
        vst = sb("vst", [P, NT, AW])
        vmix = vst[:, :, :].rearrange("p n (c f) -> p n c f", c=C)
        vgnn = vst[:, :, :].rearrange("p n (h f) -> p n h f", h=HEADS)
        KV = sb("KV", [P, 2, T, KVW])
        QWB = sb("QWB", [P, N])
        ring = QWB[:, 0:G * HID].rearrange("p (j f) -> p j f", j=G)
        Q = QWB[:, 0:2 * T * HID].rearrange("p (k t f) -> p k t f", k=2, t=T)
        S = sb("S", [P, 2, T, TW])
        L7 = sb("L7", [P, 2, HEADS * W7])
        F7 = sb("F7", [P, HEADS * W7])
        M7 = sb("M7", [P, 2, HEADS * W7])
        E7 = sb("E7", [P, 2, HEADS * W7])
        P7 = sb("P7", [P, HEADS * W7 + 1])
        src_i = sb("src_i", [P, EPP], I32)
        dst_i = sb("dst_i", [P, EPP], I32)
        part_ring = sb("part_ring", [P, G], I32)
        part_i = sb("part_i", [P, NT], I32)
        end_i = sb("end_i", [P, NT + 1], I32)
        node = sb("node", [P, NT])
        part_f = sb("part_f", [P, NT])
        firsts = sb("firsts", [P, NT])
        upto = sb("upto", [P, NT])
        own = sb("own", [P, NT])
        end_f = sb("end_f", [P, NT + 1])
        run1 = sb("run1", [P, 1])
        same = sb("same", [P, EPP])
        sm = sb("sm", [P, 2, T])
        idx = sb("idx", [P, 2, 2, T], I32)
        xh = sb("xh", [P, G, HID])
        dst_x = xh[:, :, :].rearrange("p j f -> p (j f)")[:, 0:EPP + 1]
        dst_f = dst_x[:, 1:EPP + 1]
        ends = sb("ends", [P, 2])
        hT = sb("hT", [128, 3, C, P])
        ek = xh
        hg = sb("hg", [128, 2, KC, P])
        w_big = sb("w_big", [128, C, FF])
        w_down = sb("w_down", [128, KC, HID])
        w_qkv = sb("w_qkv", [128, C, 3 * HID])
        w_o = sb("w_o", [128, C, HID])
        m_sb = sb("m_sb", [128, C, HID])
        ln1 = sb("ln1", [128, 2, LAYERS, C])
        ln2 = sb("ln2", [128, 2, LAYERS, C])
        b1_mix = sb("b1_mix", [128, LAYERS, KC])
        cur = sb("cur", [128, 4, C])
        cur_b1 = sb("cur_b1", [128, KC])
        b1_ffn = sb("b1_ffn", [128, KC])
        b2_b = sb("b2_b", [P, HID])
        bo_b = sb("bo_b", [DH, HID])
        br_b = sb("br_b", [P, 1])
        vecs = w_qkv[0:P, 0, :].rearrange("p (i f) -> p i f", i=3)
        gnn_b = hg[0:P, :, :, :].rearrange("p a k n -> p (a k n)")[:, 0:4 * HID]
        onehots = hg[0:P, :, :, :].rearrange("p a k n -> p (a k n)")[:, 0:10 * P].rearrange("p (j s n) -> p j s n", j=G, s=2)
        ident = sb("ident", [128, 128])
        ones = sb("ones", [128, 128])
        zeros = sb("zeros", [128, 129])
        iota_tile = sb("iota_tile", [P, NT])
        part_base = sb("part_base", [P, 1])
        bst = sb("bst", [P, G, 6])
        mv = sb("mv", [P, NT, 2])
        mvs = sb("mvs", [P, G, 2])
        rstd = sb("rstd", [P, NT])
        nmr = sb("nmr", [P, NT])
        nr_v = sb("nr_v", [P, NT])
        nr_i = sb("nr_i", [P, NT], I32)
        nr_t = sb("nr_t", [P, NT])
        kmx = sb("kmx", [P, HID])
        kmx_b = sb("kmx_b", [P, HID])
        iota_row, lower = kmx[:, 0:P], kmx[:, P:2 * P]
        km = sb("km", [128, C])
        s40 = sb("s40", [P, G * HEADS])
        mx8 = s40[:, :].rearrange("p (j h) -> p j h", j=G)
        qsum = sb("qsum", [P, NT * HEADS])
        rS = sb("rS", [128, C])
        BD = sb("BD", [128, C, 128])
        BDT = sb("BDT", [128, C, 128])
        dg = BDT
        hd = sb("hd", [P, TW])
        carried = hd[:, 0:AW]
        keys = sb("keys", [P, 4, HEADS])
        K2, V2 = w_o[0:HEADS, 0, 0:2 * P], w_o[0:HEADS, 1, 0:2 * P]
        F2, M2 = m_sb[0:HEADS, 0, 0:2 * P], m_sb[0:HEADS, 1, 0:2 * P]
        pen2 = BDT[0:HEADS, :, :].rearrange("h c n -> h (c n)")[:, 0:2 * P + 1]
        fac = sb("fac", [P, 2, HEADS])
        key_tile = sb("key_tile", [P, 2, NT])
        wcol = s40[:, 0:NT]
        cnt = BDT[0:P, :, :].rearrange("p c n -> p (c n)")[:, 0:3 * NT].rearrange("p (s n) -> p s n", s=3)
        kv_flat = KV[:, :, :, :].rearrange("p a t f -> p (a t f)")
        first_row = QWB[:, G * HID:G * HID + P]
        compared = kv_flat[:, 0:N].rearrange("p (n q) -> p n q", n=NT)
        dst_rows = kv_flat[:, 0:G * EPP].rearrange("p (j t) -> p j t", j=G)
        dst_junk = kv_flat[:, G * EPP:(G + 1) * EPP]
        fl = kv_flat[:, 0:G * TW].rearrange("p (j f) -> p j f", j=G)
        agg = QWB[:, 0:G * AW]
        mean = QWB[:, G * AW:G * AW + G * HID]
        dots = mean.rearrange("p (j f) -> p j f", j=G)
        junk = KV[:, :, :, :].rearrange("p a t f -> p (a t f)")[:, 0:N]

        bank = [ctx.enter_context(nc.psum_tensor(f"bank{i}", [128, 512], F32)) for i in range(8)]

        def psT(j):
            return bank[j % 2][:, 0:C * P].rearrange("p (c n) -> p c n", c=C)

        def psQ(j):
            return bank[2 + j % 2][0:P, 0:HID]

        def psKV(j):
            return bank[4 + j % 2][0:P, :]

        def psQK(j):
            return bank[2 + j % 2][0:P, :]

        def psVS(j):
            return bank[4 + j % 2][0:P, :]

        def psY(j):
            return bank[6 + j % 2][0:P, 0:HID]

        def psH(j, half):
            return bank[2 + 2 * (j % 2) + half][:, 0:4 * P].rearrange("p (k n) -> p k n", k=4)

        def psC(c):
            return bank[2 + c][:, 0:129]

        def psB(j):
            return bank[2 + j % 2][0:P, 0:AW]

        psX, psM = bank[7], bank[4]

        s_x, s_dst, s_idx, s_wg, s_const = [sem(f"x_loaded{g}") for g in range(NG)], sem("destinations_loaded"), sem("sources_loaded"), sem("gnn_weights_loaded"), sem("constants_loaded")
        s_wqkv, s_wo, s_w1, s_w2 = sem("wqkv_loaded"), sem("wo_loaded"), sem("w1_loaded"), sem("w2_loaded")
        s_vec, s_b2 = sem("last_vectors_loaded"), sem("last_bias_loaded")
        gn = sem("made_constants")
        waited = sem("waited")
        xh_ready, pt_done, hT_ready = sem("xh_ready"), sem("transposed_plus_5"), sem("hT_ready_plus_2")
        xh_copied = sem("xh_copied_plus_5")
        gp_done, gp_free, gp_stored = sem("gnn_products_done"), sem("gnn_products_read_plus_2"), sem("gnn_rows_stored_plus_1")
        skip_st = [sem(f"skips_stored{i}_plus_1") for i in range(2)]
        mix_start = sem("value_ones_set")
        d_f, d_st, d_b, d_row = sem("destinations_ready"), sem("destinations_stored"), sem("firsts_spread"), sem("node_partitions_ready")
        d_in, d_used, d_ok = [sem(f"destinations_gathered{j}") for j in range(G)], sem("destinations_used_plus_5"), sem("run_ends_ready")
        e_prep, e_gath, e_logits_used, e_used, e_logit, e_exp, e_state, e_scat, e_idx = (
            sem("edge_tables_ready"), [sem(f"gathered{k}") for k in range(2)],
            sem("queries_used_plus_2"), sem("keys_and_values_used_plus_2"),
            sem("logits_ready"), sem("weights_ready"), sem("sums_ready"), [sem(f"scattered{k}_plus_16") for k in range(2)],
            sem("indices_copied"))
        qk_done, qk_act, qsub, qexp = (sem("qkv_done"), sem("qkv_read_by_act_plus_2"),
                                       sem("q_shifted_plus_2"), sem("q_exponentiated"))
        km_col, km_t, km_dg, km_b, km_ok = sem("kmax_columns"), sem("kmax_transposed"), sem("kmax_diagonal"), sem("kmax_spread"), sem("kmax_read")
        kd, ek_ok, ek_used = sem("k_shifted"), sem("k_exponentiated"), sem("ek_used_plus_5")
        ctx_done, bd_ok, bdt, bdt_ok, m_done, m_ok = (sem("context_done_plus_1"), sem("context_scaled"), sem("context_transposed"),
                                                      sem("contextT_read"), sem("M_done"), sem("M_read_plus_1"))
        at_done, at_free = sem("attention_done"), sem("attention_read_plus_2")
        q_ok = sem("query_sums_ready")
        ln1_ok, ln2_ok, b2_ok = sem("layer_norm_1_ready_by_group"), sem("layer_norm_2_ready"), sem("b2_added")
        h_done, hg_ok, y_done, y_free = sem("hidden_done"), sem("gelu_done_plus_1"), sem("ffn_done"), sem("ffn_read_plus_2")
        hd_in, hd_used = sem("first_runs_loaded"), sem("boundary_ready")
        b_t, b_k, b_m, b_f, b_d, b_e = sem("keys_transposed"), sem("keys_ready"), sem("maxima_found"), sem("maxima_transposed"), sem("factor_logits_ready"), sem("factors_ready")
        x_in, xn_in, skip_in = sem("x_reloaded"), sem("normalised_x_reloaded"), sem("skips_reloaded")
        f_run = [sem(f"runs_gathered{j}") for j in range(G)]
        f_used, oh_ok, oh_ps = sem("runs_summed_plus_5"), sem("onehots_ready"), sem("boundary_sums")
        f_pre, f_gelu, f_xmx = sem("gnn_out_ready_plus_1"), sem("gnn_gelu_done"), sem("residuals_added")
        y_norm, y_normed, x1_norm = sem("gnn_layer_norm_ready"), sem("gnn_rows_normalised"), sem("x1_layer_norm_ready")
        xx_ok, yb_ok = sem("x1_used"), sem("ffn_bias_added")
        xh_all = sem("x1_rows_normalised")
        w_ok, w_st, w_b = sem("w_ready"), sem("w_stored"), sem("w_spread")
        f_y, o_ok, o_st = sem("ffn_rows_ready"), sem("out_ready"), sem("out_stored")
        dve_order, act_order, pool_order = sem("dve_order"), sem("act_order"), sem("pool_order")

        x_v = A["x"].rearrange("(n p) f -> p n f", p=P)
        out_v = out.rearrange("(n p) f -> p n f", p=P)
        kv_v = kv_tab.rearrange("(n p) f -> p n f", p=P)
        q_v = q_tab.rearrange("(n p) f -> p n f", p=P)
        skip_v = skip_d.rearrange("(n p) f -> p n f", p=P)
        xn_v = xn_d.rearrange("(n p) f -> p n f", p=P)
        log_v = log[0:E, :].rearrange("(p t) f -> p t f", p=P)

        def row(v):
            return v.rearrange("(a n) -> a n", a=1)

        PER_LAYER = 3 * NT

        def w_a(L, i):
            return L * PER_LAYER + i + NT

        def w_c1(L, i):
            return L * PER_LAYER + i + 2 * NT

        def w_c2(L, i):
            return L * PER_LAYER + i + 3 * NT

        def w_f(i):
            return i + NT + LAYERS * PER_LAYER

        def settle(engine):
            engine.sem_inc(waited, 1)

        def groups(engine, body):
            with engine.Fori(0, NG - 1) as g:
                body(g, False)
            body(NG - 1, True)

        block = ctx.enter_context(nc.Block())

        @block.sync
        def _(sp):
            sp.dma_start(dst_i[:, :], A["dst"].rearrange("(p t) -> p t", p=P)).then_inc(s_dst, 16)
            for g in range(NG):
                sp.dma_start(xm[:, g * G:(g + 1) * G, :], x_v[:, g * G:(g + 1) * G, :]).then_inc(s_x[g], 16)
            for i, w in enumerate(("L0_gnn_Wq", "L0_gnn_Wk", "L0_gnn_Wv", "L0_gnn_Wskip")):
                sp.dma_start(w_big[:, :, i * HID:(i + 1) * HID], A[w].rearrange("(c k) n -> k c n", k=128)).then_inc(s_wg, 16)
            for i, b in enumerate(("L0_gnn_bq", "L0_gnn_bk", "L0_gnn_bv", "L0_gnn_bskip")):
                sp.dma_start(gnn_b[:, i * HID:(i + 1) * HID], row(A[b]).to_broadcast([P, HID])).then_inc(s_wg, 16)
            sp.dma_start(src_i[:, :], A["src"].rearrange("(p t) -> p t", p=P)).then_inc(s_idx, 16)
            sp.wait_ge(d_f, 1)
            sp.dma_start(dst_tab, dst_f[:, :]).then_inc(d_st, 16)
            for t, (g_, b_) in ((ln1, ("L0_mix_ln1_g", "L0_mix_ln1_b")), (ln2, ("L0_mix_ln2_g", "L0_mix_ln2_b"))):
                for i, v in enumerate((g_, b_)):
                    sp.dma_start(t[:, i, :, :], A[v].rearrange("l (c k) -> k l c", k=128), allow_slow_non_contiguous=True).then_inc(s_const, 16)
            sp.dma_start(b1_mix[:, :, :], A["L0_mix_b1"].rearrange("l (c k) -> k l c", k=128), allow_slow_non_contiguous=True).then_inc(s_const, 16)
            sp.dma_start(b1_ffn[:, :], A["L0_ffn_b1"].rearrange("(c k) -> k c", k=128), allow_slow_non_contiguous=True).then_inc(s_const, 16)
            sp.dma_start(br_b[:, :], row(A["L0_ffn_br"]).to_broadcast([P, 1])).then_inc(s_const, 16)
            def projection_weights(L):
                for i, w in enumerate(("L0_mix_Wq", "L0_mix_Wk", "L0_mix_Wv")):
                    sp.dma_start(w_qkv[:, :, i * HID:(i + 1) * HID], A[w][bass.ds(L, 1), :, :].rearrange("l (c k) n -> k (l c) n", k=128)).then_inc(s_wqkv, 16)

            def output_weights(L):
                sp.dma_start(w_o[:, :, :], A["L0_mix_Wo"][bass.ds(L, 1), :, :].rearrange("l (c k) n -> k (l c) n", k=128)).then_inc(s_wo, 16)
                sp.dma_start(bo_b[:, :], A["L0_mix_bo"][bass.ds(L, 1), :].to_broadcast([DH, HID])).then_inc(s_wo, 16)

            projection_weights(0)
            output_weights(0)
            with sp.Fori(0, NG) as g:
                sp.wait_ge(gp_free, g * G + 2 + 2)
                settle(sp)
                sp.dma_start(skip_v[:, bass.ds(g * G, 2), :], ring[:, 0:2, :]).then_inc(skip_st[0], 16)
                sp.wait_ge(gp_free, g * G + G + 2)
                settle(sp)
                sp.wait_ge(xh_copied, g * G + G + G)
                settle(sp)
                sp.dma_start(skip_v[:, bass.ds(g * G + 2, G - 2), :], ring[:, 2:G, :]).then_inc(skip_st[1], 16)
                sp.dma_start(q_v[:, bass.ds(g * G, G), :], qe[:, bass.ds(g * G, G), :]).then_inc(gp_stored, 16)
                sp.dma_start(kv_v[:, bass.ds(g * G, G), 0:HID], kst[:, bass.ds(g * G, G), :]).then_inc(gp_stored, 16)
                sp.dma_start(kv_v[:, bass.ds(g * G, G), HID:KVW], vst[:, bass.ds(g * G, G), :]).then_inc(gp_stored, 16)
                sp.dma_start(xn_v[:, bass.ds(g * G, G), :], xm[:, bass.ds(g * G, G), :]).then_inc(gp_stored, 16)
            def ffn_weights(L):
                sp.wait_ge(gp_done, NT)
                sp.wait_ge(y_free, L * NT + 2)
                sp.dma_start(w_big[:, :, :], A["L0_mix_W1"][bass.ds(L, 1), :, :].rearrange("l (c k) n -> k (l c) n", k=128)).then_inc(s_w1, 16)
                sp.dma_start(w_down[:, :, :], A["L0_mix_W2"][bass.ds(L, 1), :, :].rearrange("l (c k) n -> k (l c) n", k=128)).then_inc(s_w2, 16)
                sp.dma_start(b2_b[:, :], A["L0_mix_b2"][bass.ds(L, 1), :].to_broadcast([P, HID])).then_inc(s_w2, 16)

            with sp.Fori(0, LAYERS - 1) as L:
                ffn_weights(L)
                sp.wait_ge(ctx_done, L + 2)
                projection_weights(L + 1)
                sp.wait_ge(m_ok, L + 2)
                output_weights(L + 1)
            ffn_weights(LAYERS - 1)
            sp.wait_ge(ctx_done, LAYERS + 1)
            for i, v in enumerate(("L0_gnn_gamma", "L0_gnn_beta")):
                sp.dma_start(vecs[:, i, :], row(A[v]).to_broadcast([P, HID])).then_inc(s_vec, 16)
            sp.dma_start(vecs[:, 2, :], A["L0_ffn_wr"].rearrange("n a -> a n").to_broadcast([P, HID])).then_inc(s_vec, 16)
            for i in range(2):
                sp.wait_ge(skip_st[i], 16 * NG + 1)
            sp.dma_start(kst[:, :, :], xn_v).then_inc(xn_in, 16)
            sp.dma_start(vst[:, :, 0:HID], skip_v).then_inc(skip_in, 16)
            sp.wait_ge(at_free, LAYERS * NT + 2)
            sp.dma_start(qe[:, :, :], x_v).then_inc(x_in, 16)
            sp.wait_ge(y_free, LAYERS * NT + 2)
            sp.dma_start(w_big[:, :, :], A["L0_ffn_w1"].rearrange("(c k) n -> k c n", k=128)).then_inc(s_w1, 16)
            sp.dma_start(w_down[:, :, :], A["L0_ffn_w2"].rearrange("(c k) n -> k c n", k=128)).then_inc(s_w2, 16)
            sp.dma_start(b2_b[:, :], row(A["L0_ffn_b2"]).to_broadcast([P, HID])).then_inc(s_b2, 16)
            sp.wait_ge(w_ok, 1)
            sp.dma_start(w_d, wcol[:, :]).then_inc(w_st, 16)
            sp.wait_ge(w_st, 16)
            sp.dma_start(QWB[:, :], w_d.rearrange("p n -> (p n)").rearrange("(a f) -> a f", a=1).to_broadcast([P, N])).then_inc(w_b, 16)
            with sp.Fori(0, NG) as g:
                sp.wait_ge(o_ok, g + 1)
                sp.dma_start(out_v[:, bass.ds(g * G, G), :], vst[:, bass.ds(g * G, G), 0:HID]).then_inc(o_st, 16)
            sp.wait_ge(o_st, 16 * NG)

        @block.gpsimd
        def _(gp):
            order = Order(gp, pool_order)
            gp.memset(ident[:, :], 0.0).then_inc(gn, 1)
            gp.memset(ones[:, :], 1.0).then_inc(gn, 1)
            gp.memset(zeros[:, :], 0.0)
            gp.memset(hd[:, 0:AW], 0.0).then_inc(gn, 1)
            gp.memset(hd[:, AW:TW], -BIG).then_inc(gn, 1)
            gp.wait_ge(gn, 4)
            gp.iota(iota_tile[:, :], pattern=[[P, NT]], base=0, channel_multiplier=0, allow_small_or_imprecise_dtypes=True).then_inc(gn, 1)
            gp.iota(part_base[:, :], pattern=[[0, 1]], base=0, channel_multiplier=EPP, allow_small_or_imprecise_dtypes=True).then_inc(gn, 1)
            gp.iota(node[:, :], pattern=[[P, NT]], base=0, channel_multiplier=1, allow_small_or_imprecise_dtypes=True).then_inc(gn, 1)
            gp.affine_select(out=ident[:, :], in_=ident[:, :], compare_op=ALU.not_equal, fill=1.0, base=0,
                             pattern=[[-1, 128]], channel_multiplier=1).then_inc(gn, 1)

            def gather(b, k, between=None):
                gp.wait_ge(e_logits_used, b + 1)
                order.mark(gp.tensor_copy(idx[:, k, 0, :], src_i[:, bass.ds(b * T, T)]))
                order.link(gp.tensor_copy(idx[:, k, 1, :], dst_i[:, bass.ds(b * T, T)]))
                settle(gp)
                for t in range(T):
                    gp.indirect_dma_start(out=Q[:, k, t, :], out_offset=None, in_=q_tab,
                                          in_offset=bass.IndirectOffsetOnAxis(ap=idx[:, k, 1, t:t + 1], axis=0)).then_inc(e_gath[k], 16)
                if between:
                    between()
                gp.wait_ge(e_used, b + 1)
                settle(gp)
                for t in range(T):
                    gp.indirect_dma_start(out=KV[:, k, t, :], out_offset=None, in_=kv_tab,
                                          in_offset=bass.IndirectOffsetOnAxis(ap=idx[:, k, 0, t:t + 1], axis=0)).then_inc(e_gath[k], 16)

            def store(b, k):
                gp.wait_ge(e_state, b + 1)
                settle(gp)
                gp.dma_start(log_v[:, bass.ds(b * T, T), :], S[:, k, :, :]).then_inc(e_scat[k], 16)

            gp.wait_ge(d_st, 16)
            gp.wait_ge(d_row, 1)
            order.link(gp.tensor_copy(part_ring[:, :], part_i[:, 0:G]))

            def destinations(g, last):
                for j in range(G):
                    gp.wait_ge(d_used, g * G + j + 1)
                    settle(gp)
                    gp.indirect_dma_start(out=dst_rows[:, j, :], out_offset=None, in_=dst_tab,
                                          in_offset=bass.IndirectOffsetOnAxis(ap=part_ring[:, j:j + 1], axis=0)).then_inc(d_in[j], 16)
                if not last:
                    for j in range(G):
                        gp.wait_ge(d_in[j], g * 16 + 16)
                        settle(gp)
                    order.base, order.n = g + 1, 0
                    order.link(gp.tensor_copy(part_ring[:, :], part_i[:, bass.ds((g + 1) * G, G)]))
                    settle(gp)

            groups(gp, destinations)
            order.base, order.n = 0, NG
            for k in range(2):
                gp.dma_start(log[E + k:E + k + 1, :], hd[k:k + 1, :]).then_inc(e_scat[k], 16)
            gp.wait_ge(e_prep, 1)
            gp.wait_ge(gp_stored, 4 * 16 * NG + 1)
            gp.memset(vmix[:, :, :, 128:129], 1.0).then_inc(mix_start, 1)
            gp.wait_ge(d_used, NT + G)
            gp.wait_ge(s_idx, 16)
            gather(0, 0)
            gather(1, 1)
            PER = 2 * 2
            start = order.n

            def turn(r, more=True, between=None):
                order.base, order.n = start + r * PER, 0
                for k in range(2):
                    if more:
                        gather(2 * r + 2 + k, k, between if k == 0 else None)
                    store(2 * r + k, k)

            def bias(L, g):
                gp.wait_ge(xh_ready, w_c2(L, g * G + G - 1) + 1)
                settle(gp)
                for j in range(G):
                    ins = gp.tensor_tensor(xm[:, g * G + j, :], xm[:, g * G + j, :], b2_b[:, :], ALU.add)
                ins.then_inc(b2_ok, 1)

            def layer(L, more):
                with gp.Fori(0, NG) as g:
                    turn(L * (2 * NG) + g)
                gp.wait_ge(q_ok, L + 1)
                settle(gp)
                gp.wait_ge(ctx_done, L + 2)
                settle(gp)
                with gp.Fori(0, NG) as g:
                    for j in range(G):
                        i = g * G + j
                        gp.wait_ge(pt_done, w_c1(L, i) + 1)
                        settle(gp)
                        gp.tensor_tensor(xh[:, j, :].rearrange("p (h d) -> p h d", d=DH), qe[:, i, :].rearrange("p (h d) -> p h d", d=DH),
                                         qsum[:, bass.ds(i * HEADS, HEADS)].unsqueeze(2).to_broadcast([P, HEADS, DH]), ALU.mult).then_inc(xh_ready, 1)
                gp.wait_ge(s_w2, L * 32 + 32)
                settle(gp)
                bias(L, 0)
                settle(gp)
                with gp.Fori(0, NG - 1) as g:
                    turn(L * (2 * NG) + NG + g, between=lambda: bias(L, g + 1))
                turn(L * (2 * NG) + 2 * NG - 1, more)

            with gp.Fori(0, LAYERS - 1) as L:
                layer(L, True)
            layer(LAYERS - 1, False)
            order.base, order.n = 0, start + (NB // 2 - 1) * PER
            gp.wait_ge(ctx_done, LAYERS + 1)
            gp.iota(iota_row[:, :], pattern=[[1, P]], base=0, channel_multiplier=0, allow_small_or_imprecise_dtypes=True).then_inc(gn, 1)
            gp.affine_select(out=lower[:, :], in_=ones[0:P, 0:P], compare_op=ALU.is_gt, fill=0.0, base=0,
                             pattern=[[-1, P]], channel_multiplier=1).then_inc(gn, 1)
            for k in range(2):
                gp.wait_ge(e_scat[k], 16 + 16 * (NB // 2))
            gp.wait_ge(d_ok, 1)
            gp.wait_ge(e_state, NB)
            gp.indirect_dma_start(out=hd[:, :], out_offset=None, in_=log,
                                  in_offset=bass.IndirectOffsetOnAxis(ap=end_i[:, NT:NT + 1], axis=0)).then_inc(hd_in, 16)
            base = order.n
            gp.wait_ge(x_in, 16)
            gp.wait_ge(s_vec, 3 * 16)
            gp.wait_ge(y_free, LAYERS * NT + 2)
            with gp.Fori(0, NG) as g:
                order.base, order.n = base + 2 * g, 0
                for j in range(G):
                    gp.wait_ge(f_used, g * G + j + 1)
                settle(gp)
                order.link(gp.tensor_copy(part_ring[:, :], end_i[:, bass.ds(g * G, G)]))
                settle(gp)
                for j in range(G):
                    gp.indirect_dma_start(out=fl[:, j, :], out_offset=None, in_=log,
                                          in_offset=bass.IndirectOffsetOnAxis(ap=part_ring[:, j:j + 1], axis=0)).then_inc(f_run[j], 16)
                rows = qe[:, bass.ds(g * G, G), :]
                order.link(gp.tensor_tensor(rows, rows, xm[:, bass.ds(g * G, G), :], ALU.add))
                settle(gp)
                gp.tensor_tensor(rows, rows, vecs[:, 1:2, :].to_broadcast([P, G, HID]), ALU.add).then_inc(f_xmx, 1)
            with gp.Fori(0, NG) as g:
                gp.wait_ge(xh_all, g + 1)
                settle(gp)
                gp.tensor_tensor(qe[:, bass.ds(g * G, G), :], vst[:, bass.ds(g * G, G), 0:HID], kst[:, bass.ds(g * G, G), 0:HID],
                                 ALU.add).then_inc(xx_ok, 1)
            gp.wait_ge(s_b2, 16)
            with gp.Fori(0, NG) as g:
                gp.wait_ge(f_y, g * G + G + 2)
                settle(gp)
                rows = vst[:, bass.ds(g * G, G), 0:HID]
                gp.tensor_tensor(rows, rows, b2_b[:, :].unsqueeze(1).to_broadcast([P, G, HID]), ALU.add).then_inc(yb_ok, 1)

        DONE = NG - 2

        @block.vector
        def _(v):
            order = Order(v, dve_order)
            link, mark, need = order.link, order.mark, order.need
            total = [0]

            def enter(register, per):
                order.base, order.n = total[0] + register * per, 0

            def leave(turns, per):
                assert order.n == per, (order.n, per)
                total[0] += turns * per
                order.base, order.n = 0, total[0]

            def straight():
                total[0] = order.n

            def inv_std(n0, n):
                a, y, t = nr_v[:, 0:n], nr_i[:, 0:n].bitcast(F32), nr_t[:, 0:n]
                link(nc.vector.tensor_scalar(a, mv[:, bass.ds(n0, n), 1], EPS, None, ALU.add))
                link(nc.vector.tensor_scalar(nr_i[:, 0:n], nr_v[:, 0:n].bitcast(I32), -0.5, RSQRT_SEED, ALU.mult, ALU.add))
                for step in range(3):
                    link(nc.vector.tensor_tensor(t, y, y, ALU.mult))
                    link(nc.vector.tensor_tensor(t, t, a, ALU.mult))
                    link(nc.vector.tensor_scalar(t, t, -0.5, 1.5, ALU.mult, ALU.add))
                    link(nc.vector.tensor_tensor(rstd[:, bass.ds(n0, n)] if step == 2 else y, y, t, ALU.mult))
                link(nc.vector.scalar_tensor_tensor(out=nmr[:, bass.ds(n0, n)], in0=mv[:, bass.ds(n0, n), 0], scalar=-1.0,
                                                    in1=rstd[:, bass.ds(n0, n)], op0=ALU.mult, op1=ALU.mult))

            INV = 15

            v.sem_inc(pt_done, G)
            v.sem_inc(xh_copied, G)
            v.sem_inc(d_used, G)
            for s in (gp_stored, *skip_st, hg_ok, ctx_done, m_ok, f_pre):
                v.sem_inc(s, 1)
            v.sem_inc(hT_ready, 2)
            v.sem_inc(gp_free, 2)
            v.sem_inc(e_used, 2)
            v.sem_inc(e_logits_used, 2)
            v.sem_inc(qsub, 2)
            v.sem_inc(f_y, 2)
            v.sem_inc(qk_act, 2)
            v.sem_inc(ek_used, G)
            v.sem_inc(at_free, 2)
            v.sem_inc(y_free, 2)
            v.sem_inc(f_used, G)

            v.wait_ge(s_dst, 16)
            v.wait_ge(gn, 8)
            link(nc.vector.tensor_copy(dst_f[:, :], dst_i[:, :]))
            link(nc.vector.memset(dst_x[:, 0:1], -1.0))
            link(nc.vector.tensor_tensor(same[:, :], dst_f[:, :], dst_x[:, 0:EPP], ALU.is_equal))
            mark(nc.vector.tensor_copy(ends[:, 0:1], dst_f[:, 0:1]))
            link(nc.vector.tensor_copy(ends[:, 1:2], dst_f[:, EPP - 1:EPP]))
            v.sem_inc(d_f, 1)
            link(nc.vector.tensor_scalar(dst_junk[:, :], dst_f[:, :], ends[:, 0:1], 0.0, ALU.is_equal, ALU.add, accum_out=run1[:, 0:1]))
            link(nc.vector.tensor_scalar(end_f[:, NT:NT + 1], run1[:, :], part_base[:, 0:1], -1.0 - NO_RUN, ALU.add, ALU.add))
            link(nc.vector.scalar_tensor_tensor(out=end_f[:, NT:NT + 1], in0=run1[:, :], scalar=EPP - 0.5, in1=end_f[:, NT:NT + 1],
                                                op0=ALU.is_lt, op1=ALU.mult))
            straight()


            def aggregate(g):
                settle(v)
                for j in range(G):
                    n = mark(nc.vector.bn_aggr(mvs[:, j, :], bst[:, j, :]))
                need(n)
                settle(v)
                link(nc.vector.tensor_copy(mv[:, bass.ds(g * G, G), :], mvs[:, :, :]))

            def stats(g):
                for j in range(G):
                    n = mark(nc.vector.bn_stats(bst[:, j, :], xm[:, g * G + j, :]))
                need(n)
                aggregate(g)

            for g in range(NG):
                v.wait_ge(s_x[g], 16)
                stats(g)
            inv_std(0, NT)
            straight()
            v.wait_ge(d_st, 16)
            def rows_of_x(i, j):
                v.wait_ge(pt_done, i + 1)
                v.wait_ge(xh_copied, i + 1)
                nc.vector.tensor_scalar(xh[:, j, :], xm[:, i, :], mv[:, i, 0:1], rstd[:, bass.ds(i, 1)],
                                        ALU.subtract, ALU.mult).then_inc(xh_ready, 1)

            for j in range(G):
                rows_of_x(j, j)
            mark(nc.vector.memset(P7[:, :], -BIG))
            mark(nc.vector.memset(L7[:, :, :], -BIG))
            mark(nc.vector.memset(M7[:, :, :], -BIG))
            mark(nc.vector.memset(S[:, :, :, :], 0.0))
            mark(nc.vector.memset(BD[:, :, :], 0.0))
            mark(nc.vector.tensor_scalar(key_tile[:, 0, :], iota_tile[:, :], -1.0, ends[:, 0:1], ALU.mult, ALU.add))
            mark(nc.vector.tensor_scalar(key_tile[:, 1, :], iota_tile[:, :], -1.0, ends[:, 1:2], ALU.mult, ALU.add))
            link(nc.vector.memset(vgnn[:, :, :, DH:VW], 1.0))
            v.sem_inc(e_prep, 1)
            v.wait_ge(d_b, 1)
            link(nc.vector.tensor_copy(first_row[:, :], psX[0:P, 0:P]))
            for t, op in ((part_f, ALU.is_le), (firsts, ALU.is_equal)):
                link(nc.vector.tensor_tensor(compared[:, :, :], first_row[:, :].unsqueeze(1).to_broadcast([P, NT, P]),
                                             node[:, :].unsqueeze(2).to_broadcast([P, NT, P]), op))
                link(nc.vector.tensor_reduce(out=t[:, :], in_=compared[:, :, :], axis=AX.X, op=ALU.add))
            link(nc.vector.tensor_scalar(part_f[:, :], part_f[:, :], -1.0, None, ALU.add))
            link(nc.vector.tensor_scalar(upto[:, :], part_f[:, :], 0.0, None, ALU.max))
            link(nc.vector.tensor_copy(part_i[:, :], upto[:, :]))
            v.sem_inc(d_row, 1)
            straight()
            v.wait_ge(s_wg, 8 * 16)

            def gnn_group(g, last):
                enter(g, 2 * G)
                for j in range(G):
                    i = g * G + j
                    v.wait_ge(gp_done, i + 1)
                    nc.vector.tensor_tensor(qe[:, i, :], psQK(j)[:, 0:HID], gnn_b[:, 0:HID], ALU.add)
                    nc.vector.tensor_tensor(kst[:, i, :], psQK(j)[:, HID:2 * HID], gnn_b[:, HID:2 * HID], ALU.add)
                    nc.vector.tensor_tensor(vgnn[:, i, :, 0:DH], psVS(j)[:, 0:HID].rearrange("p (h d) -> p h d", d=DH),
                                            gnn_b[:, 2 * HID:3 * HID].rearrange("p (h d) -> p h d", d=DH), ALU.add)
                    if j in (0, 2):
                        v.wait_ge(skip_st[j // 2], g * 16 + 1)
                    nc.vector.tensor_tensor(ring[:, j, :], psVS(j)[:, HID:2 * HID], gnn_b[:, 3 * HID:4 * HID], ALU.add).then_inc(gp_free, 1)
                    if not last:
                        rows_of_x(i + G, j)
                    v.wait_ge(d_in[j], g * 16 + 16)
                    if not last:
                        settle(v)
                    for t, op in ((upto, ALU.is_le), (own, ALU.is_equal)):
                        link(nc.vector.tensor_scalar(dst_junk[:, :], dst_rows[:, j, :], node[:, bass.ds(i, 1)], 0.0, op, ALU.add,
                                                     accum_out=t[:, bass.ds(i, 1)]))
                    v.sem_inc(d_used, 1)

            groups(v, gnn_group)
            leave(NG, 2 * G)
            v.wait_ge(xh_ready, NT)
            mark(nc.vector.memset(mv[:, :, 0], 0.0))
            link(nc.vector.tensor_tensor(mv[:, :, 1], mv[:, :, 1], rstd[:, :], ALU.mult))
            link(nc.vector.tensor_tensor(mv[:, :, 1], mv[:, :, 1], rstd[:, :], ALU.mult))
            straight()

            inv_std(0, NT)
            v.sem_inc(ln1_ok, NG)
            link(nc.vector.tensor_scalar(part_f[:, :], part_f[:, :], float(EPP), -1.0 - NO_RUN, ALU.mult, ALU.add))
            link(nc.vector.tensor_tensor(end_f[:, 0:NT], part_f[:, :], upto[:, :], ALU.add))
            for t, op in ((own, ALU.is_gt), (firsts, ALU.is_lt)):
                link(nc.vector.scalar_tensor_tensor(out=end_f[:, 0:NT], in0=t[:, :], scalar=0.5, in1=end_f[:, 0:NT], op0=op, op1=ALU.mult))
            link(nc.vector.tensor_scalar(end_f[:, :], end_f[:, :], float(NO_RUN), None, ALU.add))
            link(nc.vector.tensor_copy(end_i[:, :], end_f[:, :]))
            v.sem_inc(d_ok, 1)
            straight()

            def seven(t):
                return t.rearrange("p (h w) -> p h w", h=HEADS)

            def edge_logits(b, turn, k):
                prev = 1 - k
                link(nc.vector.tensor_copy(sm[:, k, :], same[:, bass.ds(b * T, T)]))
                mark(nc.vector.tensor_scalar(seven(P7[:, 0:HEADS * W7])[:, :, 1:1 + T],
                                                   sm[:, k, :].unsqueeze(1).to_broadcast([P, HEADS, T]),
                                                   -1.0, BIG, ALU.add, ALU.mult))
                mark(nc.vector.tensor_copy(seven(L7[:, k, :])[:, :, 0], seven(M7[:, prev, :])[:, :, T]))
                v.wait_ge(e_gath[k], turn * (2 * T * 16) + 2 * T * 16)
                link(nc.vector.tensor_tensor(Q[:, k, :, :], Q[:, k, :, :], KV[:, k, :, 0:HID], ALU.mult))
                link(nc.vector.tensor_reduce(out=seven(L7[:, k, :])[:, :, 1:1 + T].rearrange("p h t -> p t h"),
                                             in_=Q[:, k, :, :].rearrange("p t (h d) -> p t h d", d=DH), axis=AX.X, op=ALU.add))
                v.sem_inc(e_logits_used, 1)
                link(nc.vector.tensor_tensor_scan(F7[:, :], P7[:, 0:HEADS * W7], L7[:, k, :], initial=-BIG, op0=ALU.add, op1=ALU.max))
                link(nc.vector.tensor_tensor_scan(M7[:, k, ::-1], P7[:, 1:HEADS * W7 + 1][:, ::-1], F7[:, ::-1], initial=-BIG,
                                                  op0=ALU.add, op1=ALU.max))
                nc.vector.tensor_tensor(E7[:, k, :], L7[:, k, :], M7[:, k, :], ALU.subtract).then_inc(e_logit, 1)

            def edge_sums(b, turn, k):
                prev = 1 - k
                v.wait_ge(e_scat[k], turn * 16 + 16)
                v.wait_ge(e_exp, b + 1)
                w = seven(E7[:, k, :])
                mark(nc.vector.tensor_tensor(seven(carried[:, :]), seven(S[:, prev, T - 1, 0:AW]),
                                             w[:, :, 0:1].to_broadcast([P, HEADS, VW]), ALU.mult))
                mark(nc.vector.tensor_copy(S[:, k, :, AW:TW], seven(M7[:, k, :])[:, :, 1:1 + T].rearrange("p h t -> p t h")))
                n = mark(nc.vector.tensor_tensor(S[:, k, :, 0:AW].rearrange("p t (h w) -> p t h w", h=HEADS),
                                             KV[:, k, :, HID:KVW].rearrange("p t (h w) -> p t h w", h=HEADS),
                                             w[:, :, 1:1 + T].rearrange("p h t -> p t h").unsqueeze(3).to_broadcast([P, T, HEADS, VW]), ALU.mult))
                need(n)
                v.sem_inc(e_used, 1)
                for t in range(T):
                    before = carried[:, :] if t == 0 else S[:, k, t - 1, 0:AW]
                    link(nc.vector.scalar_tensor_tensor(out=S[:, k, t, 0:AW], in0=before, scalar=sm[:, k, t:t + 1],
                                                        in1=S[:, k, t, 0:AW], op0=ALU.mult, op1=ALU.add))
                v.sem_inc(e_state, 1)

            EDGE = 10 + T

            def edge_steps(turn):
                b = 2 * turn
                edge_logits(b, turn, 0)
                yield
                edge_sums(b, turn, 0)
                edge_logits(b + 1, turn, 1)
                yield
                edge_sums(b + 1, turn, 1)
                yield

            def residual(L, g, done, free, prepare=None):
                for j in range(G + 1):
                    i = g * G + j
                    if j < G:
                        v.wait_ge(done, L * NT + i + 1)
                        nc.vector.tensor_tensor(xm[:, i, :], psY(j), xm[:, i, :], ALU.add).then_inc(free, 1)
                        if prepare:
                            prepare(j)
                    if j:
                        v.wait_ge(free, L * NT + i - 1 + 3)
                        settle(v)
                        n = mark(nc.vector.bn_stats(bst[:, j - 1, :], xm[:, i - 1, :]))
                need(n)
                aggregate(g)

            def layer_a(L, g):
                edges = edge_steps(L * (2 * NG) + g)
                for j in range(G):
                    i = g * G + j
                    if j in (0, 2, 4):
                        next(edges)
                    ps = psQ(j).rearrange("p (h d) -> p h d", d=DH)
                    v.wait_ge(qk_done, L * NT + i + 1)
                    link(nc.vector.tensor_reduce(out=mx8[:, j, :], in_=ps, axis=AX.X, op=ALU.max))
                    nc.vector.tensor_tensor(qe[:, i, :].rearrange("p (h d) -> p h d", d=DH), ps,
                                            mx8[:, j, :].unsqueeze(2).to_broadcast([P, HEADS, DH]), ALU.subtract).then_inc(qsub, 1)
                    v.wait_ge(qk_act, L * NT + i + 3)
                    n = mark(nc.vector.tensor_tensor(kmx[:, :], kmx[:, :], kst[:, i, :], ALU.max))
                need(n)

            LA = 2 * G + 2 * EDGE
            assert NB == LAYERS * 2 * NG * 2

            with v.Fori(0, LAYERS) as L:
                LAYER = 1 + NG * LA + 4 + (NG + 1) + 12 + NG * (1 + 2 * G) + INV + NG * (1 + 2 * G + INV + 2 * EDGE)
                lbase = total[0] + L * LAYER
                used = [0]

                def part(register, per):
                    order.base, order.n = lbase + used[0] + register * per, 0

                def end_part(turns, per):
                    assert order.n == per, (order.n, per)
                    used[0] += turns * per

                part(0, 1)
                link(nc.vector.memset(kmx[:, :], -3e38))
                end_part(1, 1)
                settle(v)
                v.wait_ge(gp_stored, 4 * 16 * NG + 1)
                with v.Fori(0, NG) as g:
                    part(g, LA)
                    layer_a(L, g)
                end_part(NG, LA)
                part(0, 4)
                v.sem_inc(km_col, 1)
                v.wait_ge(km_t, L + 1)
                link(nc.vector.tensor_reduce(out=km[:, :], in_=psX[:, 0:C * P].rearrange("p (c n) -> p c n", c=C), axis=AX.X, op=ALU.max))
                for c in range(C):
                    link(nc.vector.tensor_scalar(dg[:, c, :], ident[:, :], km[:, c:c + 1], None, ALU.mult))
                v.sem_inc(km_dg, 1)
                v.wait_ge(km_b, L + 1)
                link(nc.vector.tensor_copy(kmx_b[:, :], psX[0:P, 256:512]))
                end_part(1, 4)
                v.wait_ge(qk_act, L * NT + NT + 2)
                settle(v)
                v.wait_ge(qexp, L * NT + NT)
                settle(v)
                with v.Fori(0, NG) as g:
                    part(g, 1)
                    for j in range(G):
                        v.wait_ge(ek_used, L * NT + g * G + j + 1)
                        nc.vector.tensor_tensor(ek[:, j, :], kst[:, g * G + j, :], kmx_b[:, :], ALU.subtract).then_inc(kd, 1)
                    mark(nc.vector.tensor_reduce(out=qsum[:, bass.ds(g * (G * HEADS), G * HEADS)],
                                                 in_=qe[:, bass.ds(g * G, G), :].rearrange("p j (h d) -> p (j h) d", d=DH),
                                                 axis=AX.X, op=ALU.add))
                end_part(NG, 1)
                part(0, 1)
                need(0)
                link(nc.vector.reciprocal(qsum[:, :], qsum[:, :]))
                end_part(1, 1)
                v.sem_inc(q_ok, 1)
                part(0, 12)
                v.wait_ge(ctx_done, L + 2)
                for c in range(C):
                    n = mark(nc.vector.reciprocal(rS[:, c:c + 1], psC(c)[:, 128:129]))
                need(n)
                for c in range(C):
                    for h in range(4):
                        r = slice(h * DH, h * DH + DH)
                        n = mark(nc.vector.tensor_scalar(BD[r, c, r], psC(c)[r, r], rS[r, c:c + 1], None, ALU.mult))
                need(n)
                v.sem_inc(bd_ok, 1)
                v.wait_ge(bdt, L + 1)
                nc.vector.tensor_copy(BDT[:, :, :], psX[:, 0:256].rearrange("p (c n) -> p c n", c=C)).then_inc(bdt_ok, 1)
                v.wait_ge(m_done, L + 1)
                link(nc.vector.tensor_copy(m_sb[:, :, :], psM[:, :].rearrange("p (c n) -> p c n", c=C)))
                link(nc.vector.tensor_tensor(m_sb[0:DH, 0, :], m_sb[0:DH, 0, :], bo_b[:, :], ALU.add))
                end_part(1, 12)
                v.sem_inc(m_ok, 1)
                PER = 1 + 2 * G
                with v.Fori(0, NG) as g:
                    part(g, PER)
                    residual(L, g, at_done, at_free)
                end_part(NG, PER)
                part(0, INV)
                inv_std(0, NT)
                v.sem_inc(ln2_ok, 1)
                end_part(1, INV)
                PER = 1 + 2 * G + INV + 2 * EDGE
                with v.Fori(0, NG) as g:
                    part(g, PER)
                    turn = L * (2 * NG) + NG + g
                    v.wait_ge(b2_ok, L * NG + g + 1)
                    settle(v)

                    def logits(j):
                        if j in (1, 3):
                            edge_logits(2 * turn + j // 2, turn, j // 2)

                    residual(L, g, y_done, y_free, logits)
                    inv_std(g * G, G)
                    v.sem_inc(ln1_ok, 1)
                    for k in range(2):
                        edge_sums(2 * turn + k, turn, k)
                end_part(NG, PER)
                assert used[0] == LAYER
            total[0] += LAYERS * LAYER
            order.base, order.n = 0, total[0]

            def node_onehots(g, j):
                for s in range(2):
                    n = mark(nc.vector.tensor_scalar(onehots[:, j, s, :], iota_row[:, :], key_tile[:, s, bass.ds(g * G + j, 1)], None, ALU.is_equal))
                need(n)
                v.sem_inc(oh_ok, 1)

            v.wait_ge(gn, 10)
            for j in range(G):
                node_onehots(0, j)
            v.wait_ge(hd_in, 16)
            last = S[:, 1, T - 1, :]
            mark(nc.vector.tensor_copy(keys[:, 0, :], hd[:, AW:TW]))
            mark(nc.vector.tensor_copy(keys[:, 1, :], last[:, AW:TW]))
            mark(nc.vector.tensor_copy(keys[:, 2, :], ends[:, 0:1].to_broadcast([P, HEADS])))
            link(nc.vector.tensor_copy(keys[:, 3, :], ends[:, 1:2].to_broadcast([P, HEADS])))
            v.sem_inc(b_k, 1)
            v.wait_ge(b_t, 1)
            for i, t in enumerate((V2, K2)):
                for s in range(2):
                    n = mark(nc.vector.tensor_copy(t[:, :].rearrange("h (p s) -> h s p", s=2)[:, s, :],
                                                   psX[0:HEADS, (2 * i + s) * 128:(2 * i + s) * 128 + P]))
            need(n)
            link(nc.vector.memset(pen2[:, :], -BIG))
            link(nc.vector.tensor_tensor(F2[:, 1:2 * P], K2[:, 1:2 * P], K2[:, 0:2 * P - 1], ALU.is_equal))
            link(nc.vector.tensor_scalar(pen2[:, 1:2 * P], F2[:, 1:2 * P], -1.0, BIG, ALU.add, ALU.mult))
            link(nc.vector.tensor_tensor_scan(F2[:, :], pen2[:, 0:2 * P], V2[:, :], initial=-BIG, op0=ALU.add, op1=ALU.max))
            link(nc.vector.tensor_tensor_scan(M2[:, ::-1], pen2[:, 1:2 * P + 1][:, ::-1], F2[:, ::-1], initial=-BIG, op0=ALU.add, op1=ALU.max))
            for s in range(2):
                n = mark(nc.vector.tensor_copy(F2[:, s * P:(s + 1) * P], M2[:, :].rearrange("h (p s) -> h s p", s=2)[:, s, :]))
            need(n)
            v.sem_inc(b_m, 1)
            v.wait_ge(b_f, 1)
            for s in range(2):
                n = mark(nc.vector.tensor_tensor(fac[:, s, :], keys[:, s, :], bank[6][0:P, s * HEADS:(s + 1) * HEADS], ALU.subtract))
            need(n)
            v.sem_inc(b_d, 1)
            v.wait_ge(b_e, 1)
            for s, t in enumerate((hd[:, 0:AW], last[:, 0:AW])):
                rows = t.rearrange("p (h w) -> p h w", h=HEADS)
                n = mark(nc.vector.tensor_tensor(rows, rows, fac[:, s, :].unsqueeze(2).to_broadcast([P, HEADS, VW]), ALU.mult))
            need(n)
            v.sem_inc(hd_used, 1)
            straight()

            v.wait_ge(s_vec, 3 * 16)
            v.wait_ge(s_const, 16 * CONSTS)
            v.wait_ge(skip_in, 16)
            heads = lambda t: t.rearrange("p (x w) -> p x w", w=VW)
            rows_of = lambda t, g: t[:, bass.ds(g * G, G), 0:HID]

            def sums_group(g, last):
                for j in range(G):
                    v.wait_ge(f_run[j], g * 16 + 16)
                    v.wait_ge(oh_ps, g * G + j + 1)
                    nc.vector.tensor_tensor(agg[:, j * AW:(j + 1) * AW], fl[:, j, 0:AW], psB(j), ALU.add).then_inc(f_used, 1)
                    if not last:
                        node_onehots(g + 1, j)
                v.wait_ge(f_used, g * G + G + G)
                settle(v)
                link(nc.vector.tensor_scalar(s40[:, :], heads(agg)[:, :, DH], 1e-30, None, ALU.max))
                link(nc.vector.reciprocal(s40[:, :], s40[:, :]))
                v.wait_ge(f_pre, g + 1)
                settle(v)
                link(nc.vector.tensor_tensor(mean.rearrange("p (x d) -> p x d", d=DH), heads(agg)[:, :, 0:DH],
                                             s40[:, :].unsqueeze(2).to_broadcast([P, G * HEADS, DH]), ALU.mult))
                nc.vector.tensor_tensor(rows_of(vst, g), rows_of(vst, g), mean.rearrange("p (j f) -> p j f", j=G), ALU.add).then_inc(f_pre, 1)

            def group_stats(g):
                settle(v)
                for j in range(G):
                    n = mark(nc.vector.bn_stats(bst[:, j, :], vst[:, g * G + j, 0:HID]))
                need(n)
                aggregate(g)

            def plus_x_group(g):
                v.wait_ge(f_gelu, g + 1)
                settle(v)
                link(nc.vector.tensor_tensor(rows_of(vst, g), rows_of(vst, g), rows_of(kst, g), ALU.add))
                group_stats(g)

            def normalised_here(g):
                for j in range(G):
                    i = g * G + j
                    n = mark(nc.vector.tensor_scalar(vst[:, i, 0:HID], vst[:, i, 0:HID], rstd[:, i:i + 1], nmr[:, i:i + 1],
                                                     ALU.mult, ALU.add))
                need(n)
                v.sem_inc(y_normed, G)

            per_group = 3 + 2 * G

            def x1_group(g):
                v.wait_ge(y_normed, g * G + G)
                settle(v)
                link(nc.vector.tensor_tensor(rows_of(vst, g), rows_of(vst, g), vecs[:, 0:1, :].to_broadcast([P, G, HID]), ALU.mult))
                v.wait_ge(f_xmx, g + 1)
                settle(v)
                link(nc.vector.tensor_tensor(rows_of(vst, g), rows_of(vst, g), rows_of(qe, g), ALU.add))
                group_stats(g)

            def x1_inv_std(g, n):
                inv_std(g * G, n * G)
                v.sem_inc(x1_norm, n)

            def weights_group(g):
                for j in range(G):
                    i = g * G + j
                    n = mark(nc.vector.tensor_scalar(kst[:, i, :], vst[:, i, 0:HID], rstd[:, bass.ds(i, 1)], nmr[:, bass.ds(i, 1)],
                                                     ALU.mult, ALU.add))
                need(n)
                v.sem_inc(xh_all, 1)
                for j in range(G):
                    i = g * G + j
                    n = mark(nc.vector.scalar_tensor_tensor(out=dots[:, j, :], in0=kst[:, i, :], scalar=1.0, in1=vecs[:, 2, :],
                                                        op0=ALU.mult, op1=ALU.mult, accum_out=wcol[:, bass.ds(i, 1)]))
                need(n)

            SUMS, PLUS = 2 * G + 3, 2 + 2 * G
            v.wait_ge(xn_in, 16)
            enter(0, SUMS)
            sums_group(0, False)
            leave(1, SUMS)
            with v.Fori(0, NG - 2) as g:
                enter(g, SUMS + PLUS)
                sums_group(g + 1, False)
                plus_x_group(g)
            leave(NG - 2, SUMS + PLUS)
            inv_std(0, DONE * G)
            v.sem_inc(y_norm, 1)
            straight()
            start = NG * (per_group + 2 * G) + 3 + 2 * (PLUS + G) + (DONE + 2) * INV
            enter(0, start)
            sums_group(NG - 1, True)
            x1_group(0)
            x1_inv_std(0, 1)
            for g in range(1, DONE):
                x1_group(g)
                x1_inv_std(g, 1)
                if g == 1:
                    weights_group(0)
                weights_group(g)
            for g in range(DONE, NG):
                plus_x_group(g)
            inv_std(DONE * G, NT - DONE * G)
            for g in range(DONE, NG):
                normalised_here(g)
            for g in range(DONE, NG):
                x1_group(g)
            x1_inv_std(DONE, NG - DONE)
            for g in range(DONE, NG):
                weights_group(g)
            leave(1, start)
            link(nc.vector.tensor_scalar(wcol[:, :], wcol[:, :], br_b[:, 0:1], None, ALU.add))
            v.sem_inc(w_ok, 1)

            v.wait_ge(w_b, 16)
            link(nc.vector.memset(cnt[:, :, :], 0.0))
            weights = QWB[:, :].rearrange("q (p n) -> q n p", n=NT)
            unused = junk.rearrange("q (n p) -> q n p", n=NT)
            for n in range(NT):
                w = wcol[:, n:n + 1]
                if n:
                    link(nc.vector.tensor_scalar(unused[:, 0:n, :], weights[:, 0:n, :], w, 0.0, ALU.is_ge, ALU.add, accum_out=cnt[:, 0, n:n + 1]))
                link(nc.vector.tensor_scalar(unused[:, n:NT, :], weights[:, n:NT, :], w, 0.0, ALU.is_gt, ALU.add, accum_out=cnt[:, 1, n:n + 1]))
                link(nc.vector.scalar_tensor_tensor(out=unused[:, n, :], in0=weights[:, n, :], scalar=w, in1=lower[:, :],
                                                    op0=ALU.is_equal, op1=ALU.mult, accum_out=cnt[:, 2, n:n + 1]))
            link(nc.vector.tensor_tensor(cnt[:, 0, :], cnt[:, 0, :], cnt[:, 1, :], ALU.add))
            link(nc.vector.tensor_tensor(cnt[:, 0, :], cnt[:, 0, :], cnt[:, 2, :], ALU.add))
            link(nc.vector.scalar_tensor_tensor(out=wcol[:, :], in0=cnt[:, 0, :], scalar=float(KEPT) - 0.5, in1=wcol[:, :],
                                                op0=ALU.is_lt, op1=ALU.mult))
            with v.Fori(0, NG) as g:
                v.wait_ge(yb_ok, g + 1)
                for j in range(G):
                    i = g * G + j
                    ins = nc.vector.scalar_tensor_tensor(out=vst[:, i, 0:HID], in0=vst[:, i, 0:HID], scalar=wcol[:, bass.ds(i, 1)],
                                                         in1=qe[:, i, :], op0=ALU.mult, op1=ALU.add)
                ins.then_inc(o_ok, 1)

        @block.scalar
        def _(act):
            order = Order(act, act_order)

            def turned(w, j, gain, shift):
                act.wait_ge(pt_done, w + 1 + G)
                if gain is None:
                    nc.scalar.activation(hT[:, j % 3, :, :], psT(j), ACT.Copy).then_inc(hT_ready, 1)
                else:
                    nc.scalar.activation(hT[:, j % 3, 0, :], psT(j)[:, 0, :], ACT.Identity, scale=gain[0], bias=shift[0])
                    nc.scalar.activation(hT[:, j % 3, 1, :], psT(j)[:, 1, :], ACT.Identity, scale=gain[1], bias=shift[1]).then_inc(hT_ready, 1)

            def normalised(w, i, j):
                act.wait_ge(pt_done, w + 1)
                settle(act)
                nc.scalar.activation(xh[:, j, :], xm[:, i, :], ACT.Identity, scale=rstd[:, bass.ds(i, 1)],
                                     bias=nmr[:, bass.ds(i, 1)]).then_inc(xh_ready, 1)

            def hidden(h0, i, j, function, bias):
                for half in range(2):
                    act.wait_ge(h_done, h0 + i * 2 + half + 1)
                    for k in range(4):
                        ins = nc.scalar.activation(hg[:, j % 2, 4 * half + k, :], psH(j, half)[:, k, :], function,
                                                   bias=bias[:, 4 * half + k:4 * half + k + 1])
                    ins.then_inc(hg_ok, 1)

            with act.Fori(0, NG) as g:
                for j in range(G):
                    i = g * G + j
                    act.wait_ge(xh_ready, i + 1)
                    nc.scalar.activation(xm[:, i, :], xh[:, j, :], ACT.Copy).then_inc(xh_copied, 1)
                    turned(i, j, None, None)
            def edge_weights(turn, k):
                act.wait_ge(e_logit, 2 * turn + k + 1)
                nc.scalar.activation(E7[:, k, :], E7[:, k, :], ACT.Exp, scale=GNN_SCALE).then_inc(e_exp, 1)

            act.wait_ge(s_const, 16 * CONSTS)
            with act.Fori(0, LAYERS) as L:
                act.wait_ge(hg_ok, L * (2 * NT) + 1)
                settle(act)
                order.base, order.n = L * 3, 0
                order.mark(nc.scalar.activation(cur[:, 0:2, :], ln1[:, :, bass.ds(L, 1), :].rearrange("k s l c -> k s (l c)"), ACT.Copy))
                order.mark(nc.scalar.activation(cur[:, 2:4, :], ln2[:, :, bass.ds(L, 1), :].rearrange("k s l c -> k s (l c)"), ACT.Copy))
                order.link(nc.scalar.activation(cur_b1[:, :], b1_mix[:, bass.ds(L, 1), :].rearrange("k l c -> k (l c)"), ACT.Copy))
                settle(act)
                gain1, shift1, gain2, shift2 = ([cur[:, s, c:c + 1] for c in range(C)] for s in range(4))
                act.wait_ge(ln1_ok, L * NG + 1)
                settle(act)
                for j in range(G):
                    normalised(w_a(L, j), j, j)
                turned(w_a(L, 0), 0, gain1, shift1)
                act.wait_ge(mix_start, 1)

                def projections(g, last):
                    if not last:
                        act.wait_ge(ln1_ok, L * NG + g + 2)
                        settle(act)
                    for j in range(G):
                        i = g * G + j
                        if j + 1 < G or not last:
                            turned(w_a(L, i + 1), (j + 1) % G, gain1, shift1)
                        act.wait_ge(qk_done, L * NT + i + 1)
                        nc.scalar.activation(kst[:, i, :], psKV(j)[:, 0:HID], ACT.Copy)
                        nc.scalar.activation(vmix[:, i, :, 0:128], psKV(j)[:, HID:2 * HID].rearrange("p (c f) -> p c f", c=C), ACT.Copy).then_inc(qk_act, 1)
                        if not last:
                            normalised(w_a(L, i + G), i + G, j)
                        act.wait_ge(qsub, L * NT + i + 3)
                        nc.scalar.activation(qe[:, i, :], qe[:, i, :], ACT.Exp, scale=MIX_SCALE).then_inc(qexp, 1)
                        if j in (0, 2):
                            edge_weights(L * (2 * NG) + g, int(j == 2))

                groups(act, projections)
                with act.Fori(0, NG) as g:
                    for j in range(G):
                        act.wait_ge(kd, L * NT + g * G + j + 1)
                        nc.scalar.activation(ek[:, j, :], ek[:, j, :], ACT.Exp, scale=MIX_SCALE).then_inc(ek_ok, 1)
                with act.Fori(0, NG) as g:
                    for j in range(G):
                        turned(w_c1(L, g * G + j), j, None, None)
                act.wait_ge(ln2_ok, L + 1)
                settle(act)
                for j in range(G):
                    normalised(w_c2(L, j), j, j)
                turned(w_c2(L, 0), 0, gain2, shift2)

                def ffn(g, last):
                    for j in range(G):
                        i = g * G + j
                        if j + 1 < G or not last:
                            turned(w_c2(L, i + 1), (j + 1) % G, gain2, shift2)
                        hidden(L * (2 * NT), i, j, ACT.Gelu, cur_b1)
                        if not last:
                            normalised(w_c2(L, i + G), i + G, j)
                    for k in range(2):
                        edge_weights(L * (2 * NG) + NG + g, k)

                groups(act, ffn)
            act.wait_ge(b_d, 1)
            nc.scalar.activation(fac[:, :, :], fac[:, :, :], ACT.Exp, scale=GNN_SCALE).then_inc(b_e, 1)

            def gelu_group(g):
                act.wait_ge(f_pre, g + 2)
                settle(act)
                nc.scalar.activation(vst[:, bass.ds(g * G, G), 0:HID], vst[:, bass.ds(g * G, G), 0:HID], ACT.Gelu).then_inc(f_gelu, 1)

            with act.Fori(0, NG - 1) as g:
                gelu_group(g)
            act.wait_ge(y_norm, 1)
            with act.Fori(0, DONE * G) as i:
                nc.scalar.activation(vst[:, i, 0:HID], vst[:, i, 0:HID], ACT.Identity, scale=rstd[:, bass.ds(i, 1)],
                                     bias=nmr[:, bass.ds(i, 1)]).then_inc(y_normed, 1)
            gelu_group(NG - 1)

            def normalised_x1(g, i, j):
                act.wait_ge(x1_norm, g + 1)
                act.wait_ge(pt_done, w_f(i) + 1)
                settle(act)
                nc.scalar.activation(xh[:, j, :], vst[:, i, 0:HID], ACT.Identity, scale=rstd[:, bass.ds(i, 1)],
                                     bias=nmr[:, bass.ds(i, 1)]).then_inc(xh_ready, 1)

            for j in range(G):
                normalised_x1(0, j, j)
            turned(w_f(0), 0, None, None)

            def ffn_rows(g, j):
                i = g * G + j
                act.wait_ge(xx_ok, g + 1)
                act.wait_ge(y_done, i + 1 + LAYERS * NT)
                settle(act)
                nc.scalar.activation(vst[:, i, 0:HID], psY(j), ACT.Copy).then_inc(f_y, 1)

            def routed_ffn(g, last):
                for j in range(G):
                    i = g * G + j
                    if j + 1 < G or not last:
                        turned(w_f(i + 1), (j + 1) % G, None, None)
                    hidden(LAYERS * 2 * NT, i, j, ACT.Gelu_apprx_tanh, b1_ffn)
                    if not last:
                        normalised_x1(g + 1, i + G, j)
                    if j:
                        ffn_rows(g, j - 1)
                ffn_rows(g, G - 1)

            groups(act, routed_ffn)

        @block.tensor
        def _(pe):
            mm = nc.tensor.matmul

            def room(sem, n, j):
                pe.wait_ge(sem, n + 1 + (j == 0))

            def turn(w, j):
                pe.wait_ge(xh_ready, w + 1)
                room(hT_ready, w, j)
                for c in range(C):
                    ins = nc.tensor.transpose(psT(j)[:, c, :], xh[:, j, c * 128:(c + 1) * 128], ident[0:P, 0:P])
                ins.then_inc(pt_done, 1)

            def ffn_up(i, j):
                for half in range(2):
                    for k in range(4):
                        for c in range(C):
                            ins = mm(psH(j, half)[:, k, :], w_big[:, c, (4 * half + k) * 128:(4 * half + k + 1) * 128], hT[:, j % 3, c, :],
                                     start=(c == 0), stop=(c == C - 1))
                    ins.then_inc(h_done, 1)

            def ffn_down(free, y0, h0, i, j):
                room(free, y0 + i, j)
                for half in range(2):
                    pe.wait_ge(hg_ok, h0 + i * 2 + half + 2)
                    for k in range(4 * half, 4 * half + 4):
                        ins = mm(psY(j), hg[:, j % 2, k, :], w_down[:, k, :], start=(k == 0), stop=(k == KC - 1))
                ins.then_inc(y_done, 1)

            def ffn(w, free, y0, h0):
                turn(w(0), 0)

                def up(i, j):
                    pe.wait_ge(hT_ready, w(i) + 3)
                    ffn_up(i, j)

                def group(g, last):
                    turn(w(g * G + 1), 1)
                    up(g * G, 0)
                    for j in range(G):
                        i = g * G + j
                        if j + 2 < G or (j + 2 == G and not last):
                            turn(w(i + 2), (j + 2) % G)
                        if j + 1 < G:
                            up(i + 1, j + 1)
                        ffn_down(free, y0, h0, i, j)

                groups(pe, group)

            pe.wait_ge(gn, 8)
            pe.wait_ge(d_f, 1)
            mm(psX[0:P, 0:P], ends[:, 0:1].to_broadcast([P, P]), ident[0:P, 0:P], start=True, stop=True).then_inc(d_b, 1)
            pe.wait_ge(s_wg, 8 * 16)
            turn(0, 0)

            def gnn_group(g, last):
                for j in range(G):
                    i = g * G + j
                    if j + 1 < G or not last:
                        turn(i + 1, (j + 1) % G)
                    pe.wait_ge(hT_ready, i + 3)
                    room(gp_free, i, j)
                    for half, ps in enumerate((psQK(j), psVS(j))):
                        for c in range(C):
                            ins = mm(ps, hT[:, j % 3, c, :], w_big[:, c, half * 512:(half + 1) * 512], start=(c == 0), stop=(c == C - 1))
                    ins.then_inc(gp_done, 1)

            groups(pe, gnn_group)
            with pe.Fori(0, LAYERS) as L:
                pe.wait_ge(s_wqkv, L * 48 + 48)
                settle(pe)
                turn(w_a(L, 0), 0)

                def projections(g, last):
                    for j in range(G):
                        i = g * G + j
                        if j + 1 < G or not last:
                            turn(w_a(L, i + 1), (j + 1) % G)
                        pe.wait_ge(hT_ready, w_a(L, i) + 3)
                        room(qsub, L * NT + i, j)
                        for c in range(C):
                            mm(psQ(j), hT[:, j % 3, c, :], w_qkv[:, c, 0:HID], start=(c == 0), stop=(c == C - 1))
                        room(qk_act, L * NT + i, j)
                        for c in range(C):
                            ins = mm(psKV(j), hT[:, j % 3, c, :], w_qkv[:, c, HID:3 * HID], start=(c == 0), stop=(c == C - 1))
                        ins.then_inc(qk_done, 1)

                groups(pe, projections)
                pe.wait_ge(km_col, L + 1)
                for c in range(C):
                    ins = nc.tensor.transpose(psX[:, c * P:(c + 1) * P], kmx[:, c * 128:(c + 1) * 128], ident[0:P, 0:P])
                ins.then_inc(km_t, 1)
                pe.wait_ge(km_dg, L + 1)
                mm(psX[0:P, 256:512], ones[:, 0:P], dg[:, :, :].rearrange("p c n -> p (c n)"), start=True, stop=True).then_inc(km_b, 1)
                for c in range(C):
                    mm(psC(c), zeros[:, 0:128], zeros[:, :], start=True, stop=False)
                with pe.Fori(0, NG) as g:
                    for j in range(G):
                        i = g * G + j
                        pe.wait_ge(ek_ok, L * NT + i + 1)
                        for c in range(C):
                            ins = mm(psC(c), ek[:, j, c * 128:(c + 1) * 128], vmix[:, i, c, 0:129], start=False, stop=False)
                        ins.then_inc(ek_used, 1)
                for c in range(C):
                    ins = mm(psC(c), zeros[:, 0:128], zeros[:, :], start=False, stop=True)
                ins.then_inc(ctx_done, 1)
                pe.wait_ge(bd_ok, L + 1)
                for c in range(C):
                    ins = nc.tensor.transpose(psX[:, c * 128:(c + 1) * 128], BD[:, c, :], ident[:, :])
                ins.then_inc(bdt, 1)
                pe.wait_ge(bdt_ok, L + 1)
                pe.wait_ge(s_wo, L * 32 + 32)
                for c in range(C):
                    ins = mm(psM[:, c * HID:(c + 1) * HID], BDT[:, c, :], w_o[:, c, :], start=True, stop=True)
                ins.then_inc(m_done, 1)
                pe.wait_ge(m_ok, L + 2)
                settle(pe)
                turn(w_c1(L, 0), 0)

                def attention(g, last):
                    for j in range(G):
                        i = g * G + j
                        if j + 1 < G or not last:
                            turn(w_c1(L, i + 1), (j + 1) % G)
                        pe.wait_ge(hT_ready, w_c1(L, i) + 3)
                        room(at_free, L * NT + i, j)
                        for c in range(C):
                            ins = mm(psY(j), hT[:, j % 3, c, :], m_sb[:, c, :], start=(c == 0), stop=(c == C - 1))
                        ins.then_inc(at_done, 1)

                groups(pe, attention)
                pe.wait_ge(s_w1, L * 16 + 16)
                pe.wait_ge(s_w2, L * 32 + 32)
                settle(pe)
                pe.wait_ge(at_free, L * NT + NT + 2)
                settle(pe)
                ffn(lambda i: w_c2(L, i), y_free, L * NT, L * (2 * NT))
            pe.wait_ge(b_k, 1)
            for i in range(4):
                ins = nc.tensor.transpose(psX[0:HEADS, i * 128:i * 128 + P], keys[:, i, :], ident[0:P, 0:P])
            ins.then_inc(b_t, 1)
            pe.wait_ge(b_m, 1)
            for s in range(2):
                ins = nc.tensor.transpose(bank[6][0:P, s * HEADS:(s + 1) * HEADS], F2[:, s * P:(s + 1) * P], ident[0:HEADS, 0:HEADS])
            ins.then_inc(b_f, 1)
            pe.wait_ge(hd_used, 1)
            with pe.Fori(0, NG) as g:
                for j in range(G):
                    i = g * G + j
                    pe.wait_ge(oh_ok, i + 1)
                    pe.wait_ge(f_used, i + 4 + (j == 0))
                    mm(psB(j), onehots[:, j, 0, :], hd[:, 0:AW], start=True, stop=False)
                    mm(psB(j), onehots[:, j, 1, :], S[:, 1, T - 1, 0:AW], start=False, stop=True).then_inc(oh_ps, 1)
            pe.wait_ge(s_const, 16 * CONSTS)
            pe.wait_ge(s_w1, LAYERS * 16 + 16)
            pe.wait_ge(s_w2, LAYERS * 32 + 16)
            ffn(w_f, f_y, 0, LAYERS * 2 * NT)


INS = ["x", "src", "dst", "L0_gnn_Wq", "L0_gnn_bq", "L0_gnn_Wk", "L0_gnn_bk", "L0_gnn_Wv", "L0_gnn_bv", "L0_gnn_Wskip", "L0_gnn_bskip",
       "L0_gnn_gamma", "L0_gnn_beta", "L0_mix_Wq", "L0_mix_Wk", "L0_mix_Wv", "L0_mix_Wo", "L0_mix_bo", "L0_mix_ln1_g", "L0_mix_ln1_b",
       "L0_mix_W1", "L0_mix_b1", "L0_mix_W2", "L0_mix_b2", "L0_mix_ln2_g", "L0_mix_ln2_b", "L0_ffn_wr", "L0_ffn_br", "L0_ffn_w1",
       "L0_ffn_b1", "L0_ffn_w2", "L0_ffn_b2"]


def kernel(**inputs):
    import numpy as np
    import concourse.bacc as bacc
    from concourse.bass_utils import run_bass_kernel_spmd

    nc = bacc.Bacc("TRN2", target_bir_lowering=False, num_devices=1)
    arrays, aps = {}, {}
    for name in INS:
        a = np.ascontiguousarray(inputs[name])
        arrays["in_" + name] = a
        aps[name] = nc.dram_tensor("in_" + name, a.shape, mybir.dt.from_np(a.dtype), kind="ExternalInput").ap()
    out = nc.dram_tensor("out", [N, HID], F32, kind="ExternalOutput").ap()
    gps_kernel(nc, aps, out)
    r = run_bass_kernel_spmd(nc, [arrays], core_ids=[0])
    return r.results[0]["out"]
```
